# Optimizing a Trainium2 kernel written in Bass

```python
import numpy as np
import jax
import jax.numpy as jnp

def _softmax(x, axis=-1):
    return jax.nn.softmax(x, axis=axis)

def _gelu(x):
    return jax.nn.gelu(x, approximate=True)

def _silu(x):
    return jax.nn.silu(x)

def _sigmoid(x):
    return jax.nn.sigmoid(x)

def _layernorm(x, axis=-1, eps=1e-05):
    m = jnp.mean(x, axis=axis, keepdims=True)
    v = jnp.var(x, axis=axis, keepdims=True)
    return (x - m) / jnp.sqrt(v + eps)

def _scatter_add(tgt, idx, src, axis=0):
    return tgt.at[idx].add(src)

def _segment_sum(src, seg, n):
    return jax.ops.segment_sum(src, seg, n)
kernel_name = 'mk_xattn_seq_d4_seqx_r4_3a11d9'

def setup_inputs(seed: int=0):
    np.random.seed(seed)
    _w = jnp.asarray

    def _rec_inputs():
        import jax
        import jax.numpy as jnp
        _rk = jax.random.key(seed)
        x = 7.22e-05 + 1 * jax.random.normal(jax.random.fold_in(_rk, 1), (8, 112, 512), jnp.float32)
        _lenS = 112 - jax.random.randint(jax.random.fold_in(_rk, 7), (8,), 0, max(1, 112 // 4) + 1, jnp.int32)
        _lenS2 = 375 - jax.random.randint(jax.random.fold_in(_rk, 8), (8,), 0, max(1, 375 // 4) + 1, jnp.int32)
        _ctx_1024P = jax.random.normal(jax.random.fold_in(_rk, 11), (8, 16, 256), jnp.float32)
        _ctx_1024c = jax.random.dirichlet(jax.random.fold_in(_rk, 511), 0.3 * jnp.ones((16,), jnp.float32), (8, 375))
        _ctx_1024t = jnp.einsum('bsk,bkd->bsd', _ctx_1024c, _ctx_1024P)
        _ctx_1024t = _ctx_1024t * jax.lax.rsqrt(jnp.mean(jnp.square(_ctx_1024t)) + 1e-12) * 0.953939
        ctx_1024 = -0.000514642 + 1.00011 * (_ctx_1024t + 0.3 * jax.random.normal(jax.random.fold_in(_rk, 611), (8, 375, 256), jnp.float32))
        pos_1xS = jnp.broadcast_to(jnp.arange(112, dtype=jnp.int32), (1, 112))
        _validS = jnp.arange(112)[None, :] < _lenS[:, None]
        _validS2 = jnp.arange(375)[None, :] < _lenS2[:, None]
        _causal = jnp.tril(jnp.ones((112, 112), dtype=bool))
        mask_BxS_ik0 = jnp.where(jnp.broadcast_to(_validS[:, :], (8, 112)), 0, 1).astype(jnp.int32)
        mask_BxS2_bk0 = jnp.logical_not(jnp.broadcast_to(_validS2[:, :], (8, 375)))
        return (x, ctx_1024, pos_1xS, mask_BxS_ik0, mask_BxS2_bk0)
    x, ctx_1024, pos_1xS, mask_BxS_ik0, mask_BxS2_bk0 = _rec_inputs()

    def _L0_xattn_setup():
        import jax, jax.numpy as jnp
        import numpy as np
        H = 512
        NH = 16
        HD = H // NH
        CH = 256
        CC = 256
        CHD = CC // NH
        I = 1376
        B = 2
        L = 512
        LE = 256
        EPS = 1e-06

        def rms_norm(x, w):
            xf = x.astype(jnp.float32)
            var = jnp.mean(xf * xf, axis=-1, keepdims=True)
            return (w * (xf * jax.lax.rsqrt(var + EPS))).astype(x.dtype)

        def expert_mask(tt):
            vm = jnp.zeros(tt.shape, dtype=bool)
            vm = vm.at[:, :-1].set((tt[:, :-1] == 1) & (tt[:, 1:] == 1))
            return vm

        def rotate_half(x):
            d = x.shape[-1] // 2
            return jnp.concatenate([-x[..., d:], x[..., :d]], axis=-1)

        def apply_rotary(q, k, position_ids, seq_len):
            inv = 1.0 / 10000.0 ** (jnp.arange(0, HD, 2, dtype=jnp.float32) / HD)
            t = jnp.arange(seq_len, dtype=jnp.float32)
            freqs = jnp.outer(t, inv)
            emb = jnp.concatenate([freqs, freqs], axis=-1)
            cos = jnp.cos(emb)[position_ids][:, None].astype(q.dtype)
            sin = jnp.sin(emb)[position_ids][:, None].astype(q.dtype)
            return (q * cos + rotate_half(q) * sin, k * cos + rotate_half(k) * sin)

        def sdpa(q, k, v, causal):
            scale = 1.0 / np.sqrt(q.shape[-1])
            scores = jnp.einsum('bhqd,bhkd->bhqk', q * scale, k)
            if causal:
                mask = jnp.tril(jnp.ones((q.shape[-2], k.shape[-2]), dtype=bool))
                scores = jnp.where(mask, scores, jnp.finfo(jnp.float32).min)
            p = jax.nn.softmax(scores.astype(jnp.float32), axis=-1).astype(q.dtype)
            return jnp.einsum('bhqk,bhkd->bhqd', p, v)

        def heads(x, nh, hd):
            b, l, _ = x.shape
            return x.reshape(b, l, nh, hd).transpose(0, 2, 1, 3)
        key = jax.random.key(seed)
        ks = jax.random.split(key, 20)
        s = 0.02
        f32 = jnp.float32
        return {'hidden_states': jax.random.normal(ks[0], (B, L, H), f32), 'encoder_outputs': jax.random.normal(ks[1], (B, LE, CH), f32), 'token_type_ids': jax.random.randint(ks[2], (B, L), 0, 2, jnp.int32), 'position_ids': jnp.arange(L, dtype=jnp.int32)[None, :], 'ln_in_w': jnp.ones((H,), f32), 'ln_post_attn_w': jnp.ones((H,), f32), 'ln_post_cross_w': jnp.ones((H,), f32), 'v_qkv': jax.random.normal(ks[3], (H, 3 * H), f32) * s, 'l_qkv': jax.random.normal(ks[4], (H, 3 * H), f32) * s, 'v_dense': jax.random.normal(ks[5], (H, H), f32) * s, 'l_dense': jax.random.normal(ks[6], (H, H), f32) * s, 'cq_w': jax.random.normal(ks[7], (H, CC), f32) * s, 'ckv_w': jax.random.normal(ks[8], (CH, 2 * CC), f32) * s, 'cdense_w': jax.random.normal(ks[9], (CC, H), f32) * s, 'v_gate': jax.random.normal(ks[10], (H, I), f32) * s, 'v_up': jax.random.normal(ks[11], (H, I), f32) * s, 'v_down': jax.random.normal(ks[12], (I, H), f32) * s, 'l_gate': jax.random.normal(ks[13], (H, I), f32) * s, 'l_up': jax.random.normal(ks[14], (H, I), f32) * s, 'l_down': jax.random.normal(ks[15], (I, H), f32) * s}
    _L0_xattn_all = _L0_xattn_setup()
    _L0_xattn_in = {k: v for k, v in _L0_xattn_all.items() if k in ('ln_in_w', 'ln_post_attn_w', 'ln_post_cross_w', 'v_qkv', 'l_qkv', 'v_dense', 'l_dense', 'cq_w', 'ckv_w', 'cdense_w', 'v_gate', 'v_up', 'v_down', 'l_gate', 'l_up', 'l_down')}
    del _L0_xattn_all

    def _L1_xattn_setup():
        import jax, jax.numpy as jnp
        import numpy as np
        DIM = 512
        DIM_MEDIA = 256
        HEADS = 16
        DIM_HEAD = 64
        INNER = HEADS * DIM_HEAD
        FF_INNER = 4 * DIM
        B, N_TOK, N_LAT = (4, 512, 64)
        EPS = 1e-05

        def layernorm(x, g, b):
            mu = jnp.mean(x, axis=-1, keepdims=True)
            var = jnp.var(x, axis=-1, keepdims=True)
            return (x - mu) * jax.lax.rsqrt(var + EPS) * g + b
        key = jax.random.key(seed)
        ks = jax.random.split(key, 12)
        x = jax.random.normal(ks[0], (B, N_TOK, DIM), dtype=jnp.float32)
        media = jax.random.normal(ks[1], (B, N_LAT, DIM_MEDIA), dtype=jnp.float32)
        media_mask = jax.random.randint(ks[2], (B, N_LAT), 0, 2).astype(bool)
        media_mask = media_mask.at[:, 0].set(True)
        s = lambda d: 1.0 / np.sqrt(d)
        Wq = jax.random.normal(ks[3], (DIM, INNER), dtype=jnp.float32) * s(DIM)
        Wkv = jax.random.normal(ks[4], (DIM_MEDIA, 2 * INNER), dtype=jnp.float32) * s(DIM_MEDIA)
        Wo = jax.random.normal(ks[5], (INNER, DIM), dtype=jnp.float32) * s(INNER)
        W1 = jax.random.normal(ks[6], (DIM, FF_INNER), dtype=jnp.float32) * s(DIM)
        W2 = jax.random.normal(ks[7], (FF_INNER, DIM), dtype=jnp.float32) * s(FF_INNER)
        return {'x': x, 'media': media, 'media_mask': media_mask, 'ln_q_g': jnp.ones((DIM,), jnp.float32), 'ln_q_b': jnp.zeros((DIM,), jnp.float32), 'Wq': Wq, 'Wkv': Wkv, 'Wo': Wo, 'attn_gate': jax.random.normal(ks[8], (1,), jnp.float32) * 0.5, 'ln_ff_g': jnp.ones((DIM,), jnp.float32), 'ln_ff_b': jnp.zeros((DIM,), jnp.float32), 'W1': W1, 'W2': W2, 'ff_gate': jax.random.normal(ks[9], (1,), jnp.float32) * 0.5}
    _L1_xattn_all = _L1_xattn_setup()
    _L1_xattn_in = {k: v for k, v in _L1_xattn_all.items() if k in ('ln_q_g', 'ln_q_b', 'Wq', 'Wkv', 'Wo', 'attn_gate', 'ln_ff_g', 'ln_ff_b', 'W1', 'W2', 'ff_gate')}
    del _L1_xattn_all

    def _L2_xattn_setup():
        import jax, jax.numpy as jnp
        import numpy as np
        EPS = 1e-06

        def _rmsnorm(x, w):
            var = jnp.mean(jnp.square(x), axis=-1, keepdims=True)
            return x * jax.lax.rsqrt(var + EPS) * w
        key = jax.random.key(seed)
        ks = jax.random.split(key, 6)
        B, N, M = (4, 1024, 512)
        d_model, memory_dim = (512, 256)
        hidden_states = jax.random.normal(ks[0], (B, N, d_model), dtype=jnp.float32)
        memory = jax.random.normal(ks[1], (B, M, memory_dim), dtype=jnp.float32)
        W_mem = jax.random.normal(ks[2], (d_model, memory_dim), dtype=jnp.float32) / np.sqrt(memory_dim)
        W_gate = jax.random.normal(ks[3], (d_model, 2 * d_model), dtype=jnp.float32) / np.sqrt(2 * d_model)
        b_gate = jax.random.normal(ks[4], (d_model,), dtype=jnp.float32) * 0.01
        norm_w = jnp.ones((d_model,), dtype=jnp.float32)
        return {'hidden_states': hidden_states, 'memory': memory, 'W_mem': W_mem, 'W_gate': W_gate, 'b_gate': b_gate, 'norm_w': norm_w}
    _L2_xattn_all = _L2_xattn_setup()
    _L2_xattn_in = {k: v for k, v in _L2_xattn_all.items() if k in ('W_mem', 'W_gate', 'b_gate', 'norm_w')}
    del _L2_xattn_all

    def _L3_xattn_setup():
        import jax, jax.numpy as jnp
        import numpy as np
        DIM = 512
        DIM_MEDIA = 256
        HEADS = 16
        DIM_HEAD = 64
        INNER = HEADS * DIM_HEAD
        FF_INNER = 4 * DIM
        B, N_TOK, N_LAT = (4, 512, 64)
        EPS = 1e-05

        def layernorm(x, g, b):
            mu = jnp.mean(x, axis=-1, keepdims=True)
            var = jnp.var(x, axis=-1, keepdims=True)
            return (x - mu) * jax.lax.rsqrt(var + EPS) * g + b
        key = jax.random.key(seed)
        ks = jax.random.split(key, 12)
        x = jax.random.normal(ks[0], (B, N_TOK, DIM), dtype=jnp.float32)
        media = jax.random.normal(ks[1], (B, N_LAT, DIM_MEDIA), dtype=jnp.float32)
        media_mask = jax.random.randint(ks[2], (B, N_LAT), 0, 2).astype(bool)
        media_mask = media_mask.at[:, 0].set(True)
        s = lambda d: 1.0 / np.sqrt(d)
        Wq = jax.random.normal(ks[3], (DIM, INNER), dtype=jnp.float32) * s(DIM)
        Wkv = jax.random.normal(ks[4], (DIM_MEDIA, 2 * INNER), dtype=jnp.float32) * s(DIM_MEDIA)
        Wo = jax.random.normal(ks[5], (INNER, DIM), dtype=jnp.float32) * s(INNER)
        W1 = jax.random.normal(ks[6], (DIM, FF_INNER), dtype=jnp.float32) * s(DIM)
        W2 = jax.random.normal(ks[7], (FF_INNER, DIM), dtype=jnp.float32) * s(FF_INNER)
        return {'x': x, 'media': media, 'media_mask': media_mask, 'ln_q_g': jnp.ones((DIM,), jnp.float32), 'ln_q_b': jnp.zeros((DIM,), jnp.float32), 'Wq': Wq, 'Wkv': Wkv, 'Wo': Wo, 'attn_gate': jax.random.normal(ks[8], (1,), jnp.float32) * 0.5, 'ln_ff_g': jnp.ones((DIM,), jnp.float32), 'ln_ff_b': jnp.zeros((DIM,), jnp.float32), 'W1': W1, 'W2': W2, 'ff_gate': jax.random.normal(ks[9], (1,), jnp.float32) * 0.5}
    _L3_xattn_all = _L3_xattn_setup()
    _L3_xattn_in = {k: v for k, v in _L3_xattn_all.items() if k in ('ln_q_g', 'ln_q_b', 'Wq', 'Wkv', 'Wo', 'attn_gate', 'ln_ff_g', 'ln_ff_b', 'W1', 'W2', 'ff_gate')}
    del _L3_xattn_all
    return {'x': x, 'ctx_1024': ctx_1024, 'pos_1xS': pos_1xS, 'mask_BxS_ik0': mask_BxS_ik0, 'mask_BxS2_bk0': mask_BxS2_bk0, 'L0_xattn_ln_in_w': _L0_xattn_in['ln_in_w'], 'L0_xattn_ln_post_attn_w': _L0_xattn_in['ln_post_attn_w'], 'L0_xattn_ln_post_cross_w': _L0_xattn_in['ln_post_cross_w'], 'L0_xattn_v_qkv': _L0_xattn_in['v_qkv'], 'L0_xattn_l_qkv': _L0_xattn_in['l_qkv'], 'L0_xattn_v_dense': _L0_xattn_in['v_dense'], 'L0_xattn_l_dense': _L0_xattn_in['l_dense'], 'L0_xattn_cq_w': _L0_xattn_in['cq_w'], 'L0_xattn_ckv_w': _L0_xattn_in['ckv_w'], 'L0_xattn_cdense_w': _L0_xattn_in['cdense_w'], 'L0_xattn_v_gate': _L0_xattn_in['v_gate'], 'L0_xattn_v_up': _L0_xattn_in['v_up'], 'L0_xattn_v_down': _L0_xattn_in['v_down'], 'L0_xattn_l_gate': _L0_xattn_in['l_gate'], 'L0_xattn_l_up': _L0_xattn_in['l_up'], 'L0_xattn_l_down': _L0_xattn_in['l_down'], 'L1_xattn_ln_q_g': _L1_xattn_in['ln_q_g'], 'L1_xattn_ln_q_b': _L1_xattn_in['ln_q_b'], 'L1_xattn_Wq': _L1_xattn_in['Wq'], 'L1_xattn_Wkv': _L1_xattn_in['Wkv'], 'L1_xattn_Wo': _L1_xattn_in['Wo'], 'L1_xattn_attn_gate': _L1_xattn_in['attn_gate'], 'L1_xattn_ln_ff_g': _L1_xattn_in['ln_ff_g'], 'L1_xattn_ln_ff_b': _L1_xattn_in['ln_ff_b'], 'L1_xattn_W1': _L1_xattn_in['W1'], 'L1_xattn_W2': _L1_xattn_in['W2'], 'L1_xattn_ff_gate': _L1_xattn_in['ff_gate'], 'L2_xattn_W_mem': _L2_xattn_in['W_mem'], 'L2_xattn_W_gate': _L2_xattn_in['W_gate'], 'L2_xattn_b_gate': _L2_xattn_in['b_gate'], 'L2_xattn_norm_w': _L2_xattn_in['norm_w'], 'L3_xattn_ln_q_g': _L3_xattn_in['ln_q_g'], 'L3_xattn_ln_q_b': _L3_xattn_in['ln_q_b'], 'L3_xattn_Wq': _L3_xattn_in['Wq'], 'L3_xattn_Wkv': _L3_xattn_in['Wkv'], 'L3_xattn_Wo': _L3_xattn_in['Wo'], 'L3_xattn_attn_gate': _L3_xattn_in['attn_gate'], 'L3_xattn_ln_ff_g': _L3_xattn_in['ln_ff_g'], 'L3_xattn_ln_ff_b': _L3_xattn_in['ln_ff_b'], 'L3_xattn_W1': _L3_xattn_in['W1'], 'L3_xattn_W2': _L3_xattn_in['W2'], 'L3_xattn_ff_gate': _L3_xattn_in['ff_gate']}

def reference(x, ctx_1024, pos_1xS, mask_BxS_ik0, mask_BxS2_bk0, L0_xattn_ln_in_w, L0_xattn_ln_post_attn_w, L0_xattn_ln_post_cross_w, L0_xattn_v_qkv, L0_xattn_l_qkv, L0_xattn_v_dense, L0_xattn_l_dense, L0_xattn_cq_w, L0_xattn_ckv_w, L0_xattn_cdense_w, L0_xattn_v_gate, L0_xattn_v_up, L0_xattn_v_down, L0_xattn_l_gate, L0_xattn_l_up, L0_xattn_l_down, L1_xattn_ln_q_g, L1_xattn_ln_q_b, L1_xattn_Wq, L1_xattn_Wkv, L1_xattn_Wo, L1_xattn_attn_gate, L1_xattn_ln_ff_g, L1_xattn_ln_ff_b, L1_xattn_W1, L1_xattn_W2, L1_xattn_ff_gate, L2_xattn_W_mem, L2_xattn_W_gate, L2_xattn_b_gate, L2_xattn_norm_w, L3_xattn_ln_q_g, L3_xattn_ln_q_b, L3_xattn_Wq, L3_xattn_Wkv, L3_xattn_Wo, L3_xattn_attn_gate, L3_xattn_ln_ff_g, L3_xattn_ln_ff_b, L3_xattn_W1, L3_xattn_W2, L3_xattn_ff_gate):
    import jax
    import jax.numpy as jnp

    def _L0_xattn_ref(hidden_states, encoder_outputs, token_type_ids, position_ids, ln_in_w, ln_post_attn_w, ln_post_cross_w, v_qkv, l_qkv, v_dense, l_dense, cq_w, ckv_w, cdense_w, v_gate, v_up, v_down, l_gate, l_up, l_down):
        import jax, jax.numpy as jnp
        import numpy as np
        H = 512
        NH = 16
        HD = H // NH
        CH = 256
        CC = 256
        CHD = CC // NH
        I = 1376
        B = 2
        L = 512
        LE = 256
        EPS = 1e-06

        def rms_norm(x, w):
            xf = x.astype(jnp.float32)
            var = jnp.mean(xf * xf, axis=-1, keepdims=True)
            return (w * (xf * jax.lax.rsqrt(var + EPS))).astype(x.dtype)

        def expert_mask(tt):
            vm = jnp.zeros(tt.shape, dtype=bool)
            vm = vm.at[:, :-1].set((tt[:, :-1] == 1) & (tt[:, 1:] == 1))
            return vm

        def rotate_half(x):
            d = x.shape[-1] // 2
            return jnp.concatenate([-x[..., d:], x[..., :d]], axis=-1)

        def apply_rotary(q, k, position_ids, seq_len):
            inv = 1.0 / 10000.0 ** (jnp.arange(0, HD, 2, dtype=jnp.float32) / HD)
            t = jnp.arange(seq_len, dtype=jnp.float32)
            freqs = jnp.outer(t, inv)
            emb = jnp.concatenate([freqs, freqs], axis=-1)
            cos = jnp.cos(emb)[position_ids][:, None].astype(q.dtype)
            sin = jnp.sin(emb)[position_ids][:, None].astype(q.dtype)
            return (q * cos + rotate_half(q) * sin, k * cos + rotate_half(k) * sin)

        def sdpa(q, k, v, causal):
            scale = 1.0 / np.sqrt(q.shape[-1])
            scores = jnp.einsum('bhqd,bhkd->bhqk', q * scale, k)
            if causal:
                mask = jnp.tril(jnp.ones((q.shape[-2], k.shape[-2]), dtype=bool))
                scores = jnp.where(mask, scores, jnp.finfo(jnp.float32).min)
            p = jax.nn.softmax(scores.astype(jnp.float32), axis=-1).astype(q.dtype)
            return jnp.einsum('bhqk,bhkd->bhqd', p, v)

        def heads(x, nh, hd):
            b, l, _ = x.shape
            return x.reshape(b, l, nh, hd).transpose(0, 2, 1, 3)
        b, l, _ = hidden_states.shape
        vm = expert_mask(token_type_ids)[..., None]
        residual = hidden_states
        x = rms_norm(hidden_states, ln_in_w)
        mixed = jnp.where(vm, x @ v_qkv, x @ l_qkv)
        q, k, v = jnp.split(mixed, 3, axis=-1)
        q, k, v = (heads(q, NH, HD), heads(k, NH, HD), heads(v, NH, HD))
        q, k = apply_rotary(q, k, position_ids, l)
        ctx = sdpa(q, k, v, causal=True)
        ctx = ctx.transpose(0, 2, 1, 3).reshape(b, l, H)
        attn_out = jnp.where(vm, ctx @ v_dense, ctx @ l_dense)
        hidden_states = residual + attn_out
        ci = rms_norm(hidden_states, ln_post_cross_w)
        cq = heads(ci @ cq_w, NH, CHD)
        ckv = encoder_outputs @ ckv_w
        ck, cv = jnp.split(ckv, 2, axis=-1)
        ck, cv = (heads(ck, NH, CHD), heads(cv, NH, CHD))
        cctx = sdpa(cq, ck, cv, causal=False)
        cctx = cctx.transpose(0, 2, 1, 3).reshape(b, l, CC)
        hidden_states = hidden_states + cctx @ cdense_w
        mi = rms_norm(hidden_states, ln_post_attn_w)
        v_out = jax.nn.silu(mi @ v_gate) * (mi @ v_up) @ v_down
        l_out = jax.nn.silu(mi @ l_gate) * (mi @ l_up) @ l_down
        hidden_states = hidden_states + jnp.where(vm, v_out, l_out)
        return hidden_states

    def _L1_xattn_ref(x, media, media_mask, ln_q_g, ln_q_b, Wq, Wkv, Wo, attn_gate, ln_ff_g, ln_ff_b, W1, W2, ff_gate):
        import jax, jax.numpy as jnp
        import numpy as np
        DIM = 512
        DIM_MEDIA = 256
        HEADS = 16
        DIM_HEAD = 64
        INNER = HEADS * DIM_HEAD
        FF_INNER = 4 * DIM
        B, N_TOK, N_LAT = (4, 512, 64)
        EPS = 1e-05

        def layernorm(x, g, b):
            mu = jnp.mean(x, axis=-1, keepdims=True)
            var = jnp.var(x, axis=-1, keepdims=True)
            return (x - mu) * jax.lax.rsqrt(var + EPS) * g + b
        scale = DIM_HEAD ** (-0.5)
        qn = layernorm(x, ln_q_g, ln_q_b)
        q = qn @ Wq * scale
        kv = media @ Wkv
        k, v = jnp.split(kv, 2, axis=-1)
        split_heads = lambda t: t.reshape(t.shape[0], t.shape[1], HEADS, DIM_HEAD).transpose(0, 2, 1, 3)
        q, k, v = (split_heads(q), split_heads(k), split_heads(v))
        sim = jnp.einsum('bhid,bhjd->bhij', q, k)
        neg_inf = jnp.finfo(sim.dtype).min
        sim = jnp.where(media_mask[:, None, None, :], sim, neg_inf)
        attn = jax.nn.softmax(sim, axis=-1)
        out = jnp.einsum('bhij,bhjd->bhid', attn, v)
        out = out.transpose(0, 2, 1, 3).reshape(x.shape[0], x.shape[1], INNER)
        attn_out = out @ Wo
        x = x + jnp.tanh(attn_gate) * attn_out
        h = layernorm(x, ln_ff_g, ln_ff_b)
        h = jax.nn.gelu(h @ W1, approximate=False) @ W2
        x = x + jnp.tanh(ff_gate) * h
        return x

    def _L2_xattn_ref(hidden_states, memory, W_mem, W_gate, b_gate, norm_w):
        import jax, jax.numpy as jnp
        import numpy as np
        EPS = 1e-06

        def _rmsnorm(x, w):
            var = jnp.mean(jnp.square(x), axis=-1, keepdims=True)
            return x * jax.lax.rsqrt(var + EPS) * w
        D = hidden_states.shape[-1]
        memory_proj = jnp.einsum('bme,de->bmd', memory, W_mem)
        scores = jnp.einsum('bnd,bmd->bnm', hidden_states, memory_proj) / jnp.sqrt(jnp.float32(D))
        attn = jax.nn.softmax(scores, axis=-1)
        memory_context = jnp.einsum('bnm,bmd->bnd', attn, memory_proj)
        gate_input = jnp.concatenate([hidden_states, memory_context], axis=-1)
        gate = jax.nn.sigmoid(jnp.einsum('bnf,df->bnd', gate_input, W_gate) + b_gate)
        fused = hidden_states + gate * memory_context
        return _rmsnorm(fused, norm_w)

    def _L3_xattn_ref(x, media, media_mask, ln_q_g, ln_q_b, Wq, Wkv, Wo, attn_gate, ln_ff_g, ln_ff_b, W1, W2, ff_gate):
        import jax, jax.numpy as jnp
        import numpy as np
        DIM = 512
        DIM_MEDIA = 256
        HEADS = 16
        DIM_HEAD = 64
        INNER = HEADS * DIM_HEAD
        FF_INNER = 4 * DIM
        B, N_TOK, N_LAT = (4, 512, 64)
        EPS = 1e-05

        def layernorm(x, g, b):
            mu = jnp.mean(x, axis=-1, keepdims=True)
            var = jnp.var(x, axis=-1, keepdims=True)
            return (x - mu) * jax.lax.rsqrt(var + EPS) * g + b
        scale = DIM_HEAD ** (-0.5)
        qn = layernorm(x, ln_q_g, ln_q_b)
        q = qn @ Wq * scale
        kv = media @ Wkv
        k, v = jnp.split(kv, 2, axis=-1)
        split_heads = lambda t: t.reshape(t.shape[0], t.shape[1], HEADS, DIM_HEAD).transpose(0, 2, 1, 3)
        q, k, v = (split_heads(q), split_heads(k), split_heads(v))
        sim = jnp.einsum('bhid,bhjd->bhij', q, k)
        neg_inf = jnp.finfo(sim.dtype).min
        sim = jnp.where(media_mask[:, None, None, :], sim, neg_inf)
        attn = jax.nn.softmax(sim, axis=-1)
        out = jnp.einsum('bhij,bhjd->bhid', attn, v)
        out = out.transpose(0, 2, 1, 3).reshape(x.shape[0], x.shape[1], INNER)
        attn_out = out @ Wo
        x = x + jnp.tanh(attn_gate) * attn_out
        h = layernorm(x, ln_ff_g, ln_ff_b)
        h = jax.nn.gelu(h @ W1, approximate=False) @ W2
        x = x + jnp.tanh(ff_gate) * h
        return x
    x = _L0_xattn_ref(x, ctx_1024, mask_BxS_ik0, pos_1xS, L0_xattn_ln_in_w, L0_xattn_ln_post_attn_w, L0_xattn_ln_post_cross_w, L0_xattn_v_qkv, L0_xattn_l_qkv, L0_xattn_v_dense, L0_xattn_l_dense, L0_xattn_cq_w, L0_xattn_ckv_w, L0_xattn_cdense_w, L0_xattn_v_gate, L0_xattn_v_up, L0_xattn_v_down, L0_xattn_l_gate, L0_xattn_l_up, L0_xattn_l_down)
    x = _L1_xattn_ref(x, ctx_1024, mask_BxS2_bk0, L1_xattn_ln_q_g, L1_xattn_ln_q_b, L1_xattn_Wq, L1_xattn_Wkv, L1_xattn_Wo, L1_xattn_attn_gate, L1_xattn_ln_ff_g, L1_xattn_ln_ff_b, L1_xattn_W1, L1_xattn_W2, L1_xattn_ff_gate)
    x = _L2_xattn_ref(x, ctx_1024, L2_xattn_W_mem, L2_xattn_W_gate, L2_xattn_b_gate, L2_xattn_norm_w)
    x = _L3_xattn_ref(x, ctx_1024, mask_BxS2_bk0, L3_xattn_ln_q_g, L3_xattn_ln_q_b, L3_xattn_Wq, L3_xattn_Wkv, L3_xattn_Wo, L3_xattn_attn_gate, L3_xattn_ln_ff_g, L3_xattn_ln_ff_b, L3_xattn_W1, L3_xattn_W2, L3_xattn_ff_gate)
    return x

_drawn_inputs = setup_inputs


def setup_inputs(seed=0):
    import zlib

    import numpy as np

    out = dict(_drawn_inputs(seed))
    spreads = {'L0_xattn_ln_in_w': (1.0, 0.6),
     'L0_xattn_ln_post_attn_w': (1.0, 0.6),
     'L0_xattn_ln_post_cross_w': (1.0, 0.6),
     'L1_xattn_ln_q_g': (1.0, 0.6),
     'L1_xattn_ln_q_b': (0.0, 0.8),
     'L1_xattn_ln_ff_g': (1.0, 0.6),
     'L1_xattn_ln_ff_b': (0.0, 0.8),
     'L2_xattn_norm_w': (1.0, 0.2),
     'L3_xattn_ln_q_g': (1.0, 0.6),
     'L3_xattn_ln_q_b': (0.0, 0.8),
     'L3_xattn_ln_ff_g': (1.0, 0.6),
     'L3_xattn_ln_ff_b': (0.0, 0.8)}
    factors = {'L0_xattn_v_qkv': 8.0,
     'L0_xattn_v_dense': 7.031,
     'L0_xattn_cq_w': 8.0,
     'L1_xattn_W1': 2.803,
     'L2_xattn_b_gate': 60.056,
     'L3_xattn_W1': 2.826,
     'L0_xattn_v_gate': 8.0,
     'L0_xattn_v_up': 8.0,
     'L0_xattn_v_down': 8.0}
    for name, (base, spread) in spreads.items():
        noise = np.random.default_rng([zlib.crc32(name.encode()), seed]).standard_normal(out[name].shape)
        drawn = base * np.exp(spread * noise) if base else spread * noise
        out[name] = jnp.asarray(drawn.astype(out[name].dtype))
    for name, factor in factors.items():
        out[name] = (out[name] * factor).astype(out[name].dtype)
    return out
```

```python
from contextlib import ExitStack

import concourse.bass as bass
from concourse import mybir

F32 = mybir.dt.float32
U8 = mybir.dt.uint8
I32 = mybir.dt.int32
ALU = mybir.AluOpType
ACT = mybir.ActivationFunctionType
AX_X = mybir.AxisListType.X

P = 128
B, S, D = 8, 112, 512
T = B * S
HALF = T // 2
BPH = B // 2
KD = D // P
S2, CC, KEYS = 375, 256, 125
KC = CC // P
CH = S2 // KEYS
NH = 16
ITILES = 11
INNER = 1024
FF = 2048
SLOT = 16 * P
RING = 5
BIG = 3.4028234663852886e38
LAG = 2
NPROB = 4
POOL = 3

STAGES = [("qk", 4), ("v", 2), ("dense", 2), ("cq", 1), ("cdense", 1),
          ("v_gu", 6), ("v_down", 4), ("l_gu", 6), ("l_down", 4),
          ("Wq1", 2), ("Wo1", 2), ("W11", 4), ("W21", 4),
          ("mem", 1), ("memT", 1), ("gate", 2),
          ("Wq3", 2), ("Wo3", 2), ("W13", 4), ("W23", 4)]
CHUNK0 = {}
NCHUNKS = 0
for _name, _n in STAGES:
    CHUNK0[_name] = NCHUNKS
    NCHUNKS += _n

VECS = ["L0_xattn_ln_in_w", "L0_xattn_ln_post_cross_w", "L0_xattn_ln_post_attn_w",
        "L1_xattn_ln_q_g", "L1_xattn_ln_q_b", "L1_xattn_ln_ff_g", "L1_xattn_ln_ff_b",
        "L2_xattn_norm_w", "L2_xattn_b_gate",
        "L3_xattn_ln_q_g", "L3_xattn_ln_q_b", "L3_xattn_ln_ff_g", "L3_xattn_ln_ff_b"]

C_ID, C_MEAN, C_ROT, C_COS, C_SIN, C_CAUSAL, C_POS, C_EVEN, C_ODD, C_END = (
    0, 128, 256, 384, 512, 640, 752, 753, 754, 755)

NORMS = [("rms", "L0_xattn_ln_in_w", None, 1e-6), ("rms", "L0_xattn_ln_post_cross_w", None, 1e-6),
         ("rms", "L0_xattn_ln_post_attn_w", None, 1e-6),
         ("ln", "L1_xattn_ln_q_g", "L1_xattn_ln_q_b", 1e-5), ("ln", "L1_xattn_ln_ff_g", "L1_xattn_ln_ff_b", 1e-5),
         ("rms", "L2_xattn_norm_w", None, 1e-6),
         ("ln", "L3_xattn_ln_q_g", "L3_xattn_ln_q_b", 1e-5), ("ln", "L3_xattn_ln_ff_g", "L3_xattn_ln_ff_b", 1e-5)]
SPLIT = {0, 2}


class PoolPlan:

    def __init__(self):
        self.n = 0
        self.count = {"act": 0, "dve": 0}
        self.tiles = {}
        self.order = []

    def add(self, key, who):
        self.count[who] += 1
        self.tiles[key] = (self.n, who, self.count[who])
        self.order.append((who, self.count[who]))
        self.n += 1
        return self.n - 1


class Attention:

    def __init__(self, name, nh, nk, group, pvgroup, mask, units, sem):
        self.name, self.nh, self.nk, self.group, self.pvgroup, self.mask = name, nh, nk, group, pvgroup, mask
        self.chunks = 1 if nk <= P else CH
        self.kw = nk // self.chunks
        self.steps = B * nh
        self.units = units
        self.pvlag = LAG + group
        self.scored = sem(name + "_scored")
        self.maxed = sem(name + "_maxed")
        self.exped = sem(name + "_exped")
        self.recip = sem(name + "_recip")
        self.scaled = sem(name + "_scaled")
        self.turned = sem(name + "_turned")
        self.probs_out = sem(name + "_probs_out")
        self.summed = sem(name + "_summed")
        self.out = sem(name + "_out")
        self.ctx_in = [sem(f"{name}_ctx_in{i}") for i in range(2)]
        self.mask_in = [sem(f"{name}_mask_in{i}") for i in range(2)]
        self.masked = sem(name + "_masked")


def build(nc, xT, ctxF, ctxK, kmask, tt, pos, walls, kvw0, kvw1, kvw3, vecs, gates, consts, outT):
    ctx = ExitStack()
    with ctx:
        def sb(name, shape, dt=F32):
            return ctx.enter_context(nc.sbuf_tensor(name, shape, dt))

        def sem(name):
            return ctx.enter_context(nc.semaphore(name))

        ring = sb("ring", [P, RING, SLOT])
        kvw = sb("kvw", [P, 2 * FF])
        x = sb("x", [P, KD, T])
        xa = sb("xa", [P, KD, T])
        xb = sb("xb", [P, KD, T])
        big = sb("big", [P, 77248 // 4])
        ctxb = sb("ctxb", [P, 2, KC, S2])
        mask8 = sb("mask8", [S, 2, S2], U8)
        maskf = sb("maskf", [S, 2, S2])
        vm = sb("vm", [P, B, S])
        scr = sb("scr", [P, 4, HALF])
        sq = sb("sq", [P, 2, HALF])
        std = sb("std", [P, HALF])
        rstd = sb("rstd", [P, HALF])
        cst = sb("cst", [P, C_END])
        vec = sb("vec", [P, len(VECS), KD])
        cosT = sb("cosT", [P, S])
        sinT = sb("sinT", [P, S])
        gate_in = sb("gate_in", [P, 4])
        gate_t = sb("gate_t", [P, 4])
        nmin = sb("nmin", [S, NPROB])
        rsum = sb("rsum", [S, NPROB])
        rinv = sb("rinv", [S, NPROB])
        eps = sb("eps", [P, 2])

        def flat(t):
            return t[:].rearrange("p a b -> p (a b)")

        def view(off, *dims, rows=P):
            n = 1
            for d in dims:
                n *= d
            v = big[0:rows, off:off + n]
            if len(dims) == 1:
                return v
            names = "abcd"[:len(dims)]
            return v.rearrange("p (%s) -> p %s" % (" ".join(names), " ".join(names)),
                               **{c: d for c, d in zip(names, dims)})

        xbf = flat(xb)
        masked_s = [xbf[0:S, i * S2:(i + 1) * S2] for i in range(2)]
        probs = [xbf[0:S, (2 + i) * S2:(3 + i) * S2] for i in range(NPROB)]
        probsT = [xbf[0:P, (6 + i) * S2:(6 + i) * S2 + 4 * S] for i in range(2)]
        probsT[1] = xbf[0:P, 6 * S2 + 4 * S:6 * S2 + 8 * S]
        O_KV, O_V = 28672 // 4, 52672 // 4
        qT = view(0, KD, T)
        kT = view(KD * T, KD, T)
        vS = view(O_KV, B, D, rows=S)
        qc = view(0, KC, T)
        kc = [view(O_KV + i * 3000, KC, 2, S2) for i in range(2)]
        vc = [view(O_V + i * 3072, CH, 2, CC, rows=KEYS) for i in range(2)]
        hid0 = view(0, ITILES, T)
        q1 = view(0, INNER // P, T)
        k1 = [view(O_KV + i * 3000, INNER // P, S2) for i in range(2)]
        v1 = [view(O_V + i * 3072, CH, INNER, rows=KEYS) for i in range(2)]
        hid1 = view(0, FF // P, T)
        hw = view(0, KC, T)
        pc = view(KC * T, KC, T)
        mc = view(2 * KC * T, KD, T)
        ctxt = [view(O_V + i * 3072, CH, CC, rows=KEYS) for i in range(2)]

        psum = ctx.enter_context(nc.psum_tensor("psum", [P, 8, 512], F32))

        def pool_bank(n):
            return psum[:, n % POOL, :]

        def s_bank(s):
            return psum[0:S, 3 + s % 2, :]

        def t_bank(g):
            return psum[:, 5 + g % 2, :]

        pv_bank = psum[:, 7, :]

        ident = cst[:, C_ID:C_ID + P]
        mean_w = cst[:, C_MEAN:C_MEAN + P]
        rot_w = cst[:, C_ROT:C_ROT + P]
        causal = cst[0:S, C_CAUSAL:C_CAUSAL + S]

        w_in = [sem(f"w_in{i}") for i in range(RING)]
        tile_ready = sem("tile_ready")
        emptied = {"act": sem("emptied_act"), "dve": sem("emptied_dve")}
        x_in = sem("x_in")
        cst_in = sem("cst_in")
        vec_in = sem("vec_in")
        tt_in = sem("tt_in")
        pos_in = sem("pos_in")
        gate_in_s = sem("gate_in_s")
        gate_done = sem("gate_done")
        kvw_in = [sem(f"kvw_in{i}") for i in range(3)]
        vm_done = sem("vm_done")
        eps_done = sem("eps_done")
        onehot_done = sem("onehot_done")
        rope_done = sem("rope_done")
        fused_done = sem("fused_done")
        vzero = sem("vzero")
        chain = sem("chain")
        out_done = sem("out_done")
        sq_ready = sem("sq_ready")
        sq_used = sem("sq_used")
        std_used = sem("std_used")
        normed = sem("normed")
        biased = sem("biased")
        centred = sem("centred")

        att_self = Attention("self", NH, S, 4, 4, "causal", [], sem)
        att_c0 = Attention("cross0", NH, S2, 1, 8, None, [(h, h) for h in range(5)], sem)
        att_1 = Attention("cross1", NH, S2, 1, 2, "keys", [(h, h) for h in range(14)], sem)
        att_2 = Attention("memory", 1, S2, 1, 1, None, [], sem)
        att_3 = Attention("cross3", NH, S2, 1, 2, "keys", [(h, h) for h in range(14)], sem)

        plan = PoolPlan()
        chunk_last = {}

        order = [(nn, half) for nn in range(5) for half in range(2)] + [
            (5, 0), (6, 0), (5, 1), (6, 1), (7, 0), (7, 1)]
        turn_of = {key: i for i, key in enumerate(order)}
        ln_turn = {key: i for i, key in enumerate([o for o in order if NORMS[o[0]][0] == "ln"])}

        def norm_done(eng, nn, half):
            if NORMS[nn][0] == "ln":
                eng.wait_ge(biased, ln_turn[nn, half] + 1)
            else:
                eng.wait_ge(normed, turn_of[nn, half] + 1)

        def tile_done(eng, key):
            _, who, count = plan.tiles[key]
            eng.wait_ge(emptied[who], count)

        def hcols(half):
            return slice(half * HALF, (half + 1) * HALF)

        def bcols(b):
            return slice(b * S, (b + 1) * S)

        def by_chunk(name, chunks, per, hooks, last=None):
            seq = []
            for c in range(chunks):
                for half in range(2):
                    for m in range(c * per, min((c + 1) * per, last or 99)):
                        seq.append(("tile", half, m, c))
                        seq += hooks.get((c, half, m), [])
            return seq

        def by_half(name, ms, mpc, hooks):
            seq = []
            for half in range(2):
                for m in range(ms):
                    seq.append(("tile", half, m, m // mpc))
                    seq += hooks.get((half, m), [])
            return seq

        def rms_pre(nn):
            return {(1, 0): [("norm", nn, 0, "v")], (1, 1): [("norm", nn, 0, "f")]}

        def rms_post(nn, first=0):
            return {(0, 0, 0): [("norm", nn, 1, "v")], (0, 0, 1): [("norm", nn, 1, "f")]}

        def ln_pre(nn):
            return {(1, 0): [("norm", nn, 0, "m")], (1, 1): [("norm", nn, 0, "v")], (1, 2): [("norm", nn, 0, "f")]}

        def ln_post(nn):
            return {(0, 0, 0): [("norm", nn, 1, "m")], (0, 0, 1): [("norm", nn, 1, "v")], (0, 0, 2): [("norm", nn, 1, "f")]}

        SEQ = {
            "qk": [("norm", 0, 0, "v"), ("norm", 0, 0, "f")] + by_chunk("qk", 4, 2, rms_post(0)),
            "dense": by_half("dense", 4, 2, rms_pre(1)),
            "cq": by_chunk("cq", 1, 2, rms_post(1)),
            "cdense": by_half("cdense", 4, 4, rms_pre(2)),
            "v_gu": by_chunk("v_gu", 6, 2, rms_post(2), ITILES),
            "v_down": by_half("v_down", 4, 1, {}),
            "l_gu": by_chunk("l_gu", 6, 2, {}, ITILES),
            "l_down": by_half("l_down", 4, 1, ln_pre(3)),
            "Wq1": by_chunk("Wq1", 2, 4, ln_post(3)),
            "Wo1": by_half("Wo1", 4, 2, ln_pre(4)),
            "W11": by_chunk("W11", 4, 4, ln_post(4)),
            "W21": by_half("W21", 4, 1, {}),
            "mem": by_half("mem", 2, 2, {}),
            "memT": by_half("memT", 4, 4, {}),
            "gate": by_half("gate", 4, 2, {(1, 0): [("norm", 5, 0, "v")], (1, 1): [("norm", 5, 0, "f")],
                                            (1, 2): [("norm", 6, 0, "m")],
                                            (1, 3): [("norm", 6, 0, "v"), ("norm", 6, 0, "f")]}),
            "Wq3": by_chunk("Wq3", 2, 4, {(0, 0, 0): [("norm", 5, 1, "v")], (0, 0, 1): [("norm", 5, 1, "f")],
                                           (0, 0, 2): [("norm", 6, 1, "m")],
                                           (0, 0, 3): [("norm", 6, 1, "v"), ("norm", 6, 1, "f")]}),
            "Wo3": by_half("Wo3", 4, 2, ln_pre(7)),
            "W13": by_chunk("W13", 4, 4, ln_post(7)),
            "W23": by_half("W23", 4, 1, {}),
        }

        GU = [(gu,) + it[1:3] for gu in ("v_gu", "l_gu") for it in SEQ[gu] if it[0] == "tile"]
        RAW = [("qk",) + it[1:3] for it in SEQ["qk"] if it[0] == "tile"]

        X_OF_NORM = {1: "dense", 2: "cdense", 3: "l_down", 4: "Wo1", 7: "Wo3"}

        def x_ready(eng, nn, half, k):
            if nn == 0:
                eng.wait_ge(x_in, 16)
            elif nn == 5:
                eng.wait_ge(fused_done, half * KD + k + 1)
            elif nn == 6:
                eng.wait_ge(normed, turn_of[5, half] + 1)
            else:
                tile_done(eng, (X_OF_NORM[nn], half, k))

        def norm_src(nn):
            return xb if nn == 5 else x

        block = ctx.enter_context(nc.Block())

        @block.tensor
        def _(pe):
            def begin_tile(key, who):
                n = plan.add(key, who)
                if n >= POOL:
                    w, count = plan.order[n - POOL]
                    pe.wait_ge(emptied[w], count)
                return n

            def product(out, pairs):
                for i, (lhsT, rhs) in enumerate(pairs):
                    last = nc.tensor.matmul(out, lhsT, rhs, start=(i == 0), stop=(i == len(pairs) - 1))
                return last

            def chunk(name, c):
                n = CHUNK0[name] + c
                pe.wait_ge(w_in[n % RING], 16 * (n // RING + 1))
                return ring[:, n % RING, :]

            def norm_part(nn, half, part):
                kind = NORMS[nn][0]
                if part == "m":
                    n = begin_tile(("mean", nn, half), "dve")
                    for k in range(KD):
                        x_ready(pe, nn, half, k)
                        last = nc.tensor.matmul(pool_bank(n)[:, 0:HALF], mean_w, x[:, k, hcols(half)],
                                                start=(k == 0), stop=(k == KD - 1))
                    last.then_inc(tile_ready, 1)
                elif part == "v":
                    n = begin_tile(("var", nn, half), "act")
                    for k in range(KD):
                        i = turn_of[nn, half] * KD + k
                        pe.wait_ge(sq_ready, i + 1)
                        last = nc.tensor.matmul(pool_bank(n)[:, 0:HALF], mean_w, sq[:, i % 2, :],
                                                start=(k == 0), stop=(k == KD - 1))
                        if k < KD - 1:
                            last.then_inc(sq_used, 1)
                    last.then_inc(tile_ready, 1)

            def stage(name, rhs_of, blocks, who, first_of=None, ready=None, whole=False):
                seq = SEQ[name]
                last_use = {}
                for j, it in enumerate(seq):
                    if it[0] == "tile":
                        last_use[it[3]] = j
                for j, it in enumerate(seq):
                    if it[0] == "norm":
                        norm_part(*it[1:])
                        continue
                    _, half, m, c = it
                    w = chunk(name, c)
                    mpc = first_of
                    if ready:
                        ready(half, m)
                    for part in range(whole or 1):
                        n = begin_tile((name, half, m, part) if whole else (name, half, m), who[part] if whole else who)
                        base = ((m % mpc) * (whole or 1) + part) * blocks
                        last = product(pool_bank(n)[:, 0:HALF],
                                       [(w[:, (base + i) * P:(base + i + 1) * P], rhs_of(half, i)) for i in range(blocks)])
                        last.then_inc(tile_ready, 1)
                    if last_use[c] == j:
                        chunk_last[CHUNK0[name] + c] = plan.n

            def kv_unit(a, b, u):
                if a is att_c0:
                    w = kvw[:, 0:KC * 2 * CC].rearrange("p (k n) -> p k n", k=KC)
                    nk_tiles, width, vper = KC, CC, CC
                else:
                    w = kvw[:, :].rearrange("p (k n) -> p k n", k=KC)
                    nk_tiles, width, vper = INNER // P, INNER, 512
                pe.wait_ge(a.ctx_in[b % 2], 16 * (b // 2 + 1))
                n = begin_tile((a.name, b, u), "act")
                cb = ctxb[:, b % 2]
                if u < nk_tiles:
                    last = product(pool_bank(n)[:, 0:S2],
                                   [(w[:, k, u * P:(u + 1) * P], cb[:, k, :]) for k in range(KC)])
                else:
                    v = u - nk_tiles
                    per = width // vper
                    c, part = v // per, v % per
                    o = width + part * vper
                    last = product(pool_bank(n)[0:KEYS, 0:vper],
                                   [(cb[:, k, c * KEYS:(c + 1) * KEYS], w[:, k, o:o + vper]) for k in range(KC)])
                last.then_inc(tile_ready, 1)

            def scores(a, s):
                b, h = s // a.nh, s % a.nh
                out = s_bank(s)[:, 0:a.nk]
                if a is att_self:
                    r = slice(32 * (h % 4), 32 * (h % 4) + 32)
                    ops = [(qT[r, h // 4, bcols(b)], kT[r, h // 4, bcols(b)])]
                elif a is att_c0:
                    r = slice(32 * (h % 8 // 2), 32 * (h % 8 // 2) + 32)
                    ops = [(qc[r, h // 8, bcols(b)], kc[b % 2][r, h // 8, h % 2, :])]
                elif a is att_2:
                    ops = [(hw[:, k, bcols(b)], ctxb[:, b % 2, k, :]) for k in range(KC)]
                else:
                    r = slice(64 * (h % 2), 64 * (h % 2) + 64)
                    ops = [(q1[r, h // 2, bcols(b)], k1[b % 2][r, h // 2, :])]
                if h == 0:
                    if a is att_self:
                        pe.wait_ge(rope_done, 16)
                        tile_done(pe, ("vproj", B - 1))
                    elif a is att_2:
                        pe.wait_ge(a.ctx_in[b % 2], 16 * (b // 2 + 1))
                        tile_done(pe, ("mem", 1, 1))
                    else:
                        tile_done(pe, ("cq", 1, 1) if a is att_c0 else ("Wq" + a.name[-1], 1, 7))
                        tile_done(pe, (a.name, b, len(a.units) - 1))
                if s >= 2:
                    pe.wait_ge(a.maxed if a.mask else a.exped, s - 1)
                product(out, ops).then_inc(a.scored, 1)

            def turn(a, s):
                g = s // a.group
                pe.wait_ge(a.scaled, s + 1)
                if g >= 2 and s % a.group == 0:
                    pe.wait_ge(a.probs_out, g - 1)
                for c in range(a.chunks):
                    o = (s % a.group + c) * S
                    last = nc.tensor.transpose(t_bank(g)[0:a.kw, o:o + S],
                                               probs[s % NPROB][:, c * a.kw:(c + 1) * a.kw], ident[0:S, 0:S])
                last.then_inc(a.turned, 1)

            def weigh(a, s):
                b, h = s // a.nh, s % a.nh
                g = s // a.group
                pe.wait_ge(a.probs_out, g + 1)
                if s % a.pvgroup == 0 and s >= a.pvgroup:
                    pe.wait_ge(a.out, s // a.pvgroup)
                pT = probsT[g % 2]
                if a is att_self:
                    last = nc.tensor.matmul(pv_bank[32 * (h % 4):32 * (h % 4) + 32, 0:S], vS[:, b, 32 * h:32 * h + 32],
                                            pT[0:S, (h % 4) * S:(h % 4 + 1) * S], start=True, stop=True)
                elif a is att_c0:
                    j = h // 2
                    o = 32 * (j % 4)
                    for c in range(CH):
                        last = nc.tensor.matmul(pv_bank[o:o + 32, 0:S], vc[b % 2][:, c, h % 2, 32 * j:32 * j + 32],
                                                pT[0:KEYS, c * S:(c + 1) * S],
                                                start=(h % 2 == 0 and c == 0), stop=(h % 2 == 1 and c == CH - 1))
                elif a is att_2:
                    pe.wait_ge(a.mask_in[b % 2], 16 * (b // 2 + 1))
                    for e in range(KC):
                        last = product(pv_bank[:, e * S:(e + 1) * S],
                                       [(ctxt[b % 2][:, c, e * P:(e + 1) * P], pT[0:KEYS, c * S:(c + 1) * S])
                                        for c in range(CH)])
                else:
                    o = 64 * (h % 2)
                    for c in range(CH):
                        last = nc.tensor.matmul(pv_bank[o:o + 64, 0:S], v1[b % 2][:, c, 64 * h:64 * h + 64],
                                                pT[0:KEYS, c * S:(c + 1) * S], start=(c == 0), stop=(c == CH - 1))
                last.then_inc(a.summed, 1)

            def attention(a):
                for s in range(a.steps + a.pvlag):
                    if s < a.steps:
                        scores(a, s)
                        for h, u in a.units:
                            if s % a.nh == h and s // a.nh + 1 < B:
                                kv_unit(a, s // a.nh + 1, u)
                    if 0 <= s - LAG < a.steps:
                        turn(a, s - LAG)
                    if s >= a.pvlag:
                        weigh(a, s - a.pvlag)

            pe.wait_ge(cst_in, 16)
            pe.wait_ge(onehot_done, 1)
            for i, c in enumerate((C_COS, C_SIN)):
                n = begin_tile(("table", i), "act")
                nc.tensor.matmul(pool_bank(n)[:, 0:S], cst[0:S, c:c + P], scr[0:S, 0, 0:S],
                                 start=True, stop=True).then_inc(tile_ready, 1)

            def xab(half, i):
                return (xa if i < KD else xb)[:, i % KD, hcols(half)]

            def rotate(i):
                tile_done(pe, RAW[i])
                n = begin_tile(("rot", i), "dve")
                nc.tensor.matmul(pool_bank(n)[:, 0:HALF], rot_w, scr[:, i % 2, :],
                                 start=True, stop=True).then_inc(tile_ready, 1)

            seq = SEQ["qk"]
            raw = 0
            for j, it in enumerate(seq):
                if it[0] == "norm":
                    norm_part(*it[1:])
                    continue
                _, half, m, c = it
                w = chunk("qk", c)
                norm_done(pe, 0, half)
                n = begin_tile(("qk", half, m), "act")
                last = product(pool_bank(n)[:, 0:HALF],
                               [(w[:, ((m % 2) * 8 + i) * P:((m % 2) * 8 + i + 1) * P], xab(half, i)) for i in range(8)])
                last.then_inc(tile_ready, 1)
                chunk_last[CHUNK0["qk"] + c] = plan.n
                if raw >= 1:
                    rotate(raw - 1)
                raw += 1
            rotate(raw - 1)

            wv = [chunk("v", e).rearrange("p (k n) -> p k n", k=KD) for e in range(2)]
            for b in range(B):
                n = begin_tile(("vproj", b), "act")
                product(pool_bank(n)[0:S, :],
                        [((xa, xb)[e][:, k, bcols(b)], wv[e][:, k, :]) for e in range(2) for k in range(KD)])\
                    .then_inc(tile_ready, 1)
            for e in range(2):
                chunk_last[CHUNK0["v"] + e] = plan.n

            attention(att_self)

            stage("dense", lambda half, i: (qT if i < KD else kT)[:, i % KD, hcols(half)], 8, "dve", 2,
                  ready=lambda half, m: pe.wait_ge(att_self.out, att_self.steps // 4))
            pe.wait_ge(kvw_in[0], 16)
            for _, u in att_c0.units:
                kv_unit(att_c0, 0, u)
            stage("cq", lambda half, i: xa[:, i, hcols(half)], KD, "act", 2,
                  ready=lambda half, m: norm_done(pe, 1, half))
            attention(att_c0)
            stage("cdense", lambda half, i: qc[:, i, hcols(half)], KC, "dve", 4,
                  ready=lambda half, m: pe.wait_ge(att_c0.out, att_c0.steps // 8))
            for e, src in ((0, xa), (1, xb)):
                gu, down = ("v_gu", "v_down") if e == 0 else ("l_gu", "l_down")
                stage(gu, lambda half, i, src=src: src[:, i, hcols(half)], KD, ("act", "dve"), 2,
                      ready=lambda half, m: norm_done(pe, 2, half), whole=2)
                stage(down, lambda half, i: hid0[:, i, hcols(half)], ITILES, "dve", 1,
                      ready=lambda half, m, gu=gu: tile_done(pe, (gu, 1, ITILES - 1, 1)))
            for L, a, nq, nf, kin in ((1, att_1, 3, 4, 1), (3, att_3, 6, 7, 2)):
                pe.wait_ge(kvw_in[kin], 16)
                for _, u in a.units:
                    kv_unit(a, 0, u)
                stage(f"Wq{L}", lambda half, i: xa[:, i, hcols(half)], KD, "act", 4,
                      ready=lambda half, m, nq=nq: norm_done(pe, nq, half))
                attention(a)
                stage(f"Wo{L}", lambda half, i: q1[:, i, hcols(half)], INNER // P, "dve", 2,
                      ready=lambda half, m, a=a: pe.wait_ge(a.out, a.steps // 2))
                stage(f"W1{L}", lambda half, i: xa[:, i, hcols(half)], KD, "act", 4,
                      ready=lambda half, m, nf=nf: norm_done(pe, nf, half))
                stage(f"W2{L}", lambda half, i: hid1[:, i, hcols(half)], FF // P, "dve", 1,
                      ready=lambda half, m, L=L: tile_done(pe, (f"W1{L}", 1, FF // P - 1)))
                if L == 1:
                    stage("mem", lambda half, i: x[:, i, hcols(half)], KD, "act", 2,
                          ready=lambda half, m: tile_done(pe, ("W21", half, KD - 1)))
                    attention(att_2)
                    stage("memT", lambda half, i: pc[:, i, hcols(half)], KC, "act", 4,
                          ready=lambda half, m: pe.wait_ge(att_2.out, B))
                    stage("gate", lambda half, i: (x if i < KD else mc)[:, i % KD, hcols(half)], 8, "act", 2,
                          ready=lambda half, m: tile_done(pe, ("memT", 1, KD - 1)))


        @block.scalar
        def _(act):
            given = [0]

            def empty(key):
                n, who, count = plan.tiles[key]
                given[0] += 1
                assert who == "act" and count == given[0]
                act.wait_ge(tile_ready, n + 1)
                return pool_bank(n)

            def norm_part(nn, half, part):
                kind, wname, bname, e = NORMS[nn]
                src = norm_src(nn) if kind == "rms" else xa
                if part == "v":
                    for k in range(KD):
                        i = turn_of[nn, half] * KD + k
                        if kind == "rms":
                            x_ready(act, nn, half, k)
                        else:
                            if k < KD - 1:
                                act.wait_ge(centred, ln_turn[nn, half] * (KD - 1) + k + 1)
                            else:
                                tile_done(act, ("mean", nn, half))
                        if i >= 2:
                            j = i - 2
                            done = j - j // KD
                            if j % KD == KD - 1:
                                nj = plan.tiles[("var",) + order[j // KD]][0]
                                act.wait_ge(tile_ready, nj + 1)
                            else:
                                act.wait_ge(sq_used, done + 1)
                        nc.scalar.activation(sq[:, i % 2, :], src[:, k, hcols(half)], ACT.Square).then_inc(sq_ready, 1)
                    bank = empty(("var", nn, half))
                    if turn_of[nn, half] >= 1:
                        act.wait_ge(std_used, turn_of[nn, half])
                    nc.scalar.activation(std[:, :], bank[:, 0:HALF], ACT.Sqrt,
                                         bias=eps[:, 0:1] if e == 1e-6 else eps[:, 1:2]).then_inc(emptied["act"], 1)
                elif part == "f" and kind == "ln":
                    act.wait_ge(normed, turn_of[nn, half] + 1)
                    for k in range(KD):
                        last = nc.scalar.activation(xa[:, k, hcols(half)], xa[:, k, hcols(half)], ACT.Identity,
                                                    bias=vec[:, VECS.index(bname), k:k + 1])
                    last.then_inc(biased, 1)

            def stage(name, each):
                for it in SEQ[name]:
                    if it[0] == "norm":
                        norm_part(*it[1:])
                    elif each:
                        each(it[1], it[2])

            def kv_unit(a, b, u):
                bank = empty((a.name, b, u))
                nk_tiles = KC if a is att_c0 else INNER // P
                if b >= 2:
                    if u < nk_tiles:
                        act.wait_ge(a.scored, a.nh * (b - 1))
                    else:
                        act.wait_ge(a.summed, a.nh * (b - 1))
                if a is att_c0:
                    if u < KC:
                        for par, col in ((0, C_EVEN), (1, C_ODD)):
                            last = nc.scalar.activation(kc[b % 2][:, u, par, :], bank[:, 0:S2], ACT.Copy,
                                                        scale=cst[:, col:col + 1])
                    else:
                        if b < 2 and u == KC:
                            act.wait_ge(vzero, b + 1)
                        c = u - KC
                        for par in range(2):
                            dst = vc[b % 2][:, c, par, :].rearrange("p (j t d) -> p j t d", t=2, d=16)[:, :, par, :]
                            srcv = bank[0:KEYS, 0:CC].rearrange("p (j t d) -> p j t d", t=2, d=16)[:, :, par, :]
                            last = nc.scalar.copy(dst, srcv)
                else:
                    if u < nk_tiles:
                        last = nc.scalar.copy(k1[b % 2][:, u, :], bank[:, 0:S2])
                    else:
                        c, part = (u - nk_tiles) // 2, (u - nk_tiles) % 2
                        last = nc.scalar.copy(v1[b % 2][:, c, part * 512:(part + 1) * 512], bank[0:KEYS, :])
                last.then_inc(emptied["act"], 1)

            def attention(a):
                for s in range(a.steps + LAG):
                    if s < a.steps:
                        act.wait_ge(a.maxed, s + 1)
                        if s >= NPROB:
                            act.wait_ge(a.turned, s - NPROB + 1)
                        src = masked_s[s % 2][:, 0:a.nk] if a.mask else s_bank(s)[:, 0:a.nk]
                        nc.scalar.activation(probs[s % NPROB][:, 0:a.nk], src, ACT.Exp, scale=-1.0,
                                             bias=nmin[:, s % NPROB:s % NPROB + 1],
                                             accum_out=rsum[:, s % NPROB:s % NPROB + 1]).then_inc(a.exped, 1)
                        for h, u in a.units:
                            if s % a.nh == h and s // a.nh + 1 < B:
                                kv_unit(a, s // a.nh + 1, u)
                    t = s - LAG
                    if t >= 0 and t % a.group == a.group - 1:
                        g = t // a.group
                        act.wait_ge(a.turned, t + 1)
                        if g >= 2:
                            act.wait_ge(a.summed, (g - 1) * a.group)
                        w = max(a.group, a.chunks) * S
                        nc.scalar.copy(probsT[g % 2][0:a.kw, 0:w], t_bank(g)[0:a.kw, 0:w]).then_inc(a.probs_out, 1)

            act.dma_start(x[:, :, :], xT).then_inc(x_in, 16)
            act.wait_ge(eps_done, 2)
            act.wait_ge(gate_in_s, 16)
            nc.scalar.activation(gate_t[:, :], gate_in[:, :], ACT.Tanh).then_inc(gate_done, 1)
            for i, dst in enumerate((cosT, sinT)):
                bank = empty(("table", i))
                nc.scalar.copy(dst[:, :], bank[:, 0:S]).then_inc(emptied["act"], 1)

            def qk(half, m):
                i = RAW.index(("qk", half, m))
                bank = empty(("qk", half, m))
                if i >= 2:
                    act.wait_ge(rope_done, i - 1)
                nc.scalar.mul(scr[:, i % 2, :], bank[:, 0:HALF],
                              -float(32) ** -0.5 if m < KD else 1.0).then_inc(emptied["act"], 1)

            stage("qk", qk)
            for b in range(B):
                bank = empty(("vproj", b))
                nc.scalar.copy(vS[:, b, :], bank[0:S, :]).then_inc(emptied["act"], 1)
            attention(att_self)
            stage("dense", None)
            for _, u in att_c0.units:
                kv_unit(att_c0, 0, u)

            def cq(half, m):
                bank = empty(("cq", half, m))
                nc.scalar.mul(qc[:, m, hcols(half)], bank[:, 0:HALF], -0.25).then_inc(emptied["act"], 1)

            stage("cq", cq)
            attention(att_c0)
            stage("cdense", None)
            ng = [0]
            for gu, down in (("v_gu", "v_down"), ("l_gu", "l_down")):
                def gate(half, m, gu=gu):
                    i = ng[0]
                    ng[0] += 1
                    bank = empty((gu, half, m, 0))
                    if i >= 2:
                        tile_done(act, GU[i - 2] + (1,))
                    nc.scalar.activation(scr[:, i % 2, :], bank[:, 0:HALF], ACT.Silu).then_inc(emptied["act"], 1)

                stage(gu, gate)
                stage(down, None)
            for L, a in ((1, att_1), (3, att_3)):
                for _, u in a.units:
                    kv_unit(a, 0, u)

                def wq(half, m, L=L):
                    bank = empty((f"Wq{L}", half, m))
                    nc.scalar.mul(q1[:, m, hcols(half)], bank[:, 0:HALF], -0.125).then_inc(emptied["act"], 1)

                stage(f"Wq{L}", wq)
                attention(a)
                stage(f"Wo{L}", None)

                def w1(half, m, L=L):
                    bank = empty((f"W1{L}", half, m))
                    nc.scalar.activation(hid1[:, m, hcols(half)], bank[:, 0:HALF], ACT.Gelu).then_inc(emptied["act"], 1)

                stage(f"W1{L}", w1)
                stage(f"W2{L}", None)
                if L == 1:
                    def memp(half, m):
                        bank = empty(("mem", half, m))
                        nc.scalar.mul(hw[:, m, hcols(half)], bank[:, 0:HALF], -float(D) ** -0.5).then_inc(emptied["act"], 1)

                    stage("mem", memp)
                    attention(att_2)

                    def memt(half, m):
                        bank = empty(("memT", half, m))
                        nc.scalar.copy(mc[:, m, hcols(half)], bank[:, 0:HALF]).then_inc(emptied["act"], 1)

                    stage("memT", memt)

                    def fgate(half, m):
                        i = half * KD + m
                        bank = empty(("gate", half, m))
                        if i >= 2:
                            act.wait_ge(fused_done, i - 1)
                        nc.scalar.activation(scr[:, i % 2, :], bank[:, 0:HALF], ACT.Sigmoid,
                                             bias=vec[:, VECS.index("L2_xattn_b_gate"), m:m + 1])\
                            .then_inc(emptied["act"], 1)

                    stage("gate", fgate)

        @block.vector
        def _(dve):
            given = [0]
            links = [0]

            def link(ins):
                links[0] += 1
                ins.then_inc(chain, 1)
                return links[0]

            def empty(key):
                n, who, count = plan.tiles[key]
                given[0] += 1
                assert who == "dve" and count == given[0]
                dve.wait_ge(tile_ready, n + 1)
                return pool_bank(n)

            def norm_part(nn, half, part):
                kind, wname, bname, e = NORMS[nn]
                cols = hcols(half)
                w = vec[:, VECS.index(wname), :]
                if part == "m":
                    bank = empty(("mean", nn, half))
                    for k in range(KD):
                        x_ready(dve, nn, half, k)
                        ins = nc.vector.tensor_sub(xa[:, k, cols], x[:, k, cols], bank[:, 0:HALF])
                        ins.then_inc(centred if k < KD - 1 else emptied["dve"], 1)
                elif part == "f":
                    tile_done(dve, ("var", nn, half))
                    nc.vector.reciprocal(rstd[:, :], std[:, :]).then_inc(std_used, 1)
                    dve.wait_ge(std_used, turn_of[nn, half] + 1)
                    if kind == "ln":
                        for k in range(KD):
                            last = nc.vector.scalar_tensor_tensor(xa[:, k, cols], xa[:, k, cols], w[:, k:k + 1],
                                                                  rstd[:, :], ALU.mult, ALU.mult)
                        last.then_inc(normed, 1)
                        return
                    src = norm_src(nn)
                    dst = xb if nn in SPLIT else (x if nn == 5 else xa)
                    for k in range(KD):
                        x_ready(dve, nn, half, k)
                        last = nc.vector.scalar_tensor_tensor(dst[:, k, cols], src[:, k, cols], w[:, k:k + 1],
                                                              rstd[:, :], ALU.mult, ALU.mult)
                        if nn in SPLIT:
                            link(last)
                    if nn not in SPLIT:
                        last.then_inc(normed, 1)
                        return
                    vmh = vm[:, half * BPH:(half + 1) * BPH, :].rearrange("p b s -> p (b s)")
                    first = links[0] - KD
                    for k in range(KD):
                        dve.wait_ge(chain, first + k + 1)
                        link(nc.vector.tensor_mul(xa[:, k, cols], xb[:, k, cols], vmh))
                    for k in range(KD):
                        dve.wait_ge(chain, first + KD + k + 1)
                        last = nc.vector.tensor_sub(xb[:, k, cols], xb[:, k, cols], xa[:, k, cols])
                    last.then_inc(normed, 1)

            def stage(name, each):
                for it in SEQ[name]:
                    if it[0] == "norm":
                        norm_part(*it[1:])
                    elif each:
                        each(it[1], it[2])

            def residual(name, gate=None):
                def each(half, m):
                    bank = empty((name, half, m))
                    xs = x[:, m, hcols(half)]
                    if gate is None:
                        ins = nc.vector.tensor_add(xs, bank[:, 0:HALF], xs)
                    else:
                        ins = nc.vector.scalar_tensor_tensor(xs, bank[:, 0:HALF], gate_t[:, gate:gate + 1], xs,
                                                             ALU.mult, ALU.add)
                    ins.then_inc(emptied["dve"], 1)
                return each

            def out_group(a, p):
                dve.wait_ge(a.summed, (p + 1) * a.pvgroup)
                s = p * a.pvgroup
                b, h = s // a.nh, s % a.nh
                if a is att_self:
                    n = link(nc.vector.tensor_mul(qT[:, h // 4, bcols(b)], pv_bank[:, 0:S], vm[:, b, :]))
                    dve.wait_ge(chain, n)
                    nc.vector.tensor_sub(kT[:, h // 4, bcols(b)], pv_bank[:, 0:S], qT[:, h // 4, bcols(b)])\
                        .then_inc(a.out, 1)
                elif a is att_c0:
                    nc.vector.tensor_copy(qc[:, h // 8, bcols(b)], pv_bank[:, 0:S]).then_inc(a.out, 1)
                elif a is att_2:
                    nc.vector.tensor_copy(pc[:, :, bcols(b)], pv_bank[:, 0:KC * S].rearrange("p (e s) -> p e s", e=KC))\
                        .then_inc(a.out, 1)
                else:
                    nc.vector.tensor_copy(q1[:, h // 2, bcols(b)], pv_bank[:, 0:S]).then_inc(a.out, 1)

            def attention(a):
                for s in range(a.steps + a.pvlag):
                    r = s - 1
                    if 0 <= r < a.steps:
                        dve.wait_ge(a.exped, r + 1)
                        nc.vector.reciprocal(rinv[:, r % NPROB:r % NPROB + 1], rsum[:, r % NPROB:r % NPROB + 1])\
                            .then_inc(a.recip, 1)
                    if s < a.steps:
                        b, h = s // a.nh, s % a.nh
                        col = nmin[:, s % NPROB:s % NPROB + 1]
                        dve.wait_ge(a.scored, s + 1)
                        if a.mask:
                            if a.mask == "keys" and h == 0:
                                dve.wait_ge(a.masked, b + 1)
                            if s >= 2:
                                dve.wait_ge(a.exped, s - 1)
                            m = causal if a.mask == "causal" else maskf[:, b % 2, :]
                            nc.vector.tensor_tensor_reduce(out=masked_s[s % 2][:, 0:a.nk], in0=s_bank(s)[:, 0:a.nk],
                                                           in1=m, scale=1.0, scalar=BIG, op0=ALU.add, op1=ALU.min,
                                                           accum_out=col).then_inc(a.maxed, 1)
                        else:
                            nc.vector.tensor_reduce(col, s_bank(s)[:, 0:a.nk], AX_X, ALU.min).then_inc(a.maxed, 1)
                    if 0 <= r < a.steps:
                        dve.wait_ge(a.recip, r + 1)
                        pr = probs[r % NPROB][:, 0:a.nk]
                        nc.vector.tensor_scalar(pr, pr, rinv[:, r % NPROB:r % NPROB + 1], None, ALU.mult)\
                            .then_inc(a.scaled, 1)
                    w = s - a.pvlag
                    if w >= 0 and w % a.pvgroup == a.pvgroup - 1:
                        out_group(a, w // a.pvgroup)

            for i in range(2):
                nc.vector.memset(vc[i].rearrange("p a b c -> p (a b c)"), 0.0).then_inc(vzero, 1)
            nc.vector.memset(eps[:, 0:1], 1e-6).then_inc(eps_done, 1)
            nc.vector.memset(eps[:, 1:2], 1e-5).then_inc(eps_done, 1)
            tti = xbf[:, 0:T].bitcast(I32).rearrange("p (b s) -> p b s", b=B)
            one = xbf[:, T:2 * T].rearrange("p (b s) -> p b s", b=B)
            dve.wait_ge(tt_in, 16)
            n1 = link(nc.vector.tensor_scalar(one, tti, 1.0, None, ALU.is_equal))
            link(nc.vector.memset(vm[:, :, :], 0.0))
            dve.wait_ge(chain, links[0])
            link(nc.vector.tensor_mul(vm[:, :, 0:S - 1], one[:, :, 0:S - 1], one[:, :, 1:S]))
            posf = scr[0:S, 1, 0:S]
            wrap = scr[0:S, 2, 0:S]
            dve.wait_ge(pos_in, 16)
            dve.wait_ge(cst_in, 16)
            dve.wait_ge(chain, link(nc.vector.tensor_copy(posf, scr[0:S, 3, 0:S].bitcast(I32))))
            dve.wait_ge(chain, link(nc.vector.tensor_scalar(wrap, posf, 0.0, float(S), ALU.is_lt, ALU.mult)))
            dve.wait_ge(chain, link(nc.vector.tensor_add(posf, posf, wrap)))
            dve.wait_ge(chain, link(nc.vector.tensor_scalar(wrap, posf, 0.0, float(S - 1), ALU.max, ALU.min)))
            nc.vector.tensor_scalar(scr[0:S, 0, 0:S], wrap, cst[0:S, C_POS:C_POS + 1], None, ALU.is_equal)\
                .then_inc(onehot_done, 1)
            dve.wait_ge(vec_in, 16)

            def rope(i):
                _, half, m = RAW[i]
                n, who, count = plan.tiles[("rot", i)]
                given[0] += 1
                assert count == given[0]
                if i == 0:
                    tile_done(dve, ("table", 1))
                tile_done(dve, RAW[i])
                raw = scr[:, i % 2, :].rearrange("p (b s) -> p b s", b=BPH)
                t = scr[:, 2 + i % 2, :].rearrange("p (b s) -> p b s", b=BPH)
                cos = cosT[:, :].unsqueeze(1).broadcast_to([P, BPH, S])
                sin = sinT[:, :].unsqueeze(1).broadcast_to([P, BPH, S])
                dst = (qT if m < KD else kT)[:, m % KD, hcols(half)].rearrange("p (b s) -> p b s", b=BPH)
                link(nc.vector.tensor_mul(t, raw, cos))
                dve.wait_ge(tile_ready, n + 1)
                bank = pool_bank(n)[:, 0:HALF].rearrange("p (b s) -> p b s", b=BPH)
                nc.vector.tensor_mul(dst, bank, sin).then_inc(emptied["dve"], 1)
                dve.wait_ge(chain, links[0])
                dve.wait_ge(emptied["dve"], count)
                nc.vector.tensor_add(dst, dst, t).then_inc(rope_done, 1)

            done = [0]

            def qk(half, m):
                if done[0] >= 1:
                    rope(done[0] - 1)
                done[0] += 1

            stage("qk", qk)
            rope(done[0] - 1)
            attention(att_self)
            stage("dense", residual("dense"))
            stage("cq", None)
            attention(att_c0)
            stage("cdense", residual("cdense"))
            ng = [0]
            for gu, down in (("v_gu", "v_down"), ("l_gu", "l_down")):
                def up(half, m, gu=gu):
                    i = ng[0]
                    ng[0] += 1
                    bank = empty((gu, half, m, 1))
                    tile_done(dve, (gu, half, m, 0))
                    nc.vector.tensor_mul(hid0[:, m, hcols(half)], bank[:, 0:HALF], scr[:, i % 2, :])\
                        .then_inc(emptied["dve"], 1)

                stage(gu, up)
                stage(down, residual(down))
            dve.wait_ge(gate_done, 1)
            for L, a in ((1, att_1), (3, att_3)):
                stage(f"Wq{L}", None)
                attention(a)
                stage(f"Wo{L}", residual(f"Wo{L}", L - 1))
                stage(f"W1{L}", None)
                stage(f"W2{L}", residual(f"W2{L}", L))
                if L == 1:
                    stage("mem", None)
                    attention(att_2)
                    stage("memT", None)

                    def fuse(half, m):
                        i = half * KD + m
                        cols = hcols(half)
                        tile_done(dve, ("gate", half, m))
                        t = scr[:, 2 + i % 2, :]
                        dve.wait_ge(chain, link(nc.vector.tensor_mul(t, scr[:, i % 2, :], mc[:, m, cols])))
                        nc.vector.tensor_add(xb[:, m, cols], t, x[:, m, cols]).then_inc(fused_done, 1)

                    stage("gate", fuse)

        @block.gpsimd
        def _(pool):
            pool.dma_start(cst[:, :], consts).then_inc(cst_in, 16)
            pool.dma_start(vec[:, :, :], vecs).then_inc(vec_in, 16)
            pool.dma_start(xbf[:, 0:T].bitcast(I32), tt.partition_broadcast(P)).then_inc(tt_in, 16)
            pool.dma_start(scr[0:S, 3, 0:S].bitcast(I32), pos.partition_broadcast(S)).then_inc(pos_in, 16)
            pool.dma_start(gate_in[:, :], gates.partition_broadcast(P)).then_inc(gate_in_s, 16)

            def last_reader(a, b):
                if a is att_2:
                    pool.wait_ge(a.scored, b + 1)
                else:
                    pool.wait_ge(tile_ready, plan.tiles[(a.name, b, len(a.units) - 1)][0] + 1)

            prev = None
            for a, kin, src in ((att_c0, 0, kvw0), (att_1, 1, kvw1), (att_2, None, None), (att_3, 2, kvw3)):
                if kin is not None:
                    if prev is not None:
                        last_reader(att_1 if a is att_3 else prev, B - 1)
                    pool.dma_start(kvw[:, 0:src.shape[1]], src).then_inc(kvw_in[kin], 16)
                for b in range(B):
                    if b >= 2:
                        last_reader(a, b - 2)
                    elif prev is not None:
                        last_reader(prev, B - 2 + b)
                    pool.dma_start(ctxb[:, b % 2], ctxF[b]).then_inc(a.ctx_in[b % 2], 16)
                    for kb in ([b - 1] if b else []) + ([b] if b == B - 1 else []) if a is att_2 else []:
                        if kb < 2:
                            pool.wait_ge(tile_ready, plan.tiles[("W21", 1, KD - 1)][0] + 1)
                        else:
                            pool.wait_ge(a.summed, kb - 1)
                        pool.dma_start(ctxt[kb % 2], ctxK[kb]).then_inc(a.mask_in[kb % 2], 16)
                    if a.mask == "keys":
                        if b >= 2:
                            pool.wait_ge(a.masked, b - 1)
                        elif a is att_3:
                            pool.wait_ge(att_1.masked, B)
                        pool.dma_start(mask8[:, b % 2, :], kmask[b].partition_broadcast(S))\
                            .then_inc(a.mask_in[b % 2], 16)
                        pool.wait_ge(a.mask_in[b % 2], 16 * (b // 2 + 1))
                        if b >= 2:
                            pool.wait_ge(a.maxed, a.nh * (b - 1))
                        elif a is att_3:
                            pool.wait_ge(att_1.maxed, att_1.steps)
                        nc.gpsimd.tensor_scalar(maskf[:, b % 2, :], mask8[:, b % 2, :], -BIG, BIG,
                                                ALU.mult, ALU.add).then_inc(a.masked, 1)
                prev = a

        @block.sync
        def _(sp):
            for n in range(NCHUNKS):
                if n >= RING:
                    sp.wait_ge(tile_ready, chunk_last[n - RING])
                sp.dma_start(ring[:, n % RING, :], walls[n]).then_inc(w_in[n % RING], 16)
            for half in range(2):
                tile_done(sp, ("W23", half, KD - 1))
                sp.dma_start(outT[:, :, hcols(half)], x[:, :, hcols(half)]).then_inc(out_done, 16)
            sp.wait_ge(out_done, 32)


def kernel(**inputs):
    import numpy as np
    import concourse.bacc as bacc
    from concourse.bass_utils import run_bass_kernel_spmd

    def get(name):
        return np.asarray(inputs[name])

    def blocks(w, m):
        k_tiles = -(-w.shape[0] // P)
        out = np.zeros((k_tiles, P, P), w.dtype)
        part = w[:, m * P:(m + 1) * P]
        for k in range(k_tiles):
            rows = part[k * P:(k + 1) * P]
            out[k, :rows.shape[0], :rows.shape[1]] = rows
        return list(out)

    def v(name):
        return get(name)

    walls = np.zeros((NCHUNKS, P, SLOT), np.float32)

    def put(name, c, blist):
        for i, blk in enumerate(blist):
            walls[CHUNK0[name] + c][:, i * P:(i + 1) * P] = blk

    def put_tiles(name, ms, mpc, weights):
        for m in range(ms):
            if m % mpc == 0:
                acc = []
            for w in weights:
                acc += blocks(w, m)
            if m % mpc == mpc - 1 or m == ms - 1:
                put(name, m // mpc, acc)

    vq, lq = v("L0_xattn_v_qkv"), v("L0_xattn_l_qkv")
    put_tiles("qk", 8, 2, [vq, lq])
    for e, w in enumerate((vq, lq)):
        walls[CHUNK0["v"] + e] = w[:, 2 * D:].reshape(KD, P, D).transpose(1, 0, 2).reshape(P, KD * D)
    put_tiles("dense", 4, 2, [v("L0_xattn_v_dense"), v("L0_xattn_l_dense")])
    put_tiles("cq", 2, 2, [v("L0_xattn_cq_w")])
    put_tiles("cdense", 4, 4, [v("L0_xattn_cdense_w")])
    for e in "vl":
        put_tiles(e + "_gu", ITILES, 2, [v(f"L0_xattn_{e}_gate"), v(f"L0_xattn_{e}_up")])
        put_tiles(e + "_down", 4, 1, [v(f"L0_xattn_{e}_down")])
    for L in "13":
        put_tiles("Wq" + L, 8, 4, [v(f"L{L}_xattn_Wq")])
        put_tiles("Wo" + L, 4, 2, [v(f"L{L}_xattn_Wo")])
        put_tiles("W1" + L, 16, 4, [v(f"L{L}_xattn_W1")])
        put_tiles("W2" + L, 4, 1, [v(f"L{L}_xattn_W2")])
    put_tiles("mem", 2, 2, [v("L2_xattn_W_mem")])
    put_tiles("memT", 4, 4, [v("L2_xattn_W_mem").T])
    put_tiles("gate", 4, 2, [v("L2_xattn_W_gate").T])

    def rows_first(w):
        k = w.shape[0] // P
        return np.ascontiguousarray(w.reshape(k, P, w.shape[1]).transpose(1, 0, 2).reshape(P, -1))

    c = np.zeros((P, C_END), np.float32)
    c[:, C_ID:C_ID + P] = np.eye(P)
    c[:, C_MEAN:C_MEAN + P] = 1.0 / D
    for m in range(P):
        if m % 32 < 16:
            c[m + 16, C_ROT + m] = -1.0
        else:
            c[m - 16, C_ROT + m] = 1.0
    inv = (1.0 / np.float32(10000.0) ** (np.arange(0, 32, 2, dtype=np.float32) / np.float32(32))).astype(np.float32)
    freqs = np.outer(np.arange(S, dtype=np.float32), inv).astype(np.float32)
    emb = np.tile(freqs, (1, P // 16))
    c[0:S, C_COS:C_COS + P] = np.cos(emb)
    c[0:S, C_SIN:C_SIN + P] = np.sin(emb)
    q, k = np.arange(S)[:, None], np.arange(S)[None, :]
    c[0:S, C_CAUSAL:C_CAUSAL + S] = np.where(k > q, np.float32(BIG), np.float32(0))
    c[:, C_POS] = np.arange(P)
    c[:, C_EVEN] = np.arange(P) // 16 % 2 == 0
    c[:, C_ODD] = np.arange(P) // 16 % 2 == 1

    ctx = get("ctx_1024")
    arrays = {
        "xT": np.ascontiguousarray(get("x").reshape(T, KD, P).transpose(2, 1, 0)),
        "ctxF": np.ascontiguousarray(ctx.reshape(B, S2, KC, P).transpose(0, 3, 2, 1)),
        "ctxK": np.ascontiguousarray(ctx.reshape(B, CH, KEYS, CC).transpose(0, 2, 1, 3)),
        "kmask": get("mask_BxS2_bk0").reshape(B, S2),
        "tt": get("mask_BxS_ik0").reshape(T),
        "pos": get("pos_1xS").reshape(S),
        "walls": walls,
        "kvw0": rows_first(get("L0_xattn_ckv_w")),
        "kvw1": rows_first(get("L1_xattn_Wkv")),
        "kvw3": rows_first(get("L3_xattn_Wkv")),
        "vecs": np.ascontiguousarray(np.stack([get(n).reshape(KD, P) for n in VECS]).transpose(2, 0, 1)),
        "gates": np.concatenate([get("L1_xattn_attn_gate"), get("L1_xattn_ff_gate"),
                                 get("L3_xattn_attn_gate"), get("L3_xattn_ff_gate")]),
        "consts": c,
    }
    nc = bacc.Bacc("TRN2", target_bir_lowering=False, num_devices=1)
    args = [nc.dram_tensor(f"in_{n}", a.shape, mybir.dt.from_np(a.dtype), kind="ExternalInput").ap()
            for n, a in arrays.items()]
    out = nc.dram_tensor("outT", [P, KD, T], F32, kind="ExternalOutput").ap()
    build(nc, *args, out)
    r = run_bass_kernel_spmd(nc, [{f"in_{n}": a for n, a in arrays.items()}], core_ids=[0])
    got = r.results[0]["outT"]
    return np.ascontiguousarray(np.asarray(got).transpose(2, 1, 0)).reshape(B, S, D)
```

```python
from contextlib import ExitStack

import concourse.bass as bass
from concourse import mybir

F32 = mybir.dt.float32
F32R = mybir.dt.float32r
U8 = mybir.dt.uint8
I32 = mybir.dt.int32
ALU = mybir.AluOpType
ACT = mybir.ActivationFunctionType
AX_X = mybir.AxisListType.X

P = 128
B, S, D = 8, 112, 512
T = B * S
HALF = T // 2
BPH = B // 2
KD = D // P
S2, CC, KEYS = 375, 256, 125
KC = CC // P
CH = S2 // KEYS
NH = 16
ITILES = 11
INNER = 1024
FF = 2048
BLOCKS = 8
SLOT = BLOCKS * P
RAW_RING = 3
RING = 5
BIG = 3.4028234663852886e38
LAG = 2
NPROB = 4
POOL = 3

STORED = [("qk", 8), ("v", 4), ("dense", 4), ("cq", 1), ("cdense", 1), ("gu", 22), ("down", 11),
          ("Wq1", 4), ("Wo1", 4), ("ff1", 16), ("mem", 1), ("memT", 1), ("gate", 4),
          ("Wq3", 4), ("Wo3", 4), ("ff3", 16)]
STORED0 = {}
N_STORED = 0
for _name, _n in STORED:
    STORED0[_name] = N_STORED
    N_STORED += _n
PLAIN = {"mem", "memT", "gate"}

ETILES = 2 * ITILES


def mlp_chunks():
    out = []
    for i in range(ETILES):
        out.append(("gu", i))
        if i % 2:
            out.append(("down", i // 2))
    return out


USES = []
for _name, _n in STORED:
    if _name == "gu":
        for _half in range(2):
            USES += [(_half, n, c) for n, c in mlp_chunks()]
    elif _name == "down":
        pass
    elif _name in ("ff1", "ff3", "gate"):
        USES += [(_half, _name, c) for _half in range(2) for c in range(_n)]
    else:
        USES += [(0, _name, c) for c in range(_n)]
USE_NO = {u: n for n, u in enumerate(USES)}
SPLIT_USES = [u for u in USES if u[1] not in PLAIN]
SPLIT_NO = {u: n for n, u in enumerate(SPLIT_USES)}

VECS = ["L0_xattn_ln_in_w", "L0_xattn_ln_post_cross_w", "L0_xattn_ln_post_attn_w",
        "L1_xattn_ln_q_g", "L1_xattn_ln_q_b", "L1_xattn_ln_ff_g", "L1_xattn_ln_ff_b",
        "L2_xattn_norm_w", "L2_xattn_b_gate",
        "L3_xattn_ln_q_g", "L3_xattn_ln_q_b", "L3_xattn_ln_ff_g", "L3_xattn_ln_ff_b"]

C_ID, C_MEAN, C_ROT, C_COS, C_SIN, C_CAUSAL, C_POS, C_EVEN, C_ODD, C_END = (
    0, 128, 256, 384, 512, 640, 752, 753, 754, 755)

NORMS = [("rms", "L0_xattn_ln_in_w", None, 1e-6), ("rms", "L0_xattn_ln_post_cross_w", None, 1e-6),
         ("rms", "L0_xattn_ln_post_attn_w", None, 1e-6),
         ("ln", "L1_xattn_ln_q_g", "L1_xattn_ln_q_b", 1e-5), ("ln", "L1_xattn_ln_ff_g", "L1_xattn_ln_ff_b", 1e-5),
         ("rms", "L2_xattn_norm_w", None, 1e-6),
         ("ln", "L3_xattn_ln_q_g", "L3_xattn_ln_q_b", 1e-5), ("ln", "L3_xattn_ln_ff_g", "L3_xattn_ln_ff_b", 1e-5)]

class PoolPlan:

    def __init__(self):
        self.n = 0
        self.count = {"act": 0, "dve": 0}
        self.tiles = {}
        self.order = []

    def add(self, key, who):
        self.count[who] += 1
        self.tiles[key] = (self.n, who, self.count[who])
        self.order.append((who, self.count[who]))
        self.n += 1
        return self.n - 1


class Attention:

    def __init__(self, name, nh, nk, group, pvgroup, mask, units, sem):
        self.name, self.nh, self.nk, self.group, self.pvgroup, self.mask = name, nh, nk, group, pvgroup, mask
        self.chunks = 1 if nk <= P else CH
        self.kw = nk // self.chunks
        self.steps = B * nh
        self.unit_heads = units
        self.pvlag = LAG + group
        self.scored = sem(name + "_scored")
        self.maxed = sem(name + "_maxed")
        self.exped = sem(name + "_exped")
        self.recip = sem(name + "_recip")
        self.scaled = sem(name + "_scaled")
        self.turned = sem(name + "_turned")
        self.probs_out = sem(name + "_probs_out")
        self.summed = sem(name + "_summed")
        self.out = sem(name + "_out")
        self.ctx_in = [sem(f"{name}_ctx_in{i}") for i in range(2)]
        self.mask_in = [sem(f"{name}_mask_in{i}") for i in range(2)]
        self.masked = sem(name + "_masked")


def build(nc, xT, ctxF, ctxK, kmask, tt, ttT, pos, walls, kvw0, kvw1, kvw3, vecs, gates, consts, outT):
    ctx = ExitStack()
    with ctx:
        place = [16512]

        def at(name, shape, dt, offset):
            return nc.alloc_sbuf_tensor_at(name, shape, dt, offset=offset)

        def sb(name, shape, dt=F32):
            size = 1 if dt == U8 else 4
            for d in shape[1:]:
                size *= d
            offset = place[0]
            place[0] += -(-size // 32) * 32
            return at(name, shape, dt, offset)

        def sem(name):
            return ctx.enter_context(nc.semaphore(name))

        raw = sb("raw", [P, RAW_RING, SLOT])
        wh = sb("wh", [P, RING, SLOT], F32R)
        wl = sb("wl", [P, RING, SLOT], F32R)
        kvw = sb("kvw", [P, 2 * FF])
        x = sb("x", [P, KD, T])
        o_f = place[0]
        nh_ = sb("nh", [P, KD, T], F32R)
        nl_ = sb("nl", [P, KD, T], F32R)
        ol8 = at("ol8", [P, INNER // P, T], F32R, o_f)
        fused = at("fused", [P, KD, T], F32, o_f)
        o_q = place[0]
        q1 = sb("q1", [P, INNER // P, T])
        qT = at("qT", [P, KD, T], F32, o_q)
        kT = at("kT", [P, KD, T], F32, o_q + 4 * KD * T)
        qc = at("qc", [P, KC, T], F32, o_q)
        oh8 = at("oh8", [P, INNER // P, T], F32R, o_q)
        hw = at("hw", [P, KC, T], F32, o_q)
        pc = at("pc", [P, KC, T], F32, o_q + 4 * KC * T)
        mc = at("mc", [P, KD, T], F32, o_q + 8 * KC * T)
        o_k = place[0]
        k1 = sb("k1", [P, 4, 376])
        v1 = sb("v1", [P, 4, CH, P])
        kc = at("kc", [P, 2, 2, 376], F32, o_k)
        vc = at("vc", [P, 2, CH, 2, P], F32, o_k + 4 * 4 * 376)
        ctxt = at("ctxt", [P, 4, CH * CC], F32, o_k)
        place[0] = max(place[0], o_k + 4 * 4 * CH * CC)
        ctxb = sb("ctxb", [P, 2, KC, S2])
        mask8 = sb("mask8", [S, 2, S2], U8)
        maskf = sb("maskf", [S, 2, S2])
        vm = sb("vm", [P, B, S])
        vml = sb("vml", [P, B, S])
        vmT = sb("vmT", [S, 2, B])
        scr = sb("scr", [P, 4, HALF])
        xc = sb("xc", [P, KD, HALF])
        sq = sb("sq", [P, 2, HALF])
        std = sb("std", [P, HALF])
        rstd = sb("rstd", [P, HALF])
        cst = sb("cst", [P, C_END])
        vec = sb("vec", [P, len(VECS), KD])
        cosT = sb("cosT", [P, S])
        sinT = sb("sinT", [P, S])
        gate_in = sb("gate_in", [P, 4])
        gate_t = sb("gate_t", [P, 4])
        nmin = sb("nmin", [S, NPROB])
        rsum = sb("rsum", [S, NPROB])
        rinv = sb("rinv", [S, NPROB])
        eps = sb("eps", [P, 2])
        o_a = place[0]
        masked_t = sb("masked_t", [S, 2, S2])
        probs_t = sb("probs_t", [S, NPROB, S2])
        probsT_t = sb("probsT_t", [P, 2, 4 * S])
        hid_h = at("hid_h", [P, 2, HALF], F32R, o_a)
        hid_l = at("hid_l", [P, 2, HALF], F32R, o_a + 8 * HALF)
        vtmp = at("vtmp", [S, 2, D], F32, o_a)
        assert place[0] <= 224 * 1024 - 2048, place[0]
        vS = kvw[0:S, :].rearrange("p (b d) -> p b d", b=B)
        masked_s = [masked_t[:, i, :] for i in range(2)]
        probs = [probs_t[:, i, :] for i in range(NPROB)]
        probsT = [probsT_t[:, i, :] for i in range(2)]

        psum = ctx.enter_context(nc.psum_tensor("psum", [P, 8, 512], F32))

        def pool_bank(n):
            return psum[:, n % POOL, :]

        def s_bank(s):
            return psum[0:S, 3 + s % 2, :]

        def t_bank(g):
            return psum[:, 5 + g % 2, :]

        pv_bank = psum[:, 7, :]

        ident = cst[:, C_ID:C_ID + P]
        mean_w = cst[:, C_MEAN:C_MEAN + P]
        rot_w = cst[:, C_ROT:C_ROT + P]
        causal = cst[0:S, C_CAUSAL:C_CAUSAL + S]

        raw_in = [sem(f"raw_in{i}") for i in range(RAW_RING)]
        split_h = sem("split_h")
        split_l = sem("split_l")
        acc_step = sem("acc_step")
        acc_used = sem("acc_used")
        hid_done = sem("hid_done")
        hid_high = sem("hid_high")
        hid_low = sem("hid_low")
        nraw = sem("nraw")
        nhigh = sem("nhigh")
        raw_qk = sem("raw_qk")
        tile_ready = sem("tile_ready")
        emptied = {"act": sem("emptied_act"), "dve": sem("emptied_dve")}
        x_in = sem("x_in")
        cst_in = sem("cst_in")
        vec_in = sem("vec_in")
        tt_in = sem("tt_in")
        ttT_in = sem("ttT_in")
        vmT_done = sem("vmT_done")
        pos_in = sem("pos_in")
        gate_in_s = sem("gate_in_s")
        gate_done = sem("gate_done")
        kvw_in = [sem(f"kvw_in{i}") for i in range(3)]
        eps_done = sem("eps_done")
        onehot_done = sem("onehot_done")
        rope_done = sem("rope_done")
        fused_done = sem("fused_done")
        vzero = sem("vzero")
        chain = sem("chain")
        out_done = sem("out_done")
        ctxt_in = [sem(f"ctxt_in{i}") for i in range(4)]
        sq_ready = sem("sq_ready")
        sq_used = sem("sq_used")
        std_used = sem("std_used")
        normed = sem("normed")
        centred = sem("centred")

        att_self = Attention("self", NH, S, 4, 4, "causal", 0, sem)
        att_c0 = Attention("cross0", NH, S2, 1, 8, None, 8, sem)
        att_1 = Attention("cross1", NH, S2, 1, 2, "keys", 2, sem)
        att_2 = Attention("memory", 1, S2, 1, 1, None, 0, sem)
        att_3 = Attention("cross3", NH, S2, 1, 2, "keys", 2, sem)

        plan = PoolPlan()
        chunk_last = {}

        order = [(nn, half) for nn in range(5) for half in range(2)] + [
            (5, 0), (6, 0), (5, 1), (6, 1), (7, 0), (7, 1)]
        turn_of = {key: i for i, key in enumerate(order)}
        ln_turn = {key: i for i, key in enumerate([o for o in order if NORMS[o[0]][0] == "ln"])}

        split_turn = {key: i for i, key in enumerate([o for o in order if o[0] != 5])}

        def norm_done(eng, nn, half):
            eng.wait_ge(normed, turn_of[nn, half] + 1)

        def tile_done(eng, key):
            _, who, count = plan.tiles[key]
            eng.wait_ge(emptied[who], count)

        def hcols(half):
            return slice(half * HALF, (half + 1) * HALF)

        def bcols(b):
            return slice(b * S, (b + 1) * S)

        def by_half(ms, mpc, hooks):
            seq = []
            for half in range(2):
                for m in range(ms):
                    seq.append(("tile", half, m, m // mpc))
                    seq += hooks.get((half, m), [])
            return seq

        def qk_order(hooks):
            seq = []
            for group in range(2):
                for half in range(2):
                    for m in range(4 * group, 4 * group + 4):
                        seq.append(("tile", half, m, m))
                        seq += hooks.get((group, half, m), [])
            return seq

        def parts(nn, half, **at_):
            return {key: [("norm", nn, half, p)] for p, key in at_.items()}

        def both(*hooks):
            out = {}
            for h in hooks:
                for key, v in h.items():
                    out[key] = out.get(key, []) + v
            return out

        SEQ = {
            "qk": [("norm", 0, 0, "v"), ("norm", 0, 0, "f")] + qk_order(parts(0, 1, v=(0, 0, 0), f=(0, 0, 1))),
            "dense": by_half(4, 1, parts(1, 0, v=(1, 0), f=(1, 1))),
            "cq": by_half(2, 2, parts(1, 1, v=(0, 0), f=(0, 1))),
            "cdense": by_half(4, 4, parts(2, 0, v=(1, 1), f=(1, 3))),
            "mlp": by_half(ETILES, 1, both(parts(2, 1, v=(0, 0), f=(0, 1)),
                                           parts(3, 0, m=(1, 1), v=(1, 2), f=(1, 4)))),
            "Wq1": by_half(8, 2, parts(3, 1, m=(0, 0), v=(0, 2), f=(0, 4))),
            "Wo1": by_half(4, 1, parts(4, 0, m=(1, 0), v=(1, 1), f=(1, 2))),
            "ff1": by_half(16, 1, parts(4, 1, m=(0, 1), v=(0, 2), f=(0, 4))),
            "mem": by_half(2, 2, {}),
            "memT": by_half(4, 4, {}),
            "gate": by_half(4, 1, both(parts(5, 0, v=(1, 0), f=(1, 1)), parts(6, 0, m=(1, 2), v=(1, 3)))) +
            [("norm", 6, 0, "f")],
            "Wq3": by_half(8, 2, both(parts(5, 1, v=(0, 0), f=(0, 1)), parts(6, 1, m=(0, 2), v=(0, 3), f=(0, 5)))),
            "Wo3": by_half(4, 1, parts(7, 0, m=(1, 0), v=(1, 1), f=(1, 2))),
            "ff3": by_half(16, 1, parts(7, 1, m=(0, 1), v=(0, 2), f=(0, 4))),
        }
        MLPS = ["mlp", "ff1", "ff3"]
        HIDDEN = {"mlp": ETILES, "ff1": 16, "ff3": 16}
        hid0 = {"mlp": 0, "ff1": 2 * ETILES, "ff3": 2 * ETILES + 32}

        def hid_no(name, half, m):
            return hid0[name] + half * HIDDEN[name] + m

        def mlp_out(name, half):
            return (MLPS.index(name) * 2 + half) * KD

        X_OF_NORM = {1: "dense", 2: "cdense", 3: "mlp", 4: "Wo1", 7: "Wo3"}

        def x_ready(eng, nn, half, k):
            if nn == 0:
                eng.wait_ge(x_in, 16)
            elif nn == 5:
                eng.wait_ge(fused_done, half * KD + k + 1)
            elif nn == 6:
                eng.wait_ge(normed, turn_of[5, half] + 1)
            elif nn == 3:
                eng.wait_ge(acc_used, mlp_out("mlp", half) + k + 1)
            elif nn == 1:
                tile_done(eng, ("dense", half, k, 1))
            else:
                tile_done(eng, (X_OF_NORM[nn], half, k))

        def norm_src(nn):
            return fused if nn == 5 else x

        RAW = [("qk",) + it[1:3] for it in SEQ["qk"] if it[0] == "tile"]

        def unit_parts(a, s):
            if not a.unit_heads or s // a.unit_heads + 1 >= B * NH // a.unit_heads:
                return []
            h = s % a.unit_heads
            if a.unit_heads == 2:
                return [h]
            return {1: [0], 4: [1]}.get(h, [])

        block = ctx.enter_context(nc.Block())

        @block.tensor
        def _(pe):
            def begin_tile(key, who):
                n = plan.add(key, who)
                if n >= POOL:
                    w, count = plan.order[n - POOL]
                    pe.wait_ge(emptied[w], count)
                return n

            def product(out, pairs):
                for i, (lhsT, rhs) in enumerate(pairs):
                    last = nc.tensor.matmul(out, lhsT, rhs, start=(i == 0), stop=(i == len(pairs) - 1))
                return last

            def product3(out, quads):
                n = len(quads)
                for i, (ah, al, bh, bl) in enumerate(quads):
                    nc.tensor.matmul(out, ah, bh, start=(i == 0), stop=False)
                    nc.tensor.matmul(out, ah, bl, start=False, stop=False)
                    last = nc.tensor.matmul(out, al, bh, start=False, stop=(i == n - 1))
                return last

            def chunk(name, c, use=0):
                u = (use, name, c)
                if name in PLAIN:
                    n = USE_NO[u]
                    pe.wait_ge(raw_in[n % RAW_RING], 16 * (n // RAW_RING + 1))
                    return raw[:, n % RAW_RING, :]
                n = SPLIT_NO[u]
                pe.wait_ge(split_l, n + 1)
                return wh[:, n % RING, :], wl[:, n % RING, :]

            def norm_part(nn, half, part):
                kind = NORMS[nn][0]
                if part == "m":
                    n = begin_tile(("mean", nn, half), "dve")
                    for k in range(KD):
                        x_ready(pe, nn, half, k)
                        last = nc.tensor.matmul(pool_bank(n)[:, 0:HALF], mean_w, x[:, k, hcols(half)],
                                                start=(k == 0), stop=(k == KD - 1))
                    last.then_inc(tile_ready, 1)
                elif part == "v":
                    n = begin_tile(("var", nn, half), "act")
                    for k in range(KD):
                        i = turn_of[nn, half] * KD + k
                        pe.wait_ge(sq_ready, i + 1)
                        last = nc.tensor.matmul(pool_bank(n)[:, 0:HALF], mean_w, sq[:, i % 2, :],
                                                start=(k == 0), stop=(k == KD - 1))
                        if k < KD - 1:
                            last.then_inc(sq_used, 1)
                    last.then_inc(tile_ready, 1)

            def stage(name, rhs_of, nblocks, who, mpc, ready=None):
                seq = SEQ[name]
                key = (lambda it: (it[1], it[3])) if name == "gate" else (lambda it: (0, it[3]))
                last_use = {key(it): j for j, it in enumerate(seq) if it[0] == "tile"}
                for j, it in enumerate(seq):
                    if it[0] == "norm":
                        norm_part(*it[1:])
                        continue
                    _, half, m, c = it
                    use, _c = key(it)
                    w = chunk(name, c, use)
                    if ready:
                        ready(half, m)
                    for e in range(len(who)):
                        n = begin_tile((name, half, m, e) if len(who) > 1 else (name, half, m), who[e])
                        out = pool_bank(n)[:, 0:HALF]
                        base = ((m % mpc) * len(who) + e) * nblocks
                        blk = [slice((base + i) * P, (base + i + 1) * P) for i in range(nblocks)]
                        if name in PLAIN:
                            last = product(out, [(w[:, blk[i]], rhs_of(half, i)) for i in range(nblocks)])
                        else:
                            last = product3(out, [(w[0][:, blk[i]], w[1][:, blk[i]], *rhs_of(half, i))
                                                  for i in range(nblocks)])
                        last.then_inc(tile_ready, 1)
                    if name == "qk" and True:
                        yield_qk(j)
                    if last_use[key(it)] == j:
                        chunk_last[(use, name, c)] = (tile_ready, plan.n)

            qk_seen = [0]

            def yield_qk(j):
                if qk_seen[0] >= 1:
                    rotate(qk_seen[0] - 1)
                qk_seen[0] += 1

            def mlp(name, ready):
                nt = HIDDEN[name]

                def down(half, i):
                    g = hid_no(name, half, i)
                    if name == "mlp":
                        u = (half, "down", i // 2)
                        base = (i % 2) * KD
                        done_with = i % 2 == 1
                    else:
                        u = (half, name, i)
                        base = KD
                        done_with = True
                    w = chunk(u[1], u[2], u[0])
                    if i == 0 and mlp_out(name, half):
                        pe.wait_ge(acc_used, mlp_out(name, half))
                    pe.wait_ge(hid_low, g + 1)
                    ah, al = hid_h[:, g % 2, :], hid_l[:, g % 2, :]
                    for m in range(KD):
                        blk = slice((base + m) * P, (base + m + 1) * P)
                        out = psum[:, 4 + m, 0:HALF]
                        nc.tensor.matmul(out, w[0][:, blk], ah, start=(i == 0), stop=False)
                        nc.tensor.matmul(out, w[0][:, blk], al, start=False, stop=False)
                        last = nc.tensor.matmul(out, w[1][:, blk], ah, start=False, stop=(i == nt - 1))
                    last.then_inc(acc_step, 1)
                    if done_with:
                        chunk_last[u] = (acc_step, g + 1)

                items = SEQ[name]
                for j, it in enumerate(items):
                    if it[0] == "norm":
                        norm_part(*it[1:])
                        continue
                    _, half, m, _c = it
                    w = chunk("gu" if name == "mlp" else name, m, half)
                    ready(half)
                    src = [(nh_[:, k, hcols(half)], nl_[:, k, hcols(half)]) for k in range(KD)]
                    for e in range(2 if name == "mlp" else 1):
                        n = begin_tile((name, half, m, e), ("act", "dve")[e])
                        blk = [slice((e * KD + k) * P, (e * KD + k + 1) * P) for k in range(KD)]
                        product3(pool_bank(n)[:, 0:HALF], [(w[0][:, blk[k]], w[1][:, blk[k]], *src[k])
                                                           for k in range(KD)]).then_inc(tile_ready, 1)
                    if name == "mlp":
                        chunk_last[(half, "gu", m)] = (tile_ready, plan.n)
                    if m >= 1:
                        down(half, m - 1)
                    if m == nt - 1:
                        down(half, m)

            def kv_unit(a, i, part):
                per = NH // a.unit_heads
                b, g = i // per, i % per
                width = CC if a is att_c0 else INNER
                w = kvw[:, 0:KC * 2 * width].rearrange("p (k n) -> p k n", k=KC)
                pe.wait_ge(a.ctx_in[b % 2], 16 * (b // 2 + 1))
                n = begin_tile((a.name, i, part), "act")
                cb = ctxb[:, b % 2]
                if part == 0:
                    last = product(pool_bank(n)[:, 0:S2],
                                   [(w[:, k, g * P:(g + 1) * P], cb[:, k, :]) for k in range(KC)])
                else:
                    o = width + g * P
                    for c in range(CH):
                        last = product(pool_bank(n)[0:KEYS, c * P:(c + 1) * P],
                                       [(cb[:, k, c * KEYS:(c + 1) * KEYS], w[:, k, o:o + P]) for k in range(KC)])
                last.then_inc(tile_ready, 1)

            def scores(a, s):
                b, h = s // a.nh, s % a.nh
                out = s_bank(s)[:, 0:a.nk]
                if a is att_self:
                    r = slice(32 * (h % 4), 32 * (h % 4) + 32)
                    ops = [(qT[r, h // 4, bcols(b)], kT[r, h // 4, bcols(b)])]
                elif a is att_c0:
                    r = slice(32 * (h % 8 // 2), 32 * (h % 8 // 2) + 32)
                    ops = [(qc[r, h // 8, bcols(b)], kc[r, s // 8 % 2, h % 2, 0:S2])]
                elif a is att_2:
                    ops = [(hw[:, k, bcols(b)], ctxb[:, b % 2, k, :]) for k in range(KC)]
                else:
                    r = slice(64 * (h % 2), 64 * (h % 2) + 64)
                    ops = [(q1[r, h // 2, bcols(b)], k1[r, s // 2 % 4, 0:S2])]
                if h == 0:
                    if a is att_self:
                        pe.wait_ge(rope_done, 16)
                        tile_done(pe, ("vproj", B - 1, 1))
                    elif a is att_2:
                        pe.wait_ge(a.ctx_in[b % 2], 16 * (b // 2 + 1))
                        tile_done(pe, ("mem", 1, 1))
                    else:
                        tile_done(pe, ("cq", 1, 1) if a is att_c0 else ("Wq" + a.name[-1], 1, 7))
                if a.unit_heads and s % a.unit_heads == 0:
                    tile_done(pe, (a.name, s // a.unit_heads, 1))
                if s >= 2:
                    pe.wait_ge(a.maxed if a.mask else a.exped, s - 1)
                product(out, ops).then_inc(a.scored, 1)

            def turn(a, s):
                g = s // a.group
                pe.wait_ge(a.scaled, s + 1)
                if g >= 2 and s % a.group == 0:
                    pe.wait_ge(a.probs_out, g - 1)
                for c in range(a.chunks):
                    o = (s % a.group + c) * S
                    last = nc.tensor.transpose(t_bank(g)[0:a.kw, o:o + S],
                                               probs[s % NPROB][:, c * a.kw:(c + 1) * a.kw], ident[0:S, 0:S])
                last.then_inc(a.turned, 1)

            def weigh(a, s):
                b, h = s // a.nh, s % a.nh
                g = s // a.group
                pe.wait_ge(a.probs_out, g + 1)
                if s % a.pvgroup == 0 and s >= a.pvgroup:
                    pe.wait_ge(a.out, s // a.pvgroup)
                pT = probsT[g % 2]
                if a is att_self:
                    last = nc.tensor.matmul(pv_bank[32 * (h % 4):32 * (h % 4) + 32, 0:S], vS[:, b, 32 * h:32 * h + 32],
                                            pT[0:S, (h % 4) * S:(h % 4 + 1) * S], start=True, stop=True)
                elif a is att_c0:
                    j = h // 2
                    o = 32 * (j % 4)
                    for c in range(CH):
                        last = nc.tensor.matmul(pv_bank[o:o + 32, 0:S], vc[0:KEYS, s // 8 % 2, c, h % 2, o:o + 32],
                                                pT[0:KEYS, c * S:(c + 1) * S],
                                                start=(h % 2 == 0 and c == 0), stop=(h % 2 == 1 and c == CH - 1))
                elif a is att_2:
                    pe.wait_ge(ctxt_in[b % 4], 16 * (b // 4 + 1))
                    for e in range(KC):
                        last = product(pv_bank[:, e * S:(e + 1) * S],
                                       [(ctxt[0:KEYS, b % 4, c * CC + e * P:c * CC + (e + 1) * P], pT[0:KEYS, c * S:(c + 1) * S])
                                        for c in range(CH)])
                else:
                    o = 64 * (h % 2)
                    for c in range(CH):
                        last = nc.tensor.matmul(pv_bank[o:o + 64, 0:S], v1[0:KEYS, s // 2 % 4, c, o:o + 64],
                                                pT[0:KEYS, c * S:(c + 1) * S], start=(c == 0), stop=(c == CH - 1))
                last.then_inc(a.summed, 1)

            def attention(a):
                for s in range(a.steps + a.pvlag):
                    if s < a.steps:
                        scores(a, s)
                        for part in unit_parts(a, s):
                            kv_unit(a, s // a.unit_heads + 1, part)
                    if 0 <= s - LAG < a.steps:
                        turn(a, s - LAG)
                    if s >= a.pvlag:
                        weigh(a, s - a.pvlag)

            pe.wait_ge(cst_in, 16)
            pe.wait_ge(onehot_done, 1)
            for i, c in enumerate((C_COS, C_SIN)):
                n = begin_tile(("table", i), "act")
                nc.tensor.matmul(pool_bank(n)[:, 0:S], cst[0:S, c:c + P], scr[0:S, 0, 0:S],
                                 start=True, stop=True).then_inc(tile_ready, 1)

            def nhl(half, i):
                return nh_[:, i, hcols(half)], nl_[:, i, hcols(half)]

            def rotate(i):
                pe.wait_ge(raw_qk, i + 1)
                n = begin_tile(("rot", i), "dve")
                nc.tensor.matmul(pool_bank(n)[:, 0:HALF], rot_w, scr[:, i % 2, :],
                                 start=True, stop=True).then_inc(tile_ready, 1)

            stage("qk", nhl, KD, ("dve", "dve"), 1, ready=lambda half, m: norm_done(pe, 0, half))
            rotate(len(RAW) - 1)

            wv = [chunk("v", c) for c in range(4)]
            for b in range(B):
                for e in range(2):
                    n = begin_tile(("vproj", b, e), ("act", "dve")[e])
                    quads = []
                    for k in range(KD):
                        h_, l_ = wv[2 * e + k // 2]
                        cols = slice((k % 2) * D, (k % 2) * D + D)
                        quads.append((nh_[:, k, bcols(b)], nl_[:, k, bcols(b)], h_[:, cols], l_[:, cols]))
                    product3(pool_bank(n)[0:S, :], quads).then_inc(tile_ready, 1)
            for c in range(4):
                chunk_last[(0, "v", c)] = (tile_ready, plan.n)

            attention(att_self)

            stage("dense", nhl, KD, ("dve", "dve"), 1,
                  ready=lambda half, m: pe.wait_ge(att_self.out, att_self.steps // 4))
            pe.wait_ge(kvw_in[0], 16)
            for part in range(2):
                kv_unit(att_c0, 0, part)
            stage("cq", nhl, KD, ("act",), 2, ready=lambda half, m: norm_done(pe, 1, half))
            attention(att_c0)
            stage("cdense", nhl, KC, ("dve",), 4, ready=lambda half, m: pe.wait_ge(att_c0.out, att_c0.steps // 8))
            mlp("mlp", lambda half: norm_done(pe, 2, half))
            for L, a, nq, nf, kin in ((1, att_1, 3, 4, 1), (3, att_3, 6, 7, 2)):
                pe.wait_ge(kvw_in[kin], 16)
                for part in range(2):
                    kv_unit(a, 0, part)
                stage(f"Wq{L}", nhl, KD, ("act",), 2, ready=lambda half, m, nq=nq: norm_done(pe, nq, half))
                attention(a)
                stage(f"Wo{L}", lambda half, i: (oh8[:, i, hcols(half)], ol8[:, i, hcols(half)]), 8, ("dve",), 1,
                      ready=lambda half, m, a=a: pe.wait_ge(a.out, a.steps // 2))
                mlp(f"ff{L}", lambda half, nf=nf: norm_done(pe, nf, half))
                if L == 1:
                    stage("mem", lambda half, i: x[:, i, hcols(half)], KD, ("act",), 2,
                          ready=lambda half, m: pe.wait_ge(acc_used, mlp_out("ff1", half) + KD))
                    attention(att_2)
                    stage("memT", lambda half, i: pc[:, i, hcols(half)], KC, ("act",), 4,
                          ready=lambda half, m: pe.wait_ge(att_2.out, B))
                    stage("gate", lambda half, i: (x if i < KD else mc)[:, i % KD, hcols(half)], 8, ("act",), 1,
                          ready=lambda half, m: tile_done(pe, ("memT", 1, KD - 1)))

        @block.scalar
        def _(act):
            given = [0]

            def empty(key):
                n, who, count = plan.tiles[key]
                given[0] += 1
                assert who == "act" and count == given[0]
                act.wait_ge(tile_ready, n + 1)
                return pool_bank(n)

            def norm_part(nn, half, part):
                kind, wname, bname, e = NORMS[nn]
                if part == "v":
                    for k in range(KD):
                        i = turn_of[nn, half] * KD + k
                        if kind == "rms":
                            x_ready(act, nn, half, k)
                        elif k < KD - 1:
                            act.wait_ge(centred, ln_turn[nn, half] * (KD - 1) + k + 1)
                        else:
                            tile_done(act, ("mean", nn, half))
                        if i >= 2:
                            j = i - 2
                            if j % KD == KD - 1:
                                act.wait_ge(tile_ready, plan.tiles[("var",) + order[j // KD]][0] + 1)
                            else:
                                act.wait_ge(sq_used, j - j // KD + 1)
                        src = norm_src(nn)[:, k, hcols(half)] if kind == "rms" else xc[:, k, :]
                        nc.scalar.activation(sq[:, i % 2, :], src, ACT.Square).then_inc(sq_ready, 1)
                    bank = empty(("var", nn, half))
                    if turn_of[nn, half] >= 1:
                        act.wait_ge(std_used, turn_of[nn, half])
                    nc.scalar.activation(std[:, :], bank[:, 0:HALF], ACT.Sqrt,
                                         bias=eps[:, 0:1] if e == 1e-6 else eps[:, 1:2]).then_inc(emptied["act"], 1)
                elif part == "f" and nn != 5:
                    for k in range(KD):
                        act.wait_ge(nraw, split_turn[nn, half] * KD + k + 1)
                        if kind == "ln":
                            ins = nc.scalar.activation(nh_[:, k, hcols(half)], xc[:, k, :], ACT.Identity,
                                                       bias=vec[:, VECS.index(bname), k:k + 1])
                        else:
                            ins = nc.scalar.copy(nh_[:, k, hcols(half)], xc[:, k, :])
                        ins.then_inc(nhigh, 1)

            def stage(name, each):
                for it in SEQ[name]:
                    if it[0] == "norm":
                        norm_part(*it[1:])
                    elif each:
                        each(it[1], it[2])

            def context(a, b):
                act.dma_start(ctxb[:, b % 2], ctxF[b]).then_inc(a.ctx_in[b % 2], 16)
                if a.mask == "keys":
                    if b >= 2:
                        act.wait_ge(a.masked, b - 1)
                    act.dma_start(mask8[:, b % 2, :], kmask[b].partition_broadcast(S)).then_inc(a.mask_in[b % 2], 16)

            def kv_unit(a, i, part):
                per = NH // a.unit_heads
                b, g = i // per, i % per
                bank = empty((a.name, i, part))
                slots = 2 if a is att_c0 else 4
                if i >= slots:
                    act.wait_ge(a.summed if part else a.scored, a.unit_heads * (i - slots + 1))
                if a is att_c0:
                    if part == 0:
                        for par, col in ((0, C_EVEN), (1, C_ODD)):
                            last = nc.scalar.activation(kc[:, i % 2, par, 0:S2], bank[:, 0:S2], ACT.Copy,
                                                        scale=cst[:, col:col + 1])
                    else:
                        if i < 2:
                            act.wait_ge(vzero, 1)
                        for par in range(2):
                            dst = vc[0:KEYS, i % 2, :, par, :].rearrange("p c (j t d) -> p c j t d", t=2, d=16)[:, :, :, par, :]
                            srcv = bank[0:KEYS, 0:CH * P].rearrange("p (c j t d) -> p c j t d", c=CH, t=2, d=16)[:, :, :, par, :]
                            last = nc.scalar.copy(dst, srcv)
                elif part == 0:
                    last = nc.scalar.copy(k1[:, i % 4, 0:S2], bank[:, 0:S2])
                else:
                    last = nc.scalar.copy(v1[0:KEYS, i % 4].rearrange("p c n -> p (c n)"), bank[0:KEYS, 0:CH * P])
                last.then_inc(emptied["act"], 1)
                if part == 1 and g == per - 1 and b + 2 < B:
                    context(a, b + 2)

            def attention(a):
                for s in range(a.steps + LAG):
                    if s < a.steps:
                        act.wait_ge(a.maxed, s + 1)
                        if s >= NPROB:
                            act.wait_ge(a.turned, s - NPROB + 1)
                        src = masked_s[s % 2][:, 0:a.nk] if a.mask else s_bank(s)[:, 0:a.nk]
                        nc.scalar.activation(probs[s % NPROB][:, 0:a.nk], src, ACT.Exp, scale=-1.0,
                                             bias=nmin[:, s % NPROB:s % NPROB + 1],
                                             accum_out=rsum[:, s % NPROB:s % NPROB + 1]).then_inc(a.exped, 1)
                        for part in unit_parts(a, s):
                            kv_unit(a, s // a.unit_heads + 1, part)
                        if a is att_2 and s + 2 < B:
                            context(a, s + 2)
                    t = s - LAG
                    if t >= 0 and t % a.group == a.group - 1:
                        g = t // a.group
                        act.wait_ge(a.turned, t + 1)
                        if g >= 2:
                            act.wait_ge(a.summed, (g - 1) * a.group)
                        w = max(a.group, a.chunks) * S
                        nc.scalar.copy(probsT[g % 2][0:a.kw, 0:w], t_bank(g)[0:a.kw, 0:w]).then_inc(a.probs_out, 1)
                        if a is att_2 and 2 <= g and g + 2 < B:
                            key_major(g + 2)

            def key_major(b):
                act.dma_start(ctxt[0:KEYS, b % 4, :], ctxK[b]).then_inc(ctxt_in[b % 4], 16)

            act.dma_start(x[:, :, :], xT).then_inc(x_in, 16)
            act.wait_ge(eps_done, 2)
            act.wait_ge(gate_in_s, 16)
            nc.scalar.activation(gate_t[:, :], gate_in[:, :], ACT.Tanh).then_inc(gate_done, 1)
            for i, dst in enumerate((cosT, sinT)):
                bank = empty(("table", i))
                nc.scalar.copy(dst[:, :], bank[:, 0:S]).then_inc(emptied["act"], 1)

            stage("qk", None)
            act.wait_ge(vmT_done, 2)
            for b in range(B):
                bank = empty(("vproj", b, 0))
                if b >= 2:
                    tile_done(act, ("vproj", b - 2, 1))
                nc.scalar.activation(vtmp[:, b % 2, :], bank[0:S, :], ACT.Copy,
                                     scale=vmT[:, 0, b:b + 1]).then_inc(emptied["act"], 1)
            for b in range(2):
                context(att_c0, b)
            attention(att_self)
            act.wait_ge(att_self.summed, att_self.steps)
            act.dma_start(kvw[:, 0:KC * 2 * CC], kvw0).then_inc(kvw_in[0], 16)
            stage("dense", None)
            for part in range(2):
                kv_unit(att_c0, 0, part)

            def cq(half, m):
                bank = empty(("cq", half, m))
                nc.scalar.mul(qc[:, m, hcols(half)], bank[:, 0:HALF], -0.25).then_inc(emptied["act"], 1)

            stage("cq", cq)
            attention(att_c0)
            act.dma_start(kvw[:, :], kvw1).then_inc(kvw_in[1], 16)
            for b in range(2):
                context(att_1, b)
            stage("cdense", None)

            def hidden(name):
                nt = HIDDEN[name]

                def high(g, src):
                    if name == "mlp":
                        act.wait_ge(hid_done, g + 1)
                    if g >= 2:
                        act.wait_ge(acc_step, g - 1)
                    nc.scalar.copy(hid_h[:, g % 2, :], src).then_inc(hid_high, 1)

                def each(half, m):
                    g = hid_no(name, half, m)
                    bank = empty((name, half, m, 0))
                    if name == "mlp":
                        if g >= 2:
                            act.wait_ge(hid_done, g - 1)
                        nc.scalar.activation(scr[:, g % 2, :], bank[:, 0:HALF], ACT.Silu).then_inc(emptied["act"], 1)
                        if m >= 1:
                            high(g - 1, scr[:, 2 + (g - 1) % 2, :])
                        if m == nt - 1:
                            high(g, scr[:, 2 + g % 2, :])
                    else:
                        if g >= 2:
                            act.wait_ge(hid_low, g - 1)
                        nc.scalar.activation(scr[:, g % 2, :], bank[:, 0:HALF], ACT.Gelu).then_inc(emptied["act"], 1)
                        tile_done(act, (name, half, m, 0))
                        high(g, scr[:, g % 2, :])
                return each

            stage("mlp", hidden("mlp"))
            for L, a in ((1, att_1), (3, att_3)):
                for part in range(2):
                    kv_unit(a, 0, part)

                def wq(half, m, L=L):
                    bank = empty((f"Wq{L}", half, m))
                    nc.scalar.mul(q1[:, m, hcols(half)], bank[:, 0:HALF], -0.125).then_inc(emptied["act"], 1)

                stage(f"Wq{L}", wq)
                attention(a)
                if L == 1:
                    act.dma_start(kvw[:, :], kvw3).then_inc(kvw_in[2], 16)
                    for b in range(2):
                        context(att_2, b)
                    act.wait_ge(att_1.summed, att_1.steps)
                    for b in range(4):
                        key_major(b)
                stage(f"Wo{L}", None)
                stage(f"ff{L}", hidden(f"ff{L}"))
                if L == 1:
                    def memp(half, m):
                        bank = empty(("mem", half, m))
                        nc.scalar.mul(hw[:, m, hcols(half)], bank[:, 0:HALF], -float(D) ** -0.5).then_inc(emptied["act"], 1)

                    stage("mem", memp)
                    attention(att_2)
                    act.wait_ge(att_1.masked, B)
                    for b in range(2):
                        context(att_3, b)

                    def memt(half, m):
                        bank = empty(("memT", half, m))
                        nc.scalar.copy(mc[:, m, hcols(half)], bank[:, 0:HALF]).then_inc(emptied["act"], 1)

                    stage("memT", memt)

                    def fgate(half, m):
                        i = half * KD + m
                        bank = empty(("gate", half, m))
                        if i >= 2:
                            act.wait_ge(fused_done, i - 1)
                        nc.scalar.activation(scr[:, i % 2, :], bank[:, 0:HALF], ACT.Sigmoid,
                                             bias=vec[:, VECS.index("L2_xattn_b_gate"), m:m + 1])\
                            .then_inc(emptied["act"], 1)

                    stage("gate", fgate)

        @block.vector
        def _(dve):
            given = [0]
            links = [0]

            def link(ins):
                links[0] += 1
                ins.then_inc(chain, 1)
                return links[0]

            def empty(key):
                n, who, count = plan.tiles[key]
                given[0] += 1
                assert who == "dve" and count == given[0]
                dve.wait_ge(tile_ready, n + 1)
                return pool_bank(n)

            def norm_part(nn, half, part):
                kind, wname, bname, e = NORMS[nn]
                cols = hcols(half)
                w = vec[:, VECS.index(wname), :]
                if part == "m":
                    bank = empty(("mean", nn, half))
                    for k in range(KD):
                        x_ready(dve, nn, half, k)
                        ins = nc.vector.tensor_sub(xc[:, k, :], x[:, k, cols], bank[:, 0:HALF])
                        ins.then_inc(centred if k < KD - 1 else emptied["dve"], 1)
                elif part == "f":
                    tile_done(dve, ("var", nn, half))
                    nc.vector.reciprocal(rstd[:, :], std[:, :]).then_inc(std_used, 1)
                    dve.wait_ge(std_used, turn_of[nn, half] + 1)
                    if nn == 5:
                        for k in range(KD):
                            last = nc.vector.scalar_tensor_tensor(x[:, k, cols], fused[:, k, cols], w[:, k:k + 1],
                                                                  rstd[:, :], ALU.mult, ALU.mult)
                        last.then_inc(normed, 1)
                        return
                    for k in range(KD):
                        if kind == "rms":
                            x_ready(dve, nn, half, k)
                        src = x[:, k, cols] if kind == "rms" else xc[:, k, :]
                        nc.vector.scalar_tensor_tensor(xc[:, k, :], src, w[:, k:k + 1], rstd[:, :],
                                                       ALU.mult, ALU.mult).then_inc(nraw, 1)
                    for k in range(KD):
                        dve.wait_ge(nhigh, split_turn[nn, half] * KD + k + 1)
                        high = nh_[:, k, cols].bitcast(F32)
                        if kind == "rms":
                            last = nc.vector.tensor_sub(nl_[:, k, cols], xc[:, k, :], high)
                        else:
                            bias = vec[:, VECS.index(bname), k:k + 1]
                            last = nc.vector.scalar_tensor_tensor(nl_[:, k, cols], xc[:, k, :], bias, high,
                                                                  ALU.add, ALU.subtract)
                    last.then_inc(normed, 1)

            def stage(name, each):
                for it in SEQ[name]:
                    if it[0] == "norm":
                        norm_part(*it[1:])
                    elif each:
                        each(it[1], it[2])

            def residual(name, gate=None):
                def each(half, m):
                    bank = empty((name, half, m))
                    xs = x[:, m, hcols(half)]
                    if gate is None:
                        ins = nc.vector.tensor_add(xs, bank[:, 0:HALF], xs)
                    else:
                        ins = nc.vector.scalar_tensor_tensor(xs, bank[:, 0:HALF], gate_t[:, gate:gate + 1], xs,
                                                             ALU.mult, ALU.add)
                    ins.then_inc(emptied["dve"], 1)
                return each

            def out_group(a, p):
                dve.wait_ge(a.summed, (p + 1) * a.pvgroup)
                s = p * a.pvgroup
                b, h = s // a.nh, s % a.nh
                if a is att_2:
                    nc.vector.tensor_copy(pc[:, :, bcols(b)], pv_bank[:, 0:KC * S].rearrange("p (e s) -> p e s", e=KC))\
                        .then_inc(a.out, 1)
                    return
                t = h // a.pvgroup
                high = (nh_ if a in (att_self, att_c0) else oh8)[:, t, bcols(b)]
                low = (nl_ if a in (att_self, att_c0) else ol8)[:, t, bcols(b)]
                n = link(nc.vector.tensor_copy(high, pv_bank[:, 0:S]))
                dve.wait_ge(chain, n)
                nc.vector.tensor_sub(low, pv_bank[:, 0:S], high.bitcast(F32)).then_inc(a.out, 1)

            def attention(a):
                for s in range(a.steps + a.pvlag):
                    r = s - 1
                    if 0 <= r < a.steps:
                        dve.wait_ge(a.exped, r + 1)
                        nc.vector.reciprocal(rinv[:, r % NPROB:r % NPROB + 1], rsum[:, r % NPROB:r % NPROB + 1])\
                            .then_inc(a.recip, 1)
                    if s < a.steps:
                        b, h = s // a.nh, s % a.nh
                        col = nmin[:, s % NPROB:s % NPROB + 1]
                        dve.wait_ge(a.scored, s + 1)
                        if a.mask:
                            if a.mask == "keys" and h == 0:
                                dve.wait_ge(a.mask_in[b % 2], 16 * (b // 2 + 1))
                                nc.vector.tensor_scalar(maskf[:, b % 2, :], mask8[:, b % 2, :], -BIG, BIG,
                                                        ALU.mult, ALU.add).then_inc(a.masked, 1)
                                dve.wait_ge(a.masked, b + 1)
                            if s >= 2:
                                dve.wait_ge(a.exped, s - 1)
                            m = causal if a.mask == "causal" else maskf[:, b % 2, :]
                            nc.vector.tensor_tensor_reduce(out=masked_s[s % 2][:, 0:a.nk], in0=s_bank(s)[:, 0:a.nk],
                                                           in1=m, scale=1.0, scalar=BIG, op0=ALU.add, op1=ALU.min,
                                                           accum_out=col).then_inc(a.maxed, 1)
                        else:
                            nc.vector.tensor_reduce(col, s_bank(s)[:, 0:a.nk], AX_X, ALU.min).then_inc(a.maxed, 1)
                    if 0 <= r < a.steps:
                        dve.wait_ge(a.recip, r + 1)
                        pr = probs[r % NPROB][:, 0:a.nk]
                        nc.vector.tensor_scalar(pr, pr, rinv[:, r % NPROB:r % NPROB + 1], None, ALU.mult)\
                            .then_inc(a.scaled, 1)
                    w = s - a.pvlag
                    if w >= 0 and w % a.pvgroup == a.pvgroup - 1:
                        out_group(a, w // a.pvgroup)

            nc.vector.memset(vc[:, :, :, :, :].rearrange("p a b c d -> p (a b c d)"), 0.0).then_inc(vzero, 1)
            nc.vector.memset(eps[:, 0:1], 1e-6).then_inc(eps_done, 1)
            nc.vector.memset(eps[:, 1:2], 1e-5).then_inc(eps_done, 1)
            tti = kvw[:, 0:T].bitcast(I32).rearrange("p (b s) -> p b s", b=B)
            one = kvw[:, T:2 * T].rearrange("p (b s) -> p b s", b=B)
            dve.wait_ge(tt_in, 16)
            link(nc.vector.tensor_scalar(one, tti, 1.0, None, ALU.is_equal))
            link(nc.vector.memset(vm[:, :, :], 0.0))
            dve.wait_ge(chain, links[0])
            dve.wait_ge(chain, link(nc.vector.tensor_mul(vm[:, :, 0:S - 1], one[:, :, 0:S - 1], one[:, :, 1:S])))
            link(nc.vector.tensor_scalar(vml[:, :, :], vm[:, :, :], -1.0, 1.0, ALU.mult, ALU.add))
            dve.wait_ge(ttT_in, 16)
            ttf = scr[0:S, 2, 0:2 * B]
            tti2 = scr[0:S, 2, 2 * B:4 * B].bitcast(I32)
            dve.wait_ge(chain, link(nc.vector.tensor_scalar(ttf, tti2, 1.0, None, ALU.is_equal)))
            nc.vector.tensor_mul(vmT[:, 0, :], ttf[:, 0:B], ttf[:, B:2 * B]).then_inc(vmT_done, 1)
            dve.wait_ge(vmT_done, 1)
            nc.vector.tensor_scalar(vmT[:, 1, :], vmT[:, 0, :], -1.0, 1.0, ALU.mult, ALU.add).then_inc(vmT_done, 1)
            posf = scr[0:S, 1, 0:S]
            wrap = scr[0:S, 2, 128:128 + S]
            dve.wait_ge(pos_in, 16)
            dve.wait_ge(cst_in, 16)
            dve.wait_ge(chain, link(nc.vector.tensor_copy(posf, scr[0:S, 3, 0:S].bitcast(I32))))
            dve.wait_ge(chain, link(nc.vector.tensor_scalar(wrap, posf, 0.0, float(S), ALU.is_lt, ALU.mult)))
            dve.wait_ge(chain, link(nc.vector.tensor_add(posf, posf, wrap)))
            dve.wait_ge(chain, link(nc.vector.tensor_scalar(wrap, posf, 0.0, float(S - 1), ALU.max, ALU.min)))
            nc.vector.tensor_scalar(scr[0:S, 0, 0:S], wrap, cst[0:S, C_POS:C_POS + 1], None, ALU.is_equal)\
                .then_inc(onehot_done, 1)
            dve.wait_ge(vec_in, 16)

            def experts(name, half, m, scale, out):
                hb = slice(half * BPH, (half + 1) * BPH)
                first = empty((name, half, m, 0))
                a0, t = out, scr[:, 2 + m % 2, :]
                n0 = link(nc.vector.scalar_tensor_tensor(a0, first[:, 0:HALF], scale,
                                                         vm[:, hb, :].rearrange("p b s -> p (b s)"), ALU.mult, ALU.mult))
                dve.wait_ge(chain, n0)
                dve.sem_inc(emptied["dve"], 1)
                second = empty((name, half, m, 1))
                n1 = link(nc.vector.scalar_tensor_tensor(t, second[:, 0:HALF], scale,
                                                         vml[:, hb, :].rearrange("p b s -> p (b s)"), ALU.mult, ALU.mult))
                dve.wait_ge(chain, n1)
                return t

            def rope(i):
                _, half, m = RAW[i]
                n, who, count = plan.tiles[("rot", i)]
                given[0] += 1
                assert count == given[0]
                if i == 0:
                    tile_done(dve, ("table", 1))
                raw_t = scr[:, i % 2, :].rearrange("p (b s) -> p b s", b=BPH)
                t = xc[:, i % 2, :].rearrange("p (b s) -> p b s", b=BPH)
                cos = cosT[:, :].unsqueeze(1).broadcast_to([P, BPH, S])
                sin = sinT[:, :].unsqueeze(1).broadcast_to([P, BPH, S])
                dst = (qT if m < KD else kT)[:, m % KD, hcols(half)].rearrange("p (b s) -> p b s", b=BPH)
                link(nc.vector.tensor_mul(t, raw_t, cos))
                dve.wait_ge(tile_ready, n + 1)
                bank = pool_bank(n)[:, 0:HALF].rearrange("p (b s) -> p b s", b=BPH)
                nc.vector.tensor_mul(dst, bank, sin).then_inc(emptied["dve"], 1)
                dve.wait_ge(chain, links[0])
                dve.wait_ge(emptied["dve"], count)
                nc.vector.tensor_add(dst, dst, t).then_inc(rope_done, 1)

            done = [0]

            def qk(half, m):
                i = done[0]
                done[0] += 1
                out = scr[:, i % 2, :]
                t = experts("qk", half, m, -float(32) ** -0.5 if m < KD else 1.0, out)
                dve.sem_inc(emptied["dve"], 1)
                nc.vector.tensor_add(out, out, t).then_inc(raw_qk, 1)
                dve.wait_ge(raw_qk, i + 1)
                if i >= 1:
                    rope(i - 1)

            stage("qk", qk)
            rope(done[0] - 1)
            for b in range(B):
                bank = empty(("vproj", b, 1))
                tile_done(dve, ("vproj", b, 0))
                nc.vector.scalar_tensor_tensor(vS[:, b, :], bank[0:S, :], vmT[:, 1, b:b + 1], vtmp[:, b % 2, :],
                                               ALU.mult, ALU.add).then_inc(emptied["dve"], 1)
            attention(att_self)

            def dense(half, m):
                xs = x[:, m, hcols(half)]
                out = scr[:, m % 2, :]
                t = experts("dense", half, m, 1.0, out)
                dve.wait_ge(chain, link(nc.vector.tensor_add(xs, xs, out)))
                nc.vector.tensor_add(xs, xs, t).then_inc(emptied["dve"], 1)

            stage("dense", dense)
            stage("cq", None)
            attention(att_c0)
            stage("cdense", residual("cdense"))

            def hidden(name, gate=None):
                nt = HIDDEN[name]

                def low(g, src):
                    dve.wait_ge(hid_high, g + 1)
                    nc.vector.tensor_sub(hid_l[:, g % 2, :], src, hid_h[:, g % 2, :].bitcast(F32)).then_inc(hid_low, 1)

                def each(half, m):
                    g = hid_no(name, half, m)
                    if name == "mlp":
                        mine = (vm if m < ITILES else vml)[:, half * BPH:(half + 1) * BPH, :].rearrange("p b s -> p (b s)")
                        tile_done(dve, (name, half, m, 0))
                        dve.wait_ge(chain, link(nc.vector.tensor_mul(scr[:, g % 2, :], scr[:, g % 2, :], mine)))
                        bank = empty((name, half, m, 1))
                        if g >= 2:
                            dve.wait_ge(hid_low, g - 1)
                        n = given[0]
                        nc.vector.tensor_mul(scr[:, 2 + g % 2, :], bank[:, 0:HALF], scr[:, g % 2, :])\
                            .then_inc(emptied["dve"], 1)
                        dve.wait_ge(emptied["dve"], n)
                        dve.sem_inc(hid_done, 1)
                        if m >= 1:
                            low(g - 1, scr[:, 2 + (g - 1) % 2, :])
                        if m == nt - 1:
                            low(g, scr[:, 2 + g % 2, :])
                    else:
                        low(g, scr[:, g % 2, :])
                    if m == nt - 1:
                        dve.wait_ge(acc_step, g + 1)
                        for k in range(KD):
                            xs, acc = x[:, k, hcols(half)], psum[:, 4 + k, 0:HALF]
                            if gate is None:
                                ins = nc.vector.tensor_add(xs, acc, xs)
                            else:
                                ins = nc.vector.scalar_tensor_tensor(xs, acc, gate_t[:, gate:gate + 1], xs,
                                                                     ALU.mult, ALU.add)
                            ins.then_inc(acc_used, 1)
                return each

            stage("mlp", hidden("mlp"))
            dve.wait_ge(gate_done, 1)
            for L, a in ((1, att_1), (3, att_3)):
                stage(f"Wq{L}", None)
                attention(a)
                stage(f"Wo{L}", residual(f"Wo{L}", L - 1))
                stage(f"ff{L}", hidden(f"ff{L}", L))
                if L == 1:
                    stage("mem", None)
                    attention(att_2)
                    stage("memT", None)

                    def fuse(half, m):
                        i = half * KD + m
                        cols = hcols(half)
                        tile_done(dve, ("gate", half, m))
                        t = scr[:, 2 + i % 2, :]
                        dve.wait_ge(chain, link(nc.vector.tensor_mul(t, scr[:, i % 2, :], mc[:, m, cols])))
                        nc.vector.tensor_add(fused[:, m, cols], t, x[:, m, cols]).then_inc(fused_done, 1)

                    stage("gate", fuse)

        @block.gpsimd
        def _(pool):
            pool.dma_start(cst[:, :], consts).then_inc(cst_in, 16)
            pool.dma_start(vec[:, :, :], vecs).then_inc(vec_in, 16)
            pool.dma_start(kvw[:, 0:T].bitcast(I32), tt.partition_broadcast(P)).then_inc(tt_in, 16)
            pool.dma_start(scr[0:S, 2, 2 * B:4 * B].bitcast(I32), ttT).then_inc(ttT_in, 16)
            pool.dma_start(scr[0:S, 3, 0:S].bitcast(I32), pos.partition_broadcast(S)).then_inc(pos_in, 16)
            pool.dma_start(gate_in[:, :], gates.partition_broadcast(P)).then_inc(gate_in_s, 16)
            for n, u in enumerate(SPLIT_USES):
                r = USE_NO[u]
                pool.wait_ge(raw_in[r % RAW_RING], 16 * (r // RAW_RING + 1))
                if n >= RING:
                    pool.wait_ge(*chunk_last[SPLIT_USES[n - RING]])
                chunk_raw = raw[:, r % RAW_RING, :]
                nc.gpsimd.tensor_scalar(wh[:, n % RING, :], chunk_raw, 1.0, 1.0, ALU.mult, ALU.mult).then_inc(split_h, 1)
                pool.wait_ge(split_h, n + 1)
                nc.gpsimd.tensor_tensor(wl[:, n % RING, :], chunk_raw, wh[:, n % RING, :].bitcast(F32),
                                        ALU.subtract).then_inc(split_l, 1)

        @block.sync
        def _(sp):
            for n, (use, name, c) in enumerate(USES):
                if n >= RAW_RING:
                    last = USES[n - RAW_RING]
                    if last[1] in PLAIN:
                        sp.wait_ge(*chunk_last[last])
                    else:
                        sp.wait_ge(split_l, SPLIT_NO[last] + 1)
                sp.dma_start(raw[:, n % RAW_RING, :], walls[STORED0[name] + c]).then_inc(raw_in[n % RAW_RING], 16)
            for half in range(2):
                sp.wait_ge(acc_used, mlp_out("ff3", half) + KD)
                sp.dma_start(outT[:, :, hcols(half)], x[:, :, hcols(half)]).then_inc(out_done, 16)
            sp.wait_ge(out_done, 32)


def kernel(**inputs):
    import numpy as np
    import concourse.bacc as bacc
    from concourse.bass_utils import run_bass_kernel_spmd

    def get(name):
        return np.asarray(inputs[name])

    def blocks(w, m):
        k_tiles = -(-w.shape[0] // P)
        out = np.zeros((k_tiles, P, P), w.dtype)
        part = w[:, m * P:(m + 1) * P]
        for k in range(k_tiles):
            rows = part[k * P:(k + 1) * P]
            out[k, :rows.shape[0], :rows.shape[1]] = rows
        return list(out)

    def v(name):
        return get(name)

    walls = np.zeros((N_STORED, P, SLOT), np.float32)

    def put(name, c, blist):
        for i, blk in enumerate(blist):
            walls[STORED0[name] + c][:, i * P:(i + 1) * P] = blk

    def put_tiles(name, ms, mpc, weights):
        for m in range(ms):
            if m % mpc == 0:
                acc = []
            for w in weights:
                acc += blocks(w, m)
            if m % mpc == mpc - 1 or m == ms - 1:
                put(name, m // mpc, acc)

    def out_blocks(w, k):
        out = np.zeros((P, D), w.dtype)
        rows = w[k * P:(k + 1) * P]
        out[:rows.shape[0]] = rows
        return [out[:, m * P:(m + 1) * P] for m in range(KD)]

    vq, lq = v("L0_xattn_v_qkv"), v("L0_xattn_l_qkv")
    put_tiles("qk", 8, 1, [vq, lq])
    for e, w in enumerate((vq, lq)):
        for j in range(2):
            part = w[2 * j * P:2 * (j + 1) * P, 2 * D:]
            walls[STORED0["v"] + 2 * e + j] = part.reshape(2, P, D).transpose(1, 0, 2).reshape(P, 2 * D)
    put_tiles("dense", 4, 1, [v("L0_xattn_v_dense"), v("L0_xattn_l_dense")])
    put_tiles("cq", 2, 2, [v("L0_xattn_cq_w")])
    put_tiles("cdense", 4, 4, [v("L0_xattn_cdense_w")])
    downs = []
    for j, e in enumerate("vl"):
        gate, up = v(f"L0_xattn_{e}_gate"), v(f"L0_xattn_{e}_up")
        for m in range(ITILES):
            put("gu", j * ITILES + m, blocks(gate, m) + blocks(up, m))
            downs += out_blocks(v(f"L0_xattn_{e}_down"), m)
    for c in range(ETILES // 2):
        put("down", c, downs[8 * c:8 * c + 8])
    for L in "13":
        put_tiles("Wq" + L, 8, 2, [v(f"L{L}_xattn_Wq")])
        put_tiles("Wo" + L, 4, 1, [v(f"L{L}_xattn_Wo")])
        for m in range(16):
            put("ff" + L, m, blocks(v(f"L{L}_xattn_W1"), m) + out_blocks(v(f"L{L}_xattn_W2"), m))
    put_tiles("mem", 2, 2, [v("L2_xattn_W_mem")])
    put_tiles("memT", 4, 4, [v("L2_xattn_W_mem").T])
    put_tiles("gate", 4, 1, [v("L2_xattn_W_gate").T])

    def rows_first(w):
        k = w.shape[0] // P
        return np.ascontiguousarray(w.reshape(k, P, w.shape[1]).transpose(1, 0, 2).reshape(P, -1))

    c = np.zeros((P, C_END), np.float32)
    c[:, C_ID:C_ID + P] = np.eye(P)
    c[:, C_MEAN:C_MEAN + P] = 1.0 / D
    for m in range(P):
        if m % 32 < 16:
            c[m + 16, C_ROT + m] = -1.0
        else:
            c[m - 16, C_ROT + m] = 1.0
    inv = (1.0 / np.float32(10000.0) ** (np.arange(0, 32, 2, dtype=np.float32) / np.float32(32))).astype(np.float32)
    freqs = np.outer(np.arange(S, dtype=np.float32), inv).astype(np.float32)
    emb = np.tile(freqs, (1, P // 16))
    c[0:S, C_COS:C_COS + P] = np.cos(emb)
    c[0:S, C_SIN:C_SIN + P] = np.sin(emb)
    q, k = np.arange(S)[:, None], np.arange(S)[None, :]
    c[0:S, C_CAUSAL:C_CAUSAL + S] = np.where(k > q, np.float32(BIG), np.float32(0))
    c[:, C_POS] = np.arange(P)
    c[:, C_EVEN] = np.arange(P) // 16 % 2 == 0
    c[:, C_ODD] = np.arange(P) // 16 % 2 == 1

    ctx = get("ctx_1024")
    types = get("mask_BxS_ik0").T
    after = np.concatenate([types[1:], np.zeros_like(types[:1])])
    arrays = {
        "xT": np.ascontiguousarray(get("x").reshape(T, KD, P).transpose(2, 1, 0)),
        "ctxF": np.ascontiguousarray(ctx.reshape(B, S2, KC, P).transpose(0, 3, 2, 1)),
        "ctxK": np.ascontiguousarray(ctx.reshape(B, CH, KEYS, CC).transpose(0, 2, 1, 3)).reshape(B, KEYS, CH * CC),
        "kmask": get("mask_BxS2_bk0").reshape(B, S2),
        "tt": get("mask_BxS_ik0").reshape(T),
        "ttT": np.ascontiguousarray(np.concatenate([types, after], axis=1)),
        "pos": get("pos_1xS").reshape(S),
        "walls": walls,
        "kvw0": rows_first(get("L0_xattn_ckv_w")),
        "kvw1": rows_first(get("L1_xattn_Wkv")),
        "kvw3": rows_first(get("L3_xattn_Wkv")),
        "vecs": np.ascontiguousarray(np.stack([get(n).reshape(KD, P) for n in VECS]).transpose(2, 0, 1)),
        "gates": np.concatenate([get("L1_xattn_attn_gate"), get("L1_xattn_ff_gate"),
                                 get("L3_xattn_attn_gate"), get("L3_xattn_ff_gate")]),
        "consts": c,
    }
    nc = bacc.Bacc("TRN2", target_bir_lowering=False, num_devices=1)
    args = [nc.dram_tensor(f"in_{n}", a.shape, mybir.dt.from_np(a.dtype), kind="ExternalInput").ap()
            for n, a in arrays.items()]
    out = nc.dram_tensor("outT", [P, KD, T], F32, kind="ExternalOutput").ap()
    build(nc, *args, out)
    r = run_bass_kernel_spmd(nc, [{f"in_{n}": a for n, a in arrays.items()}], core_ids=[0])
    got = r.results[0]["outT"]
    return np.ascontiguousarray(np.asarray(got).transpose(2, 1, 0)).reshape(B, S, D)
```

```python
from contextlib import ExitStack

import concourse.bass as bass
from concourse import mybir

F32 = mybir.dt.float32
F32R = mybir.dt.float32r
U8 = mybir.dt.uint8
I32 = mybir.dt.int32
ALU = mybir.AluOpType
ACT = mybir.ActivationFunctionType
AX_X = mybir.AxisListType.X

P = 128
SCRATCH = 1024
B, S, D = 8, 112, 512
T = B * S
HALF = T // 2
BPH = B // 2
KD = D // P
S2, CC, KEYS = 375, 256, 125
KC = CC // P
CH = S2 // KEYS
NH = 16
ITILES = 11
INNER = 1024
FF = 2048
BLOCKS = 8
SLOT = BLOCKS * P
RAW_RING = 3
RING = 4
BIG = 3.4028234663852886e38
LAG = 2
NPROB = 4
NTURN = 3
POOL = 3

STORED = [("qk", 8), ("v", 4), ("dense", 4), ("kv0", 1), ("cq", 1), ("cdense", 1), ("gu", 22), ("down", 11),
          ("kv1", 4), ("Wq1", 4), ("Wo1", 4), ("kv3", 4), ("ff1", 16), ("mem", 1), ("memT", 1), ("gate", 4),
          ("Wq3", 4), ("Wo3", 4), ("ff3", 16)]
STORED0 = {}
N_STORED = 0
for _name, _n in STORED:
    STORED0[_name] = N_STORED
    N_STORED += _n
PLAIN = {"mem", "memT", "gate"}

ETILES = 2 * ITILES


def mlp_chunks():
    out = []
    for i in range(ETILES):
        out.append(("gu", i))
        if i % 2:
            out.append(("down", i // 2))
    return out


def uses(name):
    n = dict(STORED)[name]
    if name == "gu":
        return [(half, m, c) for half in range(2) for m, c in mlp_chunks()]
    if name in ("ff1", "ff3", "gate"):
        return [(half, name, c) for half in range(2) for c in range(n)]
    return [(0, name, c) for c in range(n)]


def batches(kind, *bs):
    return [(0, kind, b) for b in bs]


def per_batch(L):
    return [u for b in range(2, B) for u in ((0, f"ctx{L}", b), (0, f"q{L}", b))]


def with_kv1(chunks):
    out = list(chunks)
    for c, u in enumerate(uses("kv1")):
        out.insert(out.index((1, "gu", 4 + 4 * c)), u)
    return out


WORK = (uses("qk") + batches("mself", 0, 1) + uses("v") + uses("dense") + batches("ctx0", 0, 1) +
        batches("mself", *range(2, B)) + uses("kv0") + uses("cq") + batches("mcross", 0, 1) +
        [u for b in range(2, B) for u in ((0, "ctx0", b), (0, "mcross", b))] + uses("cdense") + with_kv1(uses("gu")) +
        batches("ctx1", 0, 1) + uses("Wq1") + batches("q1", 0, 1) + uses("Wo1") + per_batch(1) + uses("kv3") +
        uses("ff1") + uses("mem") + uses("memT") + uses("gate") +
        batches("ctx3", 0, 1) + uses("Wq3") + batches("q3", 0, 1) + uses("Wo3") + per_batch(3) + uses("ff3"))
MASKINGS = ("mself", "mcross")
USES = [u for u in WORK if u[1] not in ("q1", "q3") + MASKINGS]
USES_OF = {name: uses(name) for name in ("kv0", "kv1", "kv3")}
USE_NO = {u: n for n, u in enumerate(USES)}
SPLITS = [u for u in WORK if u[1] not in PLAIN and u[1] not in MASKINGS]
SPLIT_NO = {u: n for n, u in enumerate(SPLITS)}
RING_USES = [u for u in SPLITS if u[1][:2] not in ("kv", "ct", "q1", "q3")]
RING_NO = {u: n for n, u in enumerate(RING_USES)}

VECS = ["L0_xattn_ln_in_w", "L0_xattn_ln_post_cross_w", "L0_xattn_ln_post_attn_w",
        "L1_xattn_ln_q_g", "L1_xattn_ln_q_b", "L1_xattn_ln_ff_g", "L1_xattn_ln_ff_b",
        "L2_xattn_norm_w", "L2_xattn_b_gate",
        "L3_xattn_ln_q_g", "L3_xattn_ln_q_b", "L3_xattn_ln_ff_g", "L3_xattn_ln_ff_b"]

C_ID, C_MEAN, C_ROT, C_COS, C_SIN, C_CAUSAL, C_POS, C_EVEN, C_ODD, C_H4, C_H8, C_END = (
    0, 128, 256, 384, 512, 640, 752, 753, 754, 755, 759, 767)

NORMS = [("rms", "L0_xattn_ln_in_w", None, 1e-6), ("rms", "L0_xattn_ln_post_cross_w", None, 1e-6),
         ("rms", "L0_xattn_ln_post_attn_w", None, 1e-6),
         ("ln", "L1_xattn_ln_q_g", "L1_xattn_ln_q_b", 1e-5), ("ln", "L1_xattn_ln_ff_g", "L1_xattn_ln_ff_b", 1e-5),
         ("rms", "L2_xattn_norm_w", None, 1e-6),
         ("ln", "L3_xattn_ln_q_g", "L3_xattn_ln_q_b", 1e-5), ("ln", "L3_xattn_ln_ff_g", "L3_xattn_ln_ff_b", 1e-5)]

class PoolPlan:

    def __init__(self):
        self.n = 0
        self.count = {"act": 0, "dve": 0}
        self.tiles = {}
        self.order = []

    def add(self, key, who):
        self.count[who] += 1
        self.tiles[key] = (self.n, who, self.count[who])
        self.order.append((who, self.count[who]))
        self.n += 1
        return self.n - 1


class Attention:

    def __init__(self, name, nh, nk, group, pvgroup, mask, k_heads, v_heads, sem):
        self.name, self.nh, self.nk, self.group, self.pvgroup, self.mask = name, nh, nk, group, pvgroup, mask
        self.chunks = 1 if nk <= P else CH
        self.kw = nk // self.chunks
        self.steps = B * nh
        self.k_heads, self.v_heads = k_heads, v_heads
        self.pvlag = LAG + group + 1
        self.scored = sem(name + "_scored")
        self.maxed = sem(name + "_maxed")
        self.exped = sem(name + "_exped")
        self.recip = sem(name + "_recip")
        self.scaled = sem(name + "_scaled")
        self.turned = sem(name + "_turned")
        self.probs_out = sem(name + "_probs_out")
        self.summed = sem(name + "_summed")
        self.out = sem(name + "_out")
        self.k_high = sem(name + "_k_high")
        self.mask_in = [sem(f"{name}_mask_in{i}") for i in range(2)]
        self.masked = sem(name + "_masked")


def build(nc, xT, ctxF, ctxK, kmask, tt, ttT, pos, walls, vecs, gates, consts, outT):
    ctx = ExitStack()
    with ctx:
        place = [SCRATCH + 128]

        def at(name, shape, dt, offset):
            return nc.alloc_sbuf_tensor_at(name, shape, dt, offset=offset)

        def sb(name, shape, dt=F32):
            size = 1 if dt == U8 else 4
            for d in shape[1:]:
                size *= d
            offset = place[0]
            place[0] += -(-size // 32) * 32
            return at(name, shape, dt, offset)

        def sem(name):
            return ctx.enter_context(nc.semaphore(name))

        raw = sb("raw", [P, RAW_RING, SLOT])
        wh = sb("wh", [P, RING, SLOT], F32R)
        wl = sb("wl", [P, RING, SLOT], F32R)
        o_h = place[0]
        kvwh = sb("kvwh", [P, 2 * FF], F32R)
        o_v = place[0]
        kvwl = sb("kvwl", [P, 2 * FF], F32R)
        qm = at("qm", [P, 2, KD, 4, S], F32, o_h)
        qmx = at("qmx", [P, 2, 2, KC, 8, S], F32R, o_h)
        vself = at("vself", [P, 2 * FF], F32, o_v)
        x = sb("x", [P, KD, T])
        o_f = place[0]
        nh_ = sb("nh", [P, KD, T], F32R)
        nl_ = sb("nl", [P, KD, T], F32R)
        ol8 = at("ol8", [P, INNER // P, T], F32R, o_f)
        fused = at("fused", [P, KD, T], F32, o_f)
        o_q = place[0]
        q1 = sb("q1", [P, INNER // P, T])
        qT = at("qT", [P, KD, T], F32, o_q)
        kT = at("kT", [P, KD, T], F32, o_q + 4 * KD * T)
        qch = at("qch", [P, KC, T], F32R, o_q)
        qcl = at("qcl", [P, KC, T], F32R, o_q + 4 * KC * T)
        kv0h = at("kv0h", [P, KC * 2 * CC], F32R, o_q + 8 * KC * T)
        kv0l = at("kv0l", [P, KC * 2 * CC], F32R, o_q + 8 * KC * T + 8 * KC * CC)
        oh8 = at("oh8", [P, INNER // P, T], F32R, o_q)
        hw = at("hw", [P, KC, T], F32, o_q)
        pc = at("pc", [P, KC, T], F32, o_q + 4 * KC * T)
        mc = at("mc", [P, KD, T], F32, o_q + 8 * KC * T)
        o_k = place[0]
        kh = sb("kh", [P, 2, 376], F32R)
        kl = sb("kl", [P, 2, 376], F32R)
        v1 = sb("v1", [P, 2, CH, 2 * P])
        ctxt = at("ctxt", [P, 4, CH * CC], F32, o_k)
        place[0] = max(place[0], o_k + 4 * 4 * CH * CC)
        o_c = place[0]
        ctxh = sb("ctxh", [P, 2, KC, 376], F32R)
        ctxl = sb("ctxl", [P, 2, KC, 376], F32R)
        ctxb = at("ctxb", [P, 2, KC, 376], F32, o_c)
        mask8 = sb("mask8", [S, 2, S2], U8)
        maskf = sb("maskf", [S, 2, S2])
        vm = sb("vm", [P, B, S])
        vml = sb("vml", [P, B, S])
        vmT = sb("vmT", [S, 2, B])
        o_s = place[0]
        scr = sb("scr", [P, 4, HALF])
        xc = sb("xc", [P, KD, HALF])
        qs = at("qs", [P, 2, 2, INNER // P, S], F32R, o_s)
        sq = sb("sq", [P, 2, HALF])
        total = sb("total", [P, HALF])
        std = sb("std", [P, HALF])
        rstd = sb("rstd", [P, HALF])
        cst = sb("cst", [P, C_END])
        vec = sb("vec", [P, len(VECS), KD])
        cosT = sb("cosT", [P, S])
        sinT = sb("sinT", [P, S])
        gate_in = sb("gate_in", [P, 4])
        gate_t = sb("gate_t", [P, 4])
        pick = sb("pick", [P, S])
        nmin = sb("nmin", [S, NPROB])
        rsum = sb("rsum", [S, NPROB])
        rinv = sb("rinv", [S, NPROB])
        eps = sb("eps", [P, 2])
        o_a = place[0]
        masked_t = sb("masked_t", [S, 2, S2])
        probs_t = sb("probs_t", [S, NPROB, S2])
        probsT_t = sb("probsT_t", [P, NTURN, 4 * S])
        hid_h = at("hid_h", [P, 2, HALF], F32R, o_a)
        hid_l = at("hid_l", [P, 2, HALF], F32R, o_a + 8 * HALF)
        vtmp = at("vtmp", [S, 2, D], F32, o_a)
        assert place[0] <= 229344, place[0]
        vS = vself[0:S, :].rearrange("p (b d) -> p b d", b=B)
        masked_s = [masked_t[:, i, :] for i in range(2)]
        probs = [probs_t[:, i, :] for i in range(NPROB)]
        probsT = [probsT_t[:, i, :] for i in range(NTURN)]

        psum = ctx.enter_context(nc.psum_tensor("psum", [P, 8, 512], F32))

        def pool_bank(n):
            return psum[:, n % POOL, :]

        def s_bank(s):
            return psum[0:S, 3 + s % 2, :]

        def t_bank(g):
            return psum[:, 5 + g % 2, :]

        pv_bank = psum[:, 7, :]

        ident = cst[:, C_ID:C_ID + P]
        mean_w = cst[:, C_MEAN:C_MEAN + P]
        rot_w = cst[:, C_ROT:C_ROT + P]
        causal = cst[0:S, C_CAUSAL:C_CAUSAL + S]

        raw_in = [sem(f"raw_in{i}") for i in range(RAW_RING)]
        split_h = sem("split_h")
        split_l = sem("split_l")
        acc_step = sem("acc_step")
        acc_used = sem("acc_used")
        hid_done = sem("hid_done")
        hid_high = sem("hid_high")
        hid_low = sem("hid_low")
        nraw = sem("nraw")
        nhigh = sem("nhigh")
        raw_qk = sem("raw_qk")
        tile_ready = sem("tile_ready")
        emptied = {"act": sem("emptied_act"), "dve": sem("emptied_dve")}
        x_in = sem("x_in")
        cst_in = sem("cst_in")
        vec_in = sem("vec_in")
        tt_in = sem("tt_in")
        ttT_in = sem("ttT_in")
        laid_out = sem("laid_out")
        pad_done = sem("pad_done")
        q_high = sem("q_high")
        vmT_done = sem("vmT_done")
        pos_in = sem("pos_in")
        gate_in_s = sem("gate_in_s")
        gate_done = sem("gate_done")
        eps_done = sem("eps_done")
        onehot_done = sem("onehot_done")
        rope_done = sem("rope_done")
        fused_done = sem("fused_done")
        chain = sem("chain")
        out_done = sem("out_done")
        ctx2_in = [sem(f"ctx2_in{i}") for i in range(2)]
        ctxt_in = [sem(f"ctxt_in{i}") for i in range(4)]
        sq_ready = sem("sq_ready")
        sq_used = sem("sq_used")
        summed_up = sem("summed_up")
        std_used = sem("std_used")
        normed = sem("normed")
        centred = sem("centred")

        att_self = Attention("self", NH, S, 4, 4, "causal", 0, 0, sem)
        att_c0 = Attention("cross0", NH, S2, 1, 8, None, 8, 16, sem)
        att_1 = Attention("cross1", NH, S2, 1, 2, "keys", 2, 4, sem)
        att_2 = Attention("memory", 1, S2, 1, 1, None, 0, 0, sem)
        att_3 = Attention("cross3", NH, S2, 1, 2, "keys", 2, 4, sem)
        ATT = {"0": att_c0, "1": att_1, "3": att_3}

        plan = PoolPlan()
        chunk_last = {}

        order = [(nn, half) for nn in range(5) for half in range(2)] + [
            (5, 0), (6, 0), (5, 1), (6, 1), (7, 0), (7, 1)]
        turn_of = {key: i for i, key in enumerate(order)}
        ln_turn = {key: i for i, key in enumerate([o for o in order if NORMS[o[0]][0] == "ln"])}

        split_turn = {key: i for i, key in enumerate([o for o in order if o[0] != 5])}

        def norm_done(eng, nn, half, k=KD - 1):
            eng.wait_ge(normed, turn_of[nn, half] * KD + k + 1)

        def tile_done(eng, key):
            _, who, count = plan.tiles[key]
            eng.wait_ge(emptied[who], count)

        def hcols(half):
            return slice(half * HALF, (half + 1) * HALF)

        def bcols(b):
            return slice(b * S, (b + 1) * S)

        def by_half(ms, mpc, hooks):
            seq = []
            for half in range(2):
                for m in range(ms):
                    seq.append(("tile", half, m, m // mpc))
                    seq += hooks.get((half, m), [])
            return seq

        def qk_order(hooks):
            seq = []
            for group in range(2):
                for half in range(2):
                    for m in range(4 * group, 4 * group + 4):
                        seq.append(("tile", half, m, m))
                        seq += hooks.get((group, half, m), [])
            return seq

        def parts(nn, half, **at_):
            out = {}
            for p, key in at_.items():
                out.setdefault(key, []).append(("norm", nn, half, p))
            return out

        def both(*hooks):
            out = {}
            for h in hooks:
                for key, v in h.items():
                    out[key] = out.get(key, []) + v
            return out

        SEQ = {
            "qk": [("norm", 0, 0, "s"), ("norm", 0, 0, "v"), ("norm", 0, 0, "f")] + qk_order(parts(0, 1, s=(0, 0, 0), v=(0, 0, 1), f=(0, 0, 1))),
            "dense": by_half(4, 1, parts(1, 0, s=(0, 3), v=(1, 0), f=(1, 1))),
            "cq": by_half(2, 2, parts(1, 1, s=(0, 0), v=(0, 0), f=(0, 1))),
            "cdense": by_half(4, 4, parts(2, 0, s=(1, 0), v=(1, 2), f=(1, 3))),
            "mlp": by_half(ETILES, 1, both(parts(2, 1, s=(0, 0), v=(0, 1), f=(0, 2)),
                                           parts(3, 0, a=(1, 1), m=(1, 2), s=(1, 3), v=(1, 4), f=(1, 5)))),
            "Wq1": by_half(8, 2, parts(3, 1, a=(0, 0), m=(0, 1), s=(0, 2), v=(0, 3), f=(0, 4))),
            "Wo1": by_half(4, 1, parts(4, 0, a=(0, 3), m=(1, 0), s=(1, 0), v=(1, 1), f=(1, 2))),
            "ff1": by_half(16, 1, parts(4, 1, a=(0, 0), m=(0, 1), s=(0, 2), v=(0, 3), f=(0, 4))),
            "mem": by_half(2, 2, {}),
            "memT": by_half(4, 4, {}),
            "gate": by_half(4, 1, both(parts(5, 0, s=(0, 3), v=(1, 0), f=(1, 0)), parts(6, 0, a=(1, 1), m=(1, 2), s=(1, 2), v=(1, 3)))) +
            [("norm", 6, 0, "f")],
            "Wq3": by_half(8, 2, both(parts(5, 1, s=(0, 0), v=(0, 0), f=(0, 1)), parts(6, 1, a=(0, 1), m=(0, 2), s=(0, 2), v=(0, 4), f=(0, 5)))),
            "Wo3": by_half(4, 1, parts(7, 0, a=(0, 3), m=(1, 0), s=(1, 0), v=(1, 1), f=(1, 2))),
            "ff3": by_half(16, 1, parts(7, 1, a=(0, 0), m=(0, 1), s=(0, 2), v=(0, 3), f=(0, 4))),
        }
        sums, sum_no = [], {}
        for name in SEQ:
            for it in SEQ[name]:
                if it[0] == "norm" and it[3] in "as":
                    what = {"a": "m", "s": "v"}[it[3]]
                    sums.append(({"m": "mean", "v": "var"}[what], it[1], it[2]))
                    sum_no[it[1], it[2], what] = len(sums)
        MLPS = ["mlp", "ff1", "ff3"]
        HIDDEN = {"mlp": ETILES, "ff1": 16, "ff3": 16}
        hid0 = {"mlp": 0, "ff1": 2 * ETILES, "ff3": 2 * ETILES + 32}

        def hid_no(name, half, m):
            return hid0[name] + half * HIDDEN[name] + m

        def mlp_out(name, half):
            return (MLPS.index(name) * 2 + half) * KD

        X_OF_NORM = {1: "dense", 2: "cdense", 3: "mlp", 4: "Wo1", 7: "Wo3"}

        def x_ready(eng, nn, half, k):
            if nn == 0:
                eng.wait_ge(x_in, 16)
            elif nn == 5:
                eng.wait_ge(fused_done, half * KD + k + 1)
            elif nn == 6:
                norm_done(eng, 5, half, k)
            elif nn == 3:
                eng.wait_ge(acc_used, mlp_out("mlp", half) + k + 1)
            elif nn == 1:
                tile_done(eng, ("dense", half, k, 1))
            else:
                tile_done(eng, (X_OF_NORM[nn], half, k))

        def norm_src(nn):
            return fused if nn == 5 else x

        RAW = [("qk",) + it[1:3] for it in SEQ["qk"] if it[0] == "tile"]

        def projected(a, s):
            if not a.k_heads:
                return []
            first = {att_c0: -4}.get(a, -1)
            second = {att_c0: -1}.get(a, 1)
            if s == -1:
                return [("K", 0, 0), ("V", 0, 0)] + ([("V", 0, 1)] if second < 0 else [])
            out = []
            if s % a.k_heads == 0:
                out.append(("K", s // a.k_heads + 1, 0))
            for part, shift in enumerate((first, second)):
                if (s - shift) % a.v_heads == 0:
                    out.append(("V", (s - shift) // a.v_heads, part))
            return [u for u in out if u[1] < a.steps // (a.k_heads if u[0] == "K" else a.v_heads)]

        block = ctx.enter_context(nc.Block())

        @block.tensor
        def _(pe):
            def begin_tile(key, who):
                n = plan.add(key, who)
                if n >= POOL:
                    w, count = plan.order[n - POOL]
                    pe.wait_ge(emptied[w], count)
                return n

            def product(out, pairs):
                for i, (lhsT, rhs) in enumerate(pairs):
                    last = nc.tensor.matmul(out, lhsT, rhs, start=(i == 0), stop=(i == len(pairs) - 1))
                return last

            def product3(out, quads, ready=None):
                n = len(quads)
                for i, (ah, al, bh, bl) in enumerate(quads):
                    if ready:
                        ready(i)
                    nc.tensor.matmul(out, ah, bh, start=(i == 0), stop=False)
                    nc.tensor.matmul(out, ah, bl, start=False, stop=False)
                    last = nc.tensor.matmul(out, al, bh, start=False, stop=(i == n - 1))
                return last

            def chunk(name, c, use=0):
                u = (use, name, c)
                if name in PLAIN:
                    n = USE_NO[u]
                    pe.wait_ge(raw_in[n % RAW_RING], 16 * (n // RAW_RING + 1))
                    return raw[:, n % RAW_RING, :]
                n = RING_NO[u]
                pe.wait_ge(split_l, SPLIT_NO[u] + 1)
                return wh[:, n % RING, :], wl[:, n % RING, :]

            def norm_part(nn, half, part):
                kind = NORMS[nn][0]
                if part == "m":
                    n = begin_tile(("mean", nn, half), "dve")
                    pe.wait_ge(summed_up, sum_no[nn, half, "m"])
                    nc.tensor.matmul(pool_bank(n)[:, 0:HALF], mean_w, total[:, :], start=True, stop=True)\
                        .then_inc(tile_ready, 1)
                elif part == "v":
                    n = begin_tile(("var", nn, half), "act")
                    pe.wait_ge(summed_up, sum_no[nn, half, "v"])
                    nc.tensor.matmul(pool_bank(n)[:, 0:HALF], mean_w, total[:, :], start=True, stop=True)\
                        .then_inc(tile_ready, 1)

            def stage(name, rhs_of, nblocks, who, mpc, ready=None, nn=None):
                seq = SEQ[name]
                seen = set()
                key = (lambda it: (it[1], it[3])) if name == "gate" else (lambda it: (0, it[3]))
                last_use = {key(it): j for j, it in enumerate(seq) if it[0] == "tile"}
                for j, it in enumerate(seq):
                    if it[0] == "norm":
                        norm_part(*it[1:])
                        continue
                    _, half, m, c = it
                    use, _c = key(it)
                    w = chunk(name, c, use)
                    first, seen = half not in seen, seen | {half}
                    if ready and (first or name in PLAIN):
                        ready(half, m)
                    for e in range(len(who)):
                        n = begin_tile((name, half, m, e) if len(who) > 1 else (name, half, m), who[e])
                        out = pool_bank(n)[:, 0:HALF]
                        base = ((m % mpc) * len(who) + e) * nblocks
                        blk = [slice((base + i) * P, (base + i + 1) * P) for i in range(nblocks)]
                        if name in PLAIN:
                            last = product(out, [(w[:, blk[i]], rhs_of(half, i)) for i in range(nblocks)])
                        else:
                            last = product3(out, [(w[0][:, blk[i]], w[1][:, blk[i]], *rhs_of(half, i))
                                                  for i in range(nblocks)],
                                            (lambda i, half=half: norm_done(pe, nn, half, i)) if nn is not None and first
                                            and e == 0 else None)
                        last.then_inc(tile_ready, 1)
                    if name == "qk" and True:
                        yield_qk(j)
                    if last_use[key(it)] == j:
                        chunk_last[(use, name, c)] = (tile_ready, plan.n)

            qk_seen = [0]

            def yield_qk(j):
                if qk_seen[0] >= 1:
                    rotate(qk_seen[0] - 1)
                qk_seen[0] += 1

            def mlp(name, nn):
                nt = HIDDEN[name]

                def down(half, i):
                    g = hid_no(name, half, i)
                    if name == "mlp":
                        u = (half, "down", i // 2)
                        base = (i % 2) * KD
                        done_with = i % 2 == 1
                    else:
                        u = (half, name, i)
                        base = KD
                        done_with = True
                    w = chunk(u[1], u[2], u[0])
                    if i == 0 and mlp_out(name, half):
                        pe.wait_ge(acc_used, mlp_out(name, half))
                    pe.wait_ge(hid_low, g + 1)
                    ah, al = hid_h[:, g % 2, :], hid_l[:, g % 2, :]
                    for m in range(KD):
                        blk = slice((base + m) * P, (base + m + 1) * P)
                        out = psum[:, 4 + m, 0:HALF]
                        nc.tensor.matmul(out, w[0][:, blk], ah, start=(i == 0), stop=False)
                        nc.tensor.matmul(out, w[0][:, blk], al, start=False, stop=False)
                        last = nc.tensor.matmul(out, w[1][:, blk], ah, start=False, stop=(i == nt - 1))
                    last.then_inc(acc_step, 1)
                    if done_with:
                        chunk_last[u] = (acc_step, g + 1)

                items = SEQ[name]
                for j, it in enumerate(items):
                    if it[0] == "norm":
                        norm_part(*it[1:])
                        continue
                    _, half, m, _c = it
                    w = chunk("gu" if name == "mlp" else name, m, half)
                    src = [(nh_[:, k, hcols(half)], nl_[:, k, hcols(half)]) for k in range(KD)]
                    for e in range(2 if name == "mlp" else 1):
                        n = begin_tile((name, half, m, e), ("act", "dve")[e])
                        blk = [slice((e * KD + k) * P, (e * KD + k + 1) * P) for k in range(KD)]
                        product3(pool_bank(n)[:, 0:HALF], [(w[0][:, blk[k]], w[1][:, blk[k]], *src[k])
                                                           for k in range(KD)],
                                 (lambda k, half=half: norm_done(pe, nn, half, k)) if m == 0 and e == 0 else None)\
                            .then_inc(tile_ready, 1)
                    if name == "mlp":
                        chunk_last[(half, "gu", m)] = (tile_ready, plan.n)
                    if m >= 1:
                        down(half, m - 1)
                    if m == nt - 1:
                        down(half, m)

            def project(a, kind, i, part):
                heads = a.k_heads if kind == "K" else a.v_heads
                b, g = i * heads // NH, i * heads % NH // heads
                width = CC if a is att_c0 else INNER
                L = a.name[-1]
                both_w = (kv0h, kv0l) if a is att_c0 else (kvwh, kvwl)
                w = [t[:, 0:KC * 2 * width].rearrange("p (k n) -> p k n", k=KC) for t in both_w]
                c = [ctxh[:, b % 2], ctxl[:, b % 2]]
                pe.wait_ge(split_l, SPLIT_NO[0, "ctx" + L, b] + 1)
                if i == 0:
                    pe.wait_ge(split_l, SPLIT_NO[USES_OF["kv" + L][-1]] + 1)
                n = begin_tile((a.name, kind, i, part), "dve" if kind == "K" else "act")
                if kind == "K":
                    cols = slice(g * P, (g + 1) * P)
                    last = product3(pool_bank(n)[:, 0:376], [(w[0][:, k, cols], w[1][:, k, cols], c[0][:, k, :], c[1][:, k, :])
                                                             for k in range(KC)])
                else:
                    cols = slice(width + g * 2 * P, width + (g + 1) * 2 * P)
                    for j in ((0, 1), (2,))[part]:
                        keys = slice(j * KEYS, (j + 1) * KEYS)
                        last = product3(pool_bank(n)[0:KEYS, j % 2 * 2 * P:(j % 2 + 1) * 2 * P],
                                        [(c[0][:, k, keys], c[1][:, k, keys], w[0][:, k, cols], w[1][:, k, cols])
                                         for k in range(KC)])
                last.then_inc(tile_ready, 1)

            def scores(a, s):
                b, h = s // a.nh, s % a.nh
                out = s_bank(s)[:, 0:a.nk]
                if a is att_self:
                    ops = [(qm[:, b % 2, h // 4, h % 4, :], kT[:, h // 4, bcols(b)])]
                elif a is att_c0:
                    q = [qmx[:, b % 2, i, h // 8, h % 8, :] for i in range(2)]
                    k = [t[:, s // 8 % 2, :] for t in (kh, kl)]
                    ops = [(*q, *k)]
                elif a is att_2:
                    ops = [(hw[:, k, bcols(b)], ctxb[:, b % 2, k, 0:S2]) for k in range(KC)]
                else:
                    r = slice(64 * (h % 2), 64 * (h % 2) + 64)
                    q = [qs[r, b % 2, i, h // 2, :] for i in range(2)]
                    k = [t[r, s // 2 % 2, :] for t in (kh, kl)]
                    ops = [(*q, *k)]
                if h == 0:
                    if a is att_self:
                        pe.wait_ge(rope_done, 16)
                        if b == 0:
                            tile_done(pe, ("vproj", B - 1, 1))
                        pe.wait_ge(laid_out, b + 1)
                    elif a is att_2:
                        pe.wait_ge(ctx2_in[b % 2], 16 * (b // 2 + 1))
                        tile_done(pe, ("mem", 1, 1))
                    elif a is att_c0:
                        pe.wait_ge(laid_out, B + b + 1)
                    else:
                        pe.wait_ge(split_l, SPLIT_NO[0, "q" + a.name[-1], b] + 1)
                if a.k_heads and s % a.k_heads == 0:
                    tile_done(pe, (a.name, "K", s // a.k_heads, 0))
                if s >= 2:
                    pe.wait_ge(a.maxed if a.mask else a.exped, s - 1)
                if a.k_heads:
                    product3(s_bank(s)[:, 0:376], ops).then_inc(a.scored, 1)
                else:
                    product(out, ops).then_inc(a.scored, 1)

            def turn(a, s):
                g = s // a.group
                pe.wait_ge(a.scaled, s + 1)
                if g >= 2 and s % a.group == 0:
                    pe.wait_ge(a.probs_out, g - 1)
                for c in range(a.chunks):
                    o = (s % a.group + c) * S
                    last = nc.tensor.transpose(t_bank(g)[0:a.kw, o:o + S],
                                               probs[s % NPROB][:, c * a.kw:(c + 1) * a.kw], ident[0:S, 0:S])
                last.then_inc(a.turned, 1)

            def weigh(a, s):
                b, h = s // a.nh, s % a.nh
                g = s // a.group
                pe.wait_ge(a.probs_out, g + 1)
                if a.v_heads and s % a.v_heads == 0:
                    tile_done(pe, (a.name, "V", s // a.v_heads, 1))
                if s % a.pvgroup == 0 and s >= a.pvgroup:
                    pe.wait_ge(a.out, s // a.pvgroup)
                pT = probsT[g % NTURN]
                if a is att_self:
                    last = nc.tensor.matmul(pv_bank[32 * (h % 4):32 * (h % 4) + 32, 0:S], vS[:, b, 32 * h:32 * h + 32],
                                            pT[0:S, (h % 4) * S:(h % 4 + 1) * S], start=True, stop=True)
                elif a is att_c0:
                    j = h // 2
                    o = 32 * (j % 4)
                    for c in range(CH):
                        last = nc.tensor.matmul(pv_bank[o:o + 32, h % 2 * S:(h % 2 + 1) * S], v1[0:KEYS, b % 2, c, 32 * j:32 * j + 32],
                                                pT[0:KEYS, c * S:(c + 1) * S], start=(c == 0), stop=(c == CH - 1))
                elif a is att_2:
                    pe.wait_ge(ctxt_in[b % 4], 16 * (b // 4 + 1))
                    for e in range(KC):
                        last = product(pv_bank[:, e * S:(e + 1) * S],
                                       [(ctxt[0:KEYS, b % 4, c * CC + e * P:c * CC + (e + 1) * P], pT[0:KEYS, c * S:(c + 1) * S])
                                        for c in range(CH)])
                else:
                    o, ov = 64 * (h % 2), 64 * (h % 4)
                    for c in range(CH):
                        last = nc.tensor.matmul(pv_bank[o:o + 64, 0:S], v1[0:KEYS, s // 4 % 2, c, ov:ov + 64],
                                                pT[0:KEYS, c * S:(c + 1) * S], start=(c == 0), stop=(c == CH - 1))
                last.then_inc(a.summed, 1)

            def attention(a):
                for s in range(a.steps + a.pvlag):
                    if s < a.steps:
                        scores(a, s)
                        for unit in projected(a, s):
                            project(a, *unit)
                    if 0 <= s - LAG < a.steps:
                        turn(a, s - LAG)
                    if s >= a.pvlag:
                        weigh(a, s - a.pvlag)

            pe.wait_ge(cst_in, 16)
            pe.wait_ge(onehot_done, 1)
            for i, c in enumerate((C_COS, C_SIN)):
                n = begin_tile(("table", i), "act")
                nc.tensor.matmul(pool_bank(n)[:, 0:S], cst[0:S, c:c + P], scr[0:S, 0, 0:S],
                                 start=True, stop=True).then_inc(tile_ready, 1)

            def nhl(half, i):
                return nh_[:, i, hcols(half)], nl_[:, i, hcols(half)]

            def rotate(i):
                pe.wait_ge(raw_qk, i + 1)
                n = begin_tile(("rot", i), "dve")
                nc.tensor.matmul(pool_bank(n)[:, 0:HALF], rot_w, scr[:, i % 2, :],
                                 start=True, stop=True).then_inc(tile_ready, 1)

            stage("qk", nhl, KD, ("dve", "dve"), 1, nn=0)
            rotate(len(RAW) - 1)

            wv = [chunk("v", c) for c in range(4)]
            for b in range(B):
                for e in range(2):
                    n = begin_tile(("vproj", b, e), ("act", "dve")[e])
                    quads = []
                    for k in range(KD):
                        h_, l_ = wv[2 * e + k // 2]
                        cols = slice((k % 2) * D, (k % 2) * D + D)
                        quads.append((nh_[:, k, bcols(b)], nl_[:, k, bcols(b)], h_[:, cols], l_[:, cols]))
                    product3(pool_bank(n)[0:S, :], quads).then_inc(tile_ready, 1)
            for c in range(4):
                chunk_last[(0, "v", c)] = (tile_ready, plan.n)

            attention(att_self)

            stage("dense", nhl, KD, ("dve", "dve"), 1,
                  ready=lambda half, m: pe.wait_ge(att_self.out, att_self.steps // 4))
            for unit in projected(att_c0, -1):
                project(att_c0, *unit)
            stage("cq", nhl, KD, ("dve",), 2, nn=1)
            attention(att_c0)
            stage("cdense", nhl, KC, ("dve",), 4, ready=lambda half, m: pe.wait_ge(att_c0.out, att_c0.steps // 8))
            mlp("mlp", 2)
            for L, a, nq, nf in ((1, att_1, 3, 4), (3, att_3, 6, 7)):
                for unit in projected(a, -1):
                    project(a, *unit)
                stage(f"Wq{L}", nhl, KD, ("act",), 2, nn=nq)
                attention(a)
                stage(f"Wo{L}", lambda half, i: (oh8[:, i, hcols(half)], ol8[:, i, hcols(half)]), 8, ("dve",), 1,
                      ready=lambda half, m, a=a: pe.wait_ge(a.out, a.steps // 2))
                mlp(f"ff{L}", nf)
                if L == 1:
                    stage("mem", lambda half, i: x[:, i, hcols(half)], KD, ("act",), 2,
                          ready=lambda half, m: pe.wait_ge(acc_used, mlp_out("ff1", half) + KD))
                    attention(att_2)
                    stage("memT", lambda half, i: pc[:, i, hcols(half)], KC, ("act",), 4,
                          ready=lambda half, m: pe.wait_ge(att_2.out, B))
                    stage("gate", lambda half, i: (x if i < KD else mc)[:, i % KD, hcols(half)], 8, ("act",), 1,
                          ready=lambda half, m: tile_done(pe, ("memT", 1, KD - 1)))

        @block.scalar
        def _(act):
            given = [0]

            def empty(key):
                n, who, count = plan.tiles[key]
                given[0] += 1
                assert who == "act" and count == given[0]
                act.wait_ge(tile_ready, n + 1)
                return pool_bank(n)

            def norm_part(nn, half, part):
                kind, wname, bname, e = NORMS[nn]
                if part == "s":
                    for k in range(KD):
                        i = turn_of[nn, half] * KD + k
                        if kind == "rms":
                            x_ready(act, nn, half, k)
                        elif k < KD - 1:
                            act.wait_ge(centred, ln_turn[nn, half] * (KD - 1) + k + 1)
                        else:
                            tile_done(act, ("mean", nn, half))
                        if i >= 2:
                            act.wait_ge(sq_used, i - 1)
                        src = norm_src(nn)[:, k, hcols(half)] if kind == "rms" else xc[:, k, :]
                        nc.scalar.activation(sq[:, i % 2, :], src, ACT.Square).then_inc(sq_ready, 1)
                elif part == "v":
                    bank = empty(("var", nn, half))
                    if turn_of[nn, half] >= 1:
                        act.wait_ge(std_used, turn_of[nn, half])
                    nc.scalar.activation(std[:, :], bank[:, 0:HALF], ACT.Sqrt,
                                         bias=eps[:, 0:1] if e == 1e-6 else eps[:, 1:2]).then_inc(emptied["act"], 1)
                elif part == "f" and nn != 5:
                    for k in range(KD):
                        act.wait_ge(nraw, split_turn[nn, half] * KD + k + 1)
                        if kind == "ln":
                            ins = nc.scalar.activation(nh_[:, k, hcols(half)], xc[:, k, :], ACT.Identity,
                                                       bias=vec[:, VECS.index(bname), k:k + 1])
                        else:
                            ins = nc.scalar.copy(nh_[:, k, hcols(half)], xc[:, k, :])
                        ins.then_inc(nhigh, 1)

            def stage(name, each):
                for it in SEQ[name]:
                    if it[0] == "norm":
                        norm_part(*it[1:])
                    elif each:
                        each(it[1], it[2])

            def context(a, b):
                if a is att_2:
                    act.dma_start(ctxb[:, b % 2, :, 0:S2], ctxF[b]).then_inc(ctx2_in[b % 2], 16)
                elif a.mask == "keys":
                    if b >= 2:
                        act.wait_ge(a.masked, b - 1)
                    act.dma_start(mask8[:, b % 2, :], kmask[b].partition_broadcast(S)).then_inc(a.mask_in[b % 2], 16)

            def project(a, kind, i, part):
                if kind == "K":
                    n = plan.tiles[a.name, kind, i, part][0]
                    act.wait_ge(tile_ready, n + 1)
                    bank = pool_bank(n)
                    if i >= 2:
                        act.wait_ge(a.scored, a.k_heads * (i - 1))
                    nc.scalar.copy(kh[:, i % 2, :], bank[:, 0:376]).then_inc(a.k_high, 1)
                    return
                bank = empty((a.name, kind, i, part))
                if i >= 2:
                    act.wait_ge(a.summed, a.v_heads * (i - 1))
                w = (2, 1)[part] * 2 * P
                dst = v1[0:KEYS, i % 2, 2 * part:2 * part + (2, 1)[part], :]
                nc.scalar.copy(dst.rearrange("p c n -> p (c n)"), bank[0:KEYS, 0:w]).then_inc(emptied["act"], 1)

            def attention(a):
                for s in range(a.steps + LAG):
                    if s < a.steps:
                        act.wait_ge(a.maxed, s + 1)
                        if s >= NPROB:
                            act.wait_ge(a.turned, s - NPROB + 1)
                        src = masked_s[s % 2][:, 0:a.nk] if a.mask else s_bank(s)[:, 0:a.nk]
                        nc.scalar.activation(probs[s % NPROB][:, 0:a.nk], src, ACT.Exp, scale=-1.0,
                                             bias=nmin[:, s % NPROB:s % NPROB + 1],
                                             accum_out=rsum[:, s % NPROB:s % NPROB + 1]).then_inc(a.exped, 1)
                        for unit in projected(a, s):
                            project(a, *unit)
                        if a.mask == "keys" and s % NH == NH - 1 and s // NH + 2 < B:
                            context(a, s // NH + 2)
                        if a is att_2 and s + 2 < B:
                            context(a, s + 2)
                    t = s - LAG
                    if t >= 0 and t % a.group == a.group - 1:
                        g = t // a.group
                        act.wait_ge(a.turned, t + 1)
                        if g >= NTURN:
                            act.wait_ge(a.summed, (g - NTURN + 1) * a.group)
                        w = max(a.group, a.chunks) * S
                        nc.scalar.copy(probsT[g % NTURN][0:a.kw, 0:w], t_bank(g)[0:a.kw, 0:w]).then_inc(a.probs_out, 1)
                        if a is att_2 and NTURN <= g and g - NTURN + 4 < B:
                            key_major(g - NTURN + 4)

            def key_major(b):
                act.dma_start(ctxt[0:KEYS, b % 4, :], ctxK[b]).then_inc(ctxt_in[b % 4], 16)

            act.dma_start(x[:, :, :], xT).then_inc(x_in, 16)
            act.dma_start(vec[:, :, :], vecs).then_inc(vec_in, 16)
            act.dma_start(gate_in[:, :], gates.partition_broadcast(P)).then_inc(gate_in_s, 16)
            act.wait_ge(eps_done, 2)
            act.wait_ge(gate_in_s, 16)
            nc.scalar.activation(gate_t[:, :], gate_in[:, :], ACT.Tanh).then_inc(gate_done, 1)
            for i, dst in enumerate((cosT, sinT)):
                bank = empty(("table", i))
                nc.scalar.copy(dst[:, :], bank[:, 0:S]).then_inc(emptied["act"], 1)

            stage("qk", None)
            act.wait_ge(vmT_done, 2)
            for b in range(B):
                bank = empty(("vproj", b, 0))
                if b >= 2:
                    tile_done(act, ("vproj", b - 2, 1))
                nc.scalar.activation(vtmp[:, b % 2, :], bank[0:S, :], ACT.Copy,
                                     scale=vmT[:, 0, b:b + 1]).then_inc(emptied["act"], 1)
            attention(att_self)
            stage("dense", None)
            for unit in projected(att_c0, -1):
                project(att_c0, *unit)

            def cq(half, m):
                n = plan.tiles["cq", half, m][0]
                act.wait_ge(tile_ready, n + 1)
                nc.scalar.mul(qch[:, m, hcols(half)], pool_bank(n)[:, 0:HALF], -0.25).then_inc(q_high, 1)

            stage("cq", cq)
            attention(att_c0)
            for b in range(2):
                context(att_1, b)
            stage("cdense", None)

            def hidden(name):
                nt = HIDDEN[name]

                def high(g, src):
                    if name == "mlp":
                        act.wait_ge(hid_done, g + 1)
                    if g >= 2:
                        act.wait_ge(acc_step, g - 1)
                    nc.scalar.copy(hid_h[:, g % 2, :], src).then_inc(hid_high, 1)

                def each(half, m):
                    g = hid_no(name, half, m)
                    if name == "mlp" and m >= 1:
                        high(g - 1, scr[:, 2 + (g - 1) % 2, :])
                    bank = empty((name, half, m, 0))
                    if name == "mlp":
                        if g >= 2:
                            act.wait_ge(hid_done, g - 1)
                        nc.scalar.activation(scr[:, g % 2, :], bank[:, 0:HALF], ACT.Silu).then_inc(emptied["act"], 1)
                        if m == nt - 1:
                            high(g, scr[:, 2 + g % 2, :])
                    else:
                        if g >= 2:
                            act.wait_ge(hid_low, g - 1)
                        nc.scalar.activation(scr[:, g % 2, :], bank[:, 0:HALF], ACT.Gelu).then_inc(emptied["act"], 1)
                        tile_done(act, (name, half, m, 0))
                        high(g, scr[:, g % 2, :])
                return each

            stage("mlp", hidden("mlp"))
            for L, a in ((1, att_1), (3, att_3)):
                for unit in projected(a, -1):
                    project(a, *unit)

                def wq(half, m, L=L):
                    bank = empty((f"Wq{L}", half, m))
                    nc.scalar.mul(q1[:, m, hcols(half)], bank[:, 0:HALF], -0.125).then_inc(emptied["act"], 1)

                stage(f"Wq{L}", wq)
                attention(a)
                if L == 1:
                    for b in range(2):
                        context(att_2, b)
                    act.wait_ge(att_1.summed, att_1.steps)
                    for b in range(4):
                        key_major(b)
                stage(f"Wo{L}", None)
                stage(f"ff{L}", hidden(f"ff{L}"))
                if L == 1:
                    def memp(half, m):
                        bank = empty(("mem", half, m))
                        nc.scalar.mul(hw[:, m, hcols(half)], bank[:, 0:HALF], -float(D) ** -0.5).then_inc(emptied["act"], 1)

                    stage("mem", memp)
                    attention(att_2)
                    act.wait_ge(att_1.masked, B)
                    for b in range(2):
                        context(att_3, b)

                    def memt(half, m):
                        bank = empty(("memT", half, m))
                        nc.scalar.copy(mc[:, m, hcols(half)], bank[:, 0:HALF]).then_inc(emptied["act"], 1)

                    stage("memT", memt)

                    def fgate(half, m):
                        i = half * KD + m
                        bank = empty(("gate", half, m))
                        if i >= 2:
                            act.wait_ge(fused_done, i - 1)
                        nc.scalar.activation(scr[:, i % 2, :], bank[:, 0:HALF], ACT.Sigmoid,
                                             bias=vec[:, VECS.index("L2_xattn_b_gate"), m:m + 1])\
                            .then_inc(emptied["act"], 1)

                    stage("gate", fgate)

        @block.vector
        def _(dve):
            given = [0]
            links = [0]

            def link(ins):
                links[0] += 1
                ins.then_inc(chain, 1)
                return links[0]

            def empty(key):
                n, who, count = plan.tiles[key]
                given[0] += 1
                assert who == "dve" and count == given[0]
                dve.wait_ge(tile_ready, n + 1)
                return pool_bank(n)

            def sum_free(nn, half, what):
                j = sum_no[nn, half, what] - 2
                if j >= 0:
                    dve.wait_ge(tile_ready, plan.tiles[sums[j]][0] + 1)

            def norm_part(nn, half, part):
                kind, wname, bname, e = NORMS[nn]
                cols = hcols(half)
                w = vec[:, VECS.index(wname), :]
                if part == "a":
                    sum_free(nn, half, "m")
                    x_ready(dve, nn, half, 0)
                    for k in range(1, KD):
                        x_ready(dve, nn, half, k)
                        ins = nc.vector.tensor_add(total[:, :], x[:, 0, cols] if k == 1 else total[:, :], x[:, k, cols])
                        if k < KD - 1:
                            dve.wait_ge(chain, link(ins))
                    ins.then_inc(summed_up, 1)
                elif part == "s":
                    sum_free(nn, half, "v")
                    i = turn_of[nn, half] * KD
                    for k in range(KD):
                        dve.wait_ge(sq_ready, i + k + 1)
                        if k == 0:
                            ins = nc.vector.tensor_copy(total[:, :], sq[:, i % 2, :])
                        else:
                            dve.wait_ge(sq_used, i + k)
                            ins = nc.vector.tensor_add(total[:, :], total[:, :], sq[:, (i + k) % 2, :])
                        ins.then_inc(sq_used, 1)
                    dve.wait_ge(sq_used, i + KD)
                    dve.sem_inc(summed_up, 1)
                elif part == "m":
                    bank = empty(("mean", nn, half))
                    for k in range(KD):
                        x_ready(dve, nn, half, k)
                        ins = nc.vector.tensor_sub(xc[:, k, :], x[:, k, cols], bank[:, 0:HALF])
                        ins.then_inc(centred if k < KD - 1 else emptied["dve"], 1)
                elif part == "f":
                    tile_done(dve, ("var", nn, half))
                    nc.vector.reciprocal(rstd[:, :], std[:, :]).then_inc(std_used, 1)
                    dve.wait_ge(std_used, turn_of[nn, half] + 1)
                    if nn == 5:
                        for k in range(KD):
                            nc.vector.scalar_tensor_tensor(x[:, k, cols], fused[:, k, cols], w[:, k:k + 1],
                                                           rstd[:, :], ALU.mult, ALU.mult).then_inc(normed, 1)
                        return
                    for k in range(KD + 1):
                        if k < KD:
                            if kind == "rms":
                                x_ready(dve, nn, half, k)
                            src = x[:, k, cols] if kind == "rms" else xc[:, k, :]
                            nc.vector.scalar_tensor_tensor(xc[:, k, :], src, w[:, k:k + 1], rstd[:, :],
                                                           ALU.mult, ALU.mult).then_inc(nraw, 1)
                        if k >= 1:
                            j = k - 1
                            dve.wait_ge(nhigh, split_turn[nn, half] * KD + j + 1)
                            high = nh_[:, j, cols].bitcast(F32)
                            if kind == "rms":
                                ins = nc.vector.tensor_sub(nl_[:, j, cols], xc[:, j, :], high)
                            else:
                                bias = vec[:, VECS.index(bname), j:j + 1]
                                ins = nc.vector.scalar_tensor_tensor(nl_[:, j, cols], xc[:, j, :], bias, high,
                                                                     ALU.add, ALU.subtract)
                            ins.then_inc(normed, 1)

            def stage(name, each):
                for it in SEQ[name]:
                    if it[0] == "norm":
                        norm_part(*it[1:])
                    elif each:
                        each(it[1], it[2])

            def residual(name, gate=None):
                def each(half, m):
                    bank = empty((name, half, m))
                    xs = x[:, m, hcols(half)]
                    if gate is None:
                        ins = nc.vector.tensor_add(xs, bank[:, 0:HALF], xs)
                    else:
                        ins = nc.vector.scalar_tensor_tensor(xs, bank[:, 0:HALF], gate_t[:, gate:gate + 1], xs,
                                                             ALU.mult, ALU.add)
                    ins.then_inc(emptied["dve"], 1)
                return each

            def out_group(a, p):
                dve.wait_ge(a.summed, (p + 1) * a.pvgroup)
                s = p * a.pvgroup
                b, h = s // a.nh, s % a.nh
                if a is att_2:
                    nc.vector.tensor_copy(pc[:, :, bcols(b)], pv_bank[:, 0:KC * S].rearrange("p (e s) -> p e s", e=KC))\
                        .then_inc(a.out, 1)
                    return
                t = h // a.pvgroup
                src = pv_bank[:, 0:S]
                if a is att_c0:
                    src = pick[:, :]
                    dve.wait_ge(chain, link(nc.vector.tensor_scalar(src, pv_bank[:, 0:S], cst[:, C_EVEN:C_EVEN + 1], None,
                                                                    ALU.mult)))
                    dve.wait_ge(chain, link(nc.vector.scalar_tensor_tensor(src, pv_bank[:, S:2 * S], cst[:, C_ODD:C_ODD + 1],
                                                                           src, ALU.mult, ALU.add)))
                high = (nh_ if a in (att_self, att_c0) else oh8)[:, t, bcols(b)]
                low = (nl_ if a in (att_self, att_c0) else ol8)[:, t, bcols(b)]
                n = link(nc.vector.tensor_copy(high, src))
                dve.wait_ge(chain, n)
                nc.vector.tensor_sub(low, src, high.bitcast(F32)).then_inc(a.out, 1)

            def project(a, kind, i, part):
                if kind == "V":
                    return
                bank = empty((a.name, kind, i, part))
                dve.wait_ge(a.k_high, i + 1)
                nc.vector.tensor_sub(kl[:, i % 2, :], bank[:, 0:376], kh[:, i % 2, :].bitcast(F32))\
                    .then_inc(emptied["dve"], 1)

            def attention(a):
                for s in range(a.steps + a.pvlag):
                    r = s - 1
                    if 0 <= r < a.steps:
                        dve.wait_ge(a.exped, r + 1)
                        nc.vector.reciprocal(rinv[:, r % NPROB:r % NPROB + 1], rsum[:, r % NPROB:r % NPROB + 1])\
                            .then_inc(a.recip, 1)
                    if s < a.steps:
                        b, h = s // a.nh, s % a.nh
                        col = nmin[:, s % NPROB:s % NPROB + 1]
                        dve.wait_ge(a.scored, s + 1)
                        if a.mask:
                            if a.mask == "keys" and h == 0:
                                dve.wait_ge(a.mask_in[b % 2], 16 * (b // 2 + 1))
                                nc.vector.tensor_scalar(maskf[:, b % 2, :], mask8[:, b % 2, :], -BIG, BIG,
                                                        ALU.mult, ALU.add).then_inc(a.masked, 1)
                                dve.wait_ge(a.masked, b + 1)
                            if s >= 2:
                                dve.wait_ge(a.exped, s - 1)
                            m = causal if a.mask == "causal" else maskf[:, b % 2, :]
                            nc.vector.tensor_tensor_reduce(out=masked_s[s % 2][:, 0:a.nk], in0=s_bank(s)[:, 0:a.nk],
                                                           in1=m, scale=1.0, scalar=BIG, op0=ALU.add, op1=ALU.min,
                                                           accum_out=col).then_inc(a.maxed, 1)
                        else:
                            nc.vector.tensor_reduce(col, s_bank(s)[:, 0:a.nk], AX_X, ALU.min).then_inc(a.maxed, 1)
                    if 0 <= r < a.steps:
                        dve.wait_ge(a.recip, r + 1)
                        pr = probs[r % NPROB][:, 0:a.nk]
                        nc.vector.tensor_scalar(pr, pr, rinv[:, r % NPROB:r % NPROB + 1], None, ALU.mult)\
                            .then_inc(a.scaled, 1)
                    if s < a.steps:
                        for unit in projected(a, s):
                            project(a, *unit)
                    w = s - a.pvlag
                    if w >= 0 and w % a.pvgroup == a.pvgroup - 1:
                        out_group(a, w // a.pvgroup)

            for t in (ctxh, ctxl):
                for b in range(2):
                    nc.vector.memset(t[:, b, :, S2:S2 + 1].bitcast(F32), 0.0).then_inc(pad_done, 1)
            nc.vector.memset(eps[:, 0:1], 1e-6).then_inc(eps_done, 1)
            nc.vector.memset(eps[:, 1:2], 1e-5).then_inc(eps_done, 1)
            tti = vself[:, 0:T].bitcast(I32).rearrange("p (b s) -> p b s", b=B)
            one = vself[:, T:2 * T].rearrange("p (b s) -> p b s", b=B)
            dve.wait_ge(tt_in, 16)
            link(nc.vector.tensor_scalar(one, tti, 1.0, None, ALU.is_equal))
            link(nc.vector.memset(vm[:, :, :], 0.0))
            dve.wait_ge(chain, links[0])
            dve.wait_ge(chain, link(nc.vector.tensor_mul(vm[:, :, 0:S - 1], one[:, :, 0:S - 1], one[:, :, 1:S])))
            link(nc.vector.tensor_scalar(vml[:, :, :], vm[:, :, :], -1.0, 1.0, ALU.mult, ALU.add))
            dve.wait_ge(ttT_in, 16)
            ttf = scr[0:S, 2, 0:2 * B]
            tti2 = scr[0:S, 2, 2 * B:4 * B].bitcast(I32)
            dve.wait_ge(chain, link(nc.vector.tensor_scalar(ttf, tti2, 1.0, None, ALU.is_equal)))
            nc.vector.tensor_mul(vmT[:, 0, :], ttf[:, 0:B], ttf[:, B:2 * B]).then_inc(vmT_done, 1)
            dve.wait_ge(vmT_done, 1)
            nc.vector.tensor_scalar(vmT[:, 1, :], vmT[:, 0, :], -1.0, 1.0, ALU.mult, ALU.add).then_inc(vmT_done, 1)
            posf = scr[0:S, 1, 0:S]
            wrap = scr[0:S, 2, 128:128 + S]
            dve.wait_ge(pos_in, 16)
            dve.wait_ge(cst_in, 16)
            dve.wait_ge(chain, link(nc.vector.tensor_copy(posf, scr[0:S, 3, 0:S].bitcast(I32))))
            dve.wait_ge(chain, link(nc.vector.tensor_scalar(wrap, posf, 0.0, float(S), ALU.is_lt, ALU.mult)))
            dve.wait_ge(chain, link(nc.vector.tensor_add(posf, posf, wrap)))
            dve.wait_ge(chain, link(nc.vector.tensor_scalar(wrap, posf, 0.0, float(S - 1), ALU.max, ALU.min)))
            nc.vector.tensor_scalar(scr[0:S, 0, 0:S], wrap, cst[0:S, C_POS:C_POS + 1], None, ALU.is_equal)\
                .then_inc(onehot_done, 1)
            dve.wait_ge(vec_in, 16)

            def experts(name, half, m, scale, out):
                hb = slice(half * BPH, (half + 1) * BPH)
                first = empty((name, half, m, 0))
                a0, t = out, scr[:, 2 + m % 2, :]
                n0 = link(nc.vector.scalar_tensor_tensor(a0, first[:, 0:HALF], scale,
                                                         vm[:, hb, :].rearrange("p b s -> p (b s)"), ALU.mult, ALU.mult))
                dve.wait_ge(chain, n0)
                dve.sem_inc(emptied["dve"], 1)
                second = empty((name, half, m, 1))
                n1 = link(nc.vector.scalar_tensor_tensor(t, second[:, 0:HALF], scale,
                                                         vml[:, hb, :].rearrange("p b s -> p (b s)"), ALU.mult, ALU.mult))
                dve.wait_ge(chain, n1)
                return t

            def rope(i):
                _, half, m = RAW[i]
                n, who, count = plan.tiles[("rot", i)]
                given[0] += 1
                assert count == given[0]
                if i == 0:
                    tile_done(dve, ("table", 1))
                raw_t = scr[:, i % 2, :].rearrange("p (b s) -> p b s", b=BPH)
                t = xc[:, i % 2, :].rearrange("p (b s) -> p b s", b=BPH)
                cos = cosT[:, :].unsqueeze(1).broadcast_to([P, BPH, S])
                sin = sinT[:, :].unsqueeze(1).broadcast_to([P, BPH, S])
                dst = (qT if m < KD else kT)[:, m % KD, hcols(half)].rearrange("p (b s) -> p b s", b=BPH)
                link(nc.vector.tensor_mul(t, raw_t, cos))
                dve.wait_ge(tile_ready, n + 1)
                bank = pool_bank(n)[:, 0:HALF].rearrange("p (b s) -> p b s", b=BPH)
                nc.vector.tensor_mul(dst, bank, sin).then_inc(emptied["dve"], 1)
                dve.wait_ge(chain, links[0])
                dve.wait_ge(emptied["dve"], count)
                nc.vector.tensor_add(dst, dst, t).then_inc(rope_done, 1)

            done = [0]

            def qk(half, m):
                i = done[0]
                done[0] += 1
                out = scr[:, i % 2, :]
                t = experts("qk", half, m, -float(32) ** -0.5 if m < KD else 1.0, out)
                dve.sem_inc(emptied["dve"], 1)
                nc.vector.tensor_add(out, out, t).then_inc(raw_qk, 1)
                dve.wait_ge(raw_qk, i + 1)
                if i >= 1:
                    rope(i - 1)

            stage("qk", qk)
            rope(done[0] - 1)
            for b in range(B):
                bank = empty(("vproj", b, 1))
                tile_done(dve, ("vproj", b, 0))
                nc.vector.scalar_tensor_tensor(vS[:, b, :], bank[0:S, :], vmT[:, 1, b:b + 1], vtmp[:, b % 2, :],
                                               ALU.mult, ALU.add).then_inc(emptied["dve"], 1)
            attention(att_self)

            def dense(half, m):
                xs = x[:, m, hcols(half)]
                out = scr[:, m % 2, :]
                t = experts("dense", half, m, 1.0, out)
                dve.wait_ge(chain, link(nc.vector.tensor_add(xs, xs, out)))
                nc.vector.tensor_add(xs, xs, t).then_inc(emptied["dve"], 1)

            stage("dense", dense)
            for unit in projected(att_c0, -1):
                project(att_c0, *unit)

            def cq(half, m):
                i = half * KC + m
                bank = empty(("cq", half, m))
                dve.wait_ge(q_high, i + 1)
                nc.vector.scalar_tensor_tensor(qcl[:, m, hcols(half)], bank[:, 0:HALF], -0.25,
                                               qch[:, m, hcols(half)].bitcast(F32), ALU.mult, ALU.subtract)\
                    .then_inc(emptied["dve"], 1)

            stage("cq", cq)
            attention(att_c0)
            stage("cdense", residual("cdense"))

            def hidden(name, gate=None):
                nt = HIDDEN[name]

                def low(g, src):
                    dve.wait_ge(hid_high, g + 1)
                    nc.vector.tensor_sub(hid_l[:, g % 2, :], src, hid_h[:, g % 2, :].bitcast(F32)).then_inc(hid_low, 1)

                def each(half, m):
                    g = hid_no(name, half, m)
                    if name == "mlp":
                        if m >= 1:
                            low(g - 1, scr[:, 2 + (g - 1) % 2, :])
                        mine = (vm if m < ITILES else vml)[:, half * BPH:(half + 1) * BPH, :].rearrange("p b s -> p (b s)")
                        tile_done(dve, (name, half, m, 0))
                        dve.wait_ge(chain, link(nc.vector.tensor_mul(scr[:, g % 2, :], scr[:, g % 2, :], mine)))
                        bank = empty((name, half, m, 1))
                        if g >= 2:
                            dve.wait_ge(hid_low, g - 1)
                        n = given[0]
                        nc.vector.tensor_mul(scr[:, 2 + g % 2, :], bank[:, 0:HALF], scr[:, g % 2, :])\
                            .then_inc(emptied["dve"], 1)
                        dve.wait_ge(emptied["dve"], n)
                        dve.sem_inc(hid_done, 1)
                        if m == nt - 1:
                            low(g, scr[:, 2 + g % 2, :])
                    else:
                        low(g, scr[:, g % 2, :])
                    if m == nt - 1:
                        dve.wait_ge(acc_step, g + 1)
                        for k in range(KD):
                            xs, acc = x[:, k, hcols(half)], psum[:, 4 + k, 0:HALF]
                            if gate is None:
                                ins = nc.vector.tensor_add(xs, acc, xs)
                            else:
                                ins = nc.vector.scalar_tensor_tensor(xs, acc, gate_t[:, gate:gate + 1], xs,
                                                                     ALU.mult, ALU.add)
                            ins.then_inc(acc_used, 1)
                return each

            stage("mlp", hidden("mlp"))
            dve.wait_ge(gate_done, 1)
            for L, a in ((1, att_1), (3, att_3)):
                for unit in projected(a, -1):
                    project(a, *unit)
                stage(f"Wq{L}", None)
                attention(a)
                stage(f"Wo{L}", residual(f"Wo{L}", L - 1))
                stage(f"ff{L}", hidden(f"ff{L}", L))
                if L == 1:
                    stage("mem", None)
                    attention(att_2)
                    stage("memT", None)

                    def fuse(half, m):
                        i = half * KD + m
                        cols = hcols(half)
                        tile_done(dve, ("gate", half, m))
                        t = scr[:, 2 + i % 2, :]
                        dve.wait_ge(chain, link(nc.vector.tensor_mul(t, scr[:, i % 2, :], mc[:, m, cols])))
                        nc.vector.tensor_add(fused[:, m, cols], t, x[:, m, cols]).then_inc(fused_done, 1)

                    stage("gate", fuse)

        @block.gpsimd
        def _(pool):
            def projected_all(a, b):
                return 1 + max(plan.tiles[a.name, "K", (b + 1) * NH // a.k_heads - 1, 0][0],
                               plan.tiles[a.name, "V", (b + 1) * NH // a.v_heads - 1, 1][0])

            def slot(u):
                _, name, c = u
                if name in ("q1", "q3"):
                    a = ATT[name[-1]]
                    half = c // BPH
                    tile_done(pool, ("Wq" + name[-1], half, 7))
                    if c == 1:
                        norm_done(pool, {"1": 3, "3": 6}[name[-1]], 1)
                    if c >= 2:
                        pool.wait_ge(a.scored, NH * (c - 1))
                    return q1[:, :, bcols(c)], qs[:, c % 2, 0], qs[:, c % 2, 1]
                n = USE_NO[u]
                pool.wait_ge(raw_in[n % RAW_RING], 16 * (n // RAW_RING + 1))
                if name[:3] == "ctx":
                    a = ATT[name[-1]]
                    if c < 2 and a is att_c0:
                        pool.wait_ge(pad_done, 4)
                    if c < 2 and a is att_3:
                        pool.wait_ge(att_2.scored, B)
                    if c >= 2:
                        pool.wait_ge(tile_ready, projected_all(a, c - 2))
                    src = raw[:, n % RAW_RING, 0:KC * S2].rearrange("p (k n) -> p k n", k=KC)
                    return src, ctxh[:, c % 2, :, 0:S2], ctxl[:, c % 2, :, 0:S2]
                chunk_raw = raw[:, n % RAW_RING, :]
                if name == "kv0":
                    pool.wait_ge(att_self.scored, att_self.steps)
                    return chunk_raw, kv0h[:, :], kv0l[:, :]
                if name[:2] == "kv":
                    if name == "kv1":
                        pool.wait_ge(att_c0.scored, att_c0.steps)
                    else:
                        pool.wait_ge(tile_ready, projected_all(att_1, B - 1))
                    cols = slice(c * SLOT, (c + 1) * SLOT)
                    return chunk_raw, kvwh[:, cols], kvwl[:, cols]
                r = RING_NO[u]
                if r >= RING:
                    pool.wait_ge(*chunk_last[RING_USES[r - RING]])
                return chunk_raw, wh[:, r % RING, :], wl[:, r % RING, :]

            def lay_out(u):
                _, name, b = u
                if name == "mself":
                    pool.wait_ge(rope_done, 8)
                    if b >= 2:
                        pool.wait_ge(att_self.scored, NH * (b - 1))
                    work = [(qm[:, b % 2, :, j, :], qT[:, :, bcols(b)], C_H4 + j) for j in range(4)]
                else:
                    if b == 0:
                        pool.wait_ge(att_self.summed, att_self.steps)
                    tile_done(pool, ("cq", b // BPH, 1))
                    if b >= 2:
                        pool.wait_ge(att_c0.scored, NH * (b - 1))
                    work = [(qmx[:, b % 2, i, :, j, :], t[:, :, bcols(b)].bitcast(F32), C_H8 + j)
                            for j in range(8) for i, t in enumerate((qch, qcl))]
                for dst, src, col in work:
                    last = nc.gpsimd.tensor_scalar(dst, src, cst[:, col:col + 1], None, ALU.mult)
                last.then_inc(laid_out, 1)

            pool.wait_ge(cst_in, 16)
            for u in WORK:
                if u[1] in PLAIN:
                    continue
                if u[1] in MASKINGS:
                    lay_out(u)
                    continue
                n = SPLIT_NO[u]
                src, high, low = slot(u)
                nc.gpsimd.tensor_scalar(high, src, 1.0, 1.0, ALU.mult, ALU.mult).then_inc(split_h, 1)
                pool.wait_ge(split_h, n + 1)
                nc.gpsimd.tensor_tensor(low, src, high.bitcast(F32), ALU.subtract).then_inc(split_l, 1)

        @block.sync
        def _(sp):
            sp.dma_start(vself[:, 0:T].bitcast(I32), tt.partition_broadcast(P)).then_inc(tt_in, 16)
            sp.dma_start(scr[0:S, 3, 0:S].bitcast(I32), pos.partition_broadcast(S)).then_inc(pos_in, 16)
            sp.dma_start(cst[:, :], consts).then_inc(cst_in, 16)
            sp.dma_start(scr[0:S, 2, 2 * B:4 * B].bitcast(I32), ttT).then_inc(ttT_in, 16)
            for n, (use, name, c) in enumerate(USES):
                if n >= RAW_RING:
                    last = USES[n - RAW_RING]
                    if last[1] in PLAIN:
                        sp.wait_ge(*chunk_last[last])
                    else:
                        sp.wait_ge(split_l, SPLIT_NO[last] + 1)
                if name[:3] == "ctx":
                    src = ctxF[c].rearrange("p k n -> p (k n)")
                    sp.dma_start(raw[:, n % RAW_RING, 0:KC * S2], src).then_inc(raw_in[n % RAW_RING], 16)
                else:
                    sp.dma_start(raw[:, n % RAW_RING, :], walls[STORED0[name] + c]).then_inc(raw_in[n % RAW_RING], 16)
            for half in range(2):
                sp.wait_ge(acc_used, mlp_out("ff3", half) + KD)
                sp.dma_start(outT[:, :, hcols(half)], x[:, :, hcols(half)]).then_inc(out_done, 16)
            sp.wait_ge(out_done, 32)


def kernel(**inputs):
    import numpy as np
    import concourse.bacc as bacc
    from concourse.bass_utils import run_bass_kernel_spmd

    def get(name):
        return np.asarray(inputs[name])

    def blocks(w, m):
        k_tiles = -(-w.shape[0] // P)
        out = np.zeros((k_tiles, P, P), w.dtype)
        part = w[:, m * P:(m + 1) * P]
        for k in range(k_tiles):
            rows = part[k * P:(k + 1) * P]
            out[k, :rows.shape[0], :rows.shape[1]] = rows
        return list(out)

    def v(name):
        return get(name)

    walls = np.zeros((N_STORED, P, SLOT), np.float32)

    def put(name, c, blist):
        for i, blk in enumerate(blist):
            walls[STORED0[name] + c][:, i * P:(i + 1) * P] = blk

    def put_tiles(name, ms, mpc, weights):
        for m in range(ms):
            if m % mpc == 0:
                acc = []
            for w in weights:
                acc += blocks(w, m)
            if m % mpc == mpc - 1 or m == ms - 1:
                put(name, m // mpc, acc)

    def out_blocks(w, k):
        out = np.zeros((P, D), w.dtype)
        rows = w[k * P:(k + 1) * P]
        out[:rows.shape[0]] = rows
        return [out[:, m * P:(m + 1) * P] for m in range(KD)]

    vq, lq = v("L0_xattn_v_qkv"), v("L0_xattn_l_qkv")
    put_tiles("qk", 8, 1, [vq, lq])
    for e, w in enumerate((vq, lq)):
        for j in range(2):
            part = w[2 * j * P:2 * (j + 1) * P, 2 * D:]
            walls[STORED0["v"] + 2 * e + j] = part.reshape(2, P, D).transpose(1, 0, 2).reshape(P, 2 * D)
    put_tiles("dense", 4, 1, [v("L0_xattn_v_dense"), v("L0_xattn_l_dense")])
    put_tiles("cq", 2, 2, [v("L0_xattn_cq_w")])
    put_tiles("cdense", 4, 4, [v("L0_xattn_cdense_w")])
    downs = []
    for j, e in enumerate("vl"):
        gate, up = v(f"L0_xattn_{e}_gate"), v(f"L0_xattn_{e}_up")
        for m in range(ITILES):
            put("gu", j * ITILES + m, blocks(gate, m) + blocks(up, m))
            downs += out_blocks(v(f"L0_xattn_{e}_down"), m)
    for c in range(ETILES // 2):
        put("down", c, downs[8 * c:8 * c + 8])
    for L in "13":
        put_tiles("Wq" + L, 8, 2, [v(f"L{L}_xattn_Wq")])
        put_tiles("Wo" + L, 4, 1, [v(f"L{L}_xattn_Wo")])
        for m in range(16):
            put("ff" + L, m, blocks(v(f"L{L}_xattn_W1"), m) + out_blocks(v(f"L{L}_xattn_W2"), m))
    put_tiles("mem", 2, 2, [v("L2_xattn_W_mem")])
    put_tiles("memT", 4, 4, [v("L2_xattn_W_mem").T])
    put_tiles("gate", 4, 1, [v("L2_xattn_W_gate").T])

    def rows_first(w):
        k = w.shape[0] // P
        return np.ascontiguousarray(w.reshape(k, P, w.shape[1]).transpose(1, 0, 2).reshape(P, -1))

    for name, w in (("kv0", "L0_xattn_ckv_w"), ("kv1", "L1_xattn_Wkv"), ("kv3", "L3_xattn_Wkv")):
        rows = rows_first(v(w))
        for c in range(rows.shape[1] // SLOT):
            walls[STORED0[name] + c] = rows[:, c * SLOT:(c + 1) * SLOT]

    c = np.zeros((P, C_END), np.float32)
    c[:, C_ID:C_ID + P] = np.eye(P)
    c[:, C_MEAN:C_MEAN + P] = 1.0 / D
    for m in range(P):
        if m % 32 < 16:
            c[m + 16, C_ROT + m] = -1.0
        else:
            c[m - 16, C_ROT + m] = 1.0
    inv = (1.0 / np.float32(10000.0) ** (np.arange(0, 32, 2, dtype=np.float32) / np.float32(32))).astype(np.float32)
    freqs = np.outer(np.arange(S, dtype=np.float32), inv).astype(np.float32)
    emb = np.tile(freqs, (1, P // 16))
    c[0:S, C_COS:C_COS + P] = np.cos(emb)
    c[0:S, C_SIN:C_SIN + P] = np.sin(emb)
    q, k = np.arange(S)[:, None], np.arange(S)[None, :]
    c[0:S, C_CAUSAL:C_CAUSAL + S] = np.where(k > q, np.float32(BIG), np.float32(0))
    c[:, C_POS] = np.arange(P)
    c[:, C_EVEN] = np.arange(P) // 16 % 2 == 0
    c[:, C_ODD] = np.arange(P) // 16 % 2 == 1

    for j in range(4):
        c[:, C_H4 + j] = np.arange(P) // 32 == j
    for j in range(8):
        c[:, C_H8 + j] = np.arange(P) // 16 == j

    ctx = get("ctx_1024")
    types = get("mask_BxS_ik0").T
    after = np.concatenate([types[1:], np.zeros_like(types[:1])])
    arrays = {
        "xT": np.ascontiguousarray(get("x").reshape(T, KD, P).transpose(2, 1, 0)),
        "ctxF": np.ascontiguousarray(ctx.reshape(B, S2, KC, P).transpose(0, 3, 2, 1)),
        "ctxK": np.ascontiguousarray(ctx.reshape(B, CH, KEYS, CC).transpose(0, 2, 1, 3)).reshape(B, KEYS, CH * CC),
        "kmask": get("mask_BxS2_bk0").reshape(B, S2),
        "tt": get("mask_BxS_ik0").reshape(T),
        "ttT": np.ascontiguousarray(np.concatenate([types, after], axis=1)),
        "pos": get("pos_1xS").reshape(S),
        "walls": walls,
        "vecs": np.ascontiguousarray(np.stack([get(n).reshape(KD, P) for n in VECS]).transpose(2, 0, 1)),
        "gates": np.concatenate([get("L1_xattn_attn_gate"), get("L1_xattn_ff_gate"),
                                 get("L3_xattn_attn_gate"), get("L3_xattn_ff_gate")]),
        "consts": c,
    }
    nc = bacc.Bacc("TRN2", target_bir_lowering=False, num_devices=1, dynamic_dma_scratch_size=SCRATCH)
    args = [nc.dram_tensor(f"in_{n}", a.shape, mybir.dt.from_np(a.dtype), kind="ExternalInput").ap()
            for n, a in arrays.items()]
    out = nc.dram_tensor("outT", [P, KD, T], F32, kind="ExternalOutput").ap()
    build(nc, *args, out)
    r = run_bass_kernel_spmd(nc, [{f"in_{n}": a for n, a in arrays.items()}], core_ids=[0])
    got = r.results[0]["outT"]
    return np.ascontiguousarray(np.asarray(got).transpose(2, 1, 0)).reshape(B, S, D)
```
